# Optimizing a Trainium2 kernel written in Bass

```python
import numpy as np
import jax
import jax.numpy as jnp

def _softmax(x, axis=-1):
    return jax.nn.softmax(x, axis=axis)

def _gelu(x):
    return jax.nn.gelu(x, approximate=True)

def _silu(x):
    return jax.nn.silu(x)

def _sigmoid(x):
    return jax.nn.sigmoid(x)

def _layernorm(x, axis=-1, eps=1e-05):
    m = jnp.mean(x, axis=axis, keepdims=True)
    v = jnp.var(x, axis=axis, keepdims=True)
    return (x - m) / jnp.sqrt(v + eps)

def _scatter_add(tgt, idx, src, axis=0):
    return tgt.at[idx].add(src)

def _segment_sum(src, seg, n):
    return jax.ops.segment_sum(src, seg, n)
kernel_name = 'mk_gnn_preln_d4_gnn_r8_dc490e'

def setup_inputs(seed: int=0):
    np.random.seed(seed)
    _w = jnp.asarray

    def _rec_inputs():
        import jax
        import jax.numpy as jnp
        _gk = jax.random.key(seed)
        x = -0.000202 + 1 * jax.random.normal(jax.random.fold_in(_gk, 1), (12500, 128), jnp.float32)
        src = jax.random.randint(jax.random.fold_in(_gk, 2), (200000,), 0, 12500, jnp.int32)
        dst = jax.random.randint(jax.random.fold_in(_gk, 3), (200000,), 0, 12500, jnp.int32)
        _o = jnp.argsort(dst, stable=True)
        src = src[_o]
        dst = dst[_o]
        edge_attr_64 = -8.16379e-05 + 0.999858 * jax.random.normal(jax.random.fold_in(_gk, 12), (200000, 64), jnp.float32)
        edge_type_50 = jax.random.randint(jax.random.fold_in(_gk, 14), (200000,), 0, 50, jnp.int32)
        edge_type_9 = jax.random.randint(jax.random.fold_in(_gk, 15), (200000,), 0, 9, jnp.int32)
        return (x, src, dst, edge_attr_64, edge_type_50, edge_type_9)
    x, src, dst, edge_attr_64, edge_type_50, edge_type_9 = _rec_inputs()

    def _L0_gnn_setup():
        import jax, jax.numpy as jnp
        import numpy as np
        NUM_EDGE_TYPES = 8
        HIDDEN = 128
        N_NODES = 6250
        N_EDGES = 75000

        def _gru_cell(x, h, W_ih, W_hh, b_ih, b_hh):
            H = h.shape[-1]
            gi = x @ W_ih.T + b_ih
            gh = h @ W_hh.T + b_hh
            i_r, i_z, i_n = (gi[:, :H], gi[:, H:2 * H], gi[:, 2 * H:])
            h_r, h_z, h_n = (gh[:, :H], gh[:, H:2 * H], gh[:, 2 * H:])
            r = jax.nn.sigmoid(i_r + h_r)
            z = jax.nn.sigmoid(i_z + h_z)
            n = jnp.tanh(i_n + r * h_n)
            return (1.0 - z) * n + z * h
        key = jax.random.key(seed)
        ks = jax.random.split(key, 10)
        H = HIDDEN
        h = jax.random.normal(ks[0], (N_NODES, H), dtype=jnp.float32)
        edge_index = jax.random.randint(ks[1], (2, N_EDGES), 0, N_NODES, dtype=jnp.int32)
        edge_type = jax.random.randint(ks[2], (N_EDGES,), 0, NUM_EDGE_TYPES + 1, dtype=jnp.int32)
        s = 1.0 / np.sqrt(H)
        W_msg = jax.random.uniform(ks[3], (H, H), jnp.float32, -s, s)
        b_msg = jax.random.uniform(ks[4], (H,), jnp.float32, -s, s)
        edge_embed = jax.random.normal(ks[5], (NUM_EDGE_TYPES + 1, H), dtype=jnp.float32)
        W_ih = jax.random.uniform(ks[6], (3 * H, H), jnp.float32, -s, s)
        W_hh = jax.random.uniform(ks[7], (3 * H, H), jnp.float32, -s, s)
        b_ih = jax.random.uniform(ks[8], (3 * H,), jnp.float32, -s, s)
        b_hh = jax.random.uniform(ks[9], (3 * H,), jnp.float32, -s, s)
        return {'h': h, 'edge_index': edge_index, 'edge_type': edge_type, 'num_nodes': N_NODES, 'W_msg': W_msg, 'b_msg': b_msg, 'edge_embed': edge_embed, 'W_ih': W_ih, 'W_hh': W_hh, 'b_ih': b_ih, 'b_hh': b_hh}
    _L0_gnn_all = _L0_gnn_setup()
    _L0_gnn_in = {k: v for k, v in _L0_gnn_all.items() if k in ('W_msg', 'b_msg', 'edge_embed', 'W_ih', 'W_hh', 'b_ih', 'b_hh')}
    del _L0_gnn_all

    def _L1_gnn_setup():
        import jax, jax.numpy as jnp
        import numpy as np
        N_NODES = 12500
        N_EDGES = 400000
        DIM = 128
        LN_EPS = 1e-05
        key = jax.random.key(seed)
        k1, k2, k3, k4 = jax.random.split(key, 4)
        x = jax.random.normal(k1, (N_NODES, DIM), dtype=jnp.float32)
        edge_index = jax.random.randint(k2, (2, N_EDGES), 0, N_NODES, dtype=jnp.int64)
        scale = 1.0 / np.sqrt(DIM)
        W = jax.random.uniform(k3, (DIM, DIM), minval=-scale, maxval=scale, dtype=jnp.float32)
        b = jax.random.uniform(k4, (DIM,), minval=-scale, maxval=scale, dtype=jnp.float32)
        gamma = jnp.ones((DIM,), dtype=jnp.float32)
        beta = jnp.zeros((DIM,), dtype=jnp.float32)
        return {'x': x, 'edge_index': edge_index, 'W': W, 'b': b, 'gamma': gamma, 'beta': beta}
    _L1_gnn_all = _L1_gnn_setup()
    _L1_gnn_in = {k: v for k, v in _L1_gnn_all.items() if k in ('W', 'b', 'gamma', 'beta')}
    del _L1_gnn_all

    def _L2_gnn_setup():
        import jax, jax.numpy as jnp
        import numpy as np
        N_ENT = 2048
        N_REL = 50
        D = 128
        B = 4
        E = 32768
        key = jax.random.key(seed)
        k1, k2, k3, k4, k5, k6 = jax.random.split(key, 6)
        x = jax.random.normal(k1, (N_ENT, D), dtype=jnp.float32)
        bases = jax.random.normal(k2, (B, D, D), dtype=jnp.float32) * 0.05
        comps = jax.random.normal(k3, (N_REL, B), dtype=jnp.float32)
        alpha = jax.random.normal(k4, (N_REL, 1), dtype=jnp.float32)
        edge_index = jax.random.randint(k5, (2, E), 0, N_ENT, dtype=jnp.int64)
        edge_type = jax.random.randint(k6, (E,), 0, N_REL, dtype=jnp.int64)
        return {'x': x, 'bases': bases, 'comps': comps, 'alpha': alpha, 'edge_index': edge_index, 'edge_type': edge_type}
    _L2_gnn_all = _L2_gnn_setup()
    _L2_gnn_in = {k: v for k, v in _L2_gnn_all.items() if k in ('bases', 'comps', 'alpha')}
    del _L2_gnn_all

    def _L3_gnn_setup():
        import jax, jax.numpy as jnp
        import numpy as np
        N_NODES = 12500
        N_EDGES = 200000
        NDIM_IN = 128
        EDIMS = 64
        NDIM_OUT = 128
        NUM_HEADS = 4
        HEAD_DIM = NDIM_OUT // NUM_HEADS
        key = jax.random.key(seed)
        ks = jax.random.split(key, 10)
        in_dim = NDIM_IN + EDIMS
        b1 = float(np.sqrt(6.0 / (in_dim + NDIM_OUT)))
        b2 = float(np.sqrt(6.0 / (NDIM_OUT + NDIM_OUT)))
        bav = float(np.sqrt(6.0 / (NUM_HEADS + HEAD_DIM)))
        return {'nfeats': jax.random.normal(ks[0], (N_NODES, NDIM_IN), dtype=jnp.float32), 'efeats': jax.random.normal(ks[1], (N_EDGES, EDIMS), dtype=jnp.float32), 'src': jax.random.randint(ks[2], (N_EDGES,), 0, N_NODES, dtype=jnp.int32), 'dst': jax.random.randint(ks[3], (N_EDGES,), 0, N_NODES, dtype=jnp.int32), 'W_proj_w': jax.random.uniform(ks[4], (NDIM_OUT, in_dim), jnp.float32, -b1, b1), 'W_proj_b': jnp.zeros((NDIM_OUT,), jnp.float32), 'attn_vec': jax.random.uniform(ks[5], (NUM_HEADS, HEAD_DIM), jnp.float32, -bav, bav), 'W_out_w': jax.random.uniform(ks[6], (NDIM_OUT, NDIM_OUT), jnp.float32, -b2, b2), 'W_out_b': jnp.zeros((NDIM_OUT,), jnp.float32), 'ln_gamma': jnp.ones((NDIM_OUT,), jnp.float32), 'ln_beta': jnp.zeros((NDIM_OUT,), jnp.float32)}
    _L3_gnn_all = _L3_gnn_setup()
    _L3_gnn_in = {k: v for k, v in _L3_gnn_all.items() if k in ('W_proj_w', 'W_proj_b', 'attn_vec', 'W_out_w', 'W_out_b', 'ln_gamma', 'ln_beta')}
    del _L3_gnn_all
    return {'x': x, 'src': src, 'dst': dst, 'edge_attr_64': edge_attr_64, 'edge_type_50': edge_type_50, 'edge_type_9': edge_type_9, 'L0_gnn_W_msg': _L0_gnn_in['W_msg'], 'L0_gnn_b_msg': _L0_gnn_in['b_msg'], 'L0_gnn_edge_embed': _L0_gnn_in['edge_embed'], 'L0_gnn_W_ih': _L0_gnn_in['W_ih'], 'L0_gnn_W_hh': _L0_gnn_in['W_hh'], 'L0_gnn_b_ih': _L0_gnn_in['b_ih'], 'L0_gnn_b_hh': _L0_gnn_in['b_hh'], 'L1_gnn_W': _L1_gnn_in['W'], 'L1_gnn_b': _L1_gnn_in['b'], 'L1_gnn_gamma': _L1_gnn_in['gamma'], 'L1_gnn_beta': _L1_gnn_in['beta'], 'L2_gnn_bases': _L2_gnn_in['bases'], 'L2_gnn_comps': _L2_gnn_in['comps'], 'L2_gnn_alpha': _L2_gnn_in['alpha'], 'L3_gnn_W_proj_w': _L3_gnn_in['W_proj_w'], 'L3_gnn_W_proj_b': _L3_gnn_in['W_proj_b'], 'L3_gnn_attn_vec': _L3_gnn_in['attn_vec'], 'L3_gnn_W_out_w': _L3_gnn_in['W_out_w'], 'L3_gnn_W_out_b': _L3_gnn_in['W_out_b'], 'L3_gnn_ln_gamma': _L3_gnn_in['ln_gamma'], 'L3_gnn_ln_beta': _L3_gnn_in['ln_beta']}

def reference(x, src, dst, edge_attr_64, edge_type_50, edge_type_9, L0_gnn_W_msg, L0_gnn_b_msg, L0_gnn_edge_embed, L0_gnn_W_ih, L0_gnn_W_hh, L0_gnn_b_ih, L0_gnn_b_hh, L1_gnn_W, L1_gnn_b, L1_gnn_gamma, L1_gnn_beta, L2_gnn_bases, L2_gnn_comps, L2_gnn_alpha, L3_gnn_W_proj_w, L3_gnn_W_proj_b, L3_gnn_attn_vec, L3_gnn_W_out_w, L3_gnn_W_out_b, L3_gnn_ln_gamma, L3_gnn_ln_beta):
    import jax
    import jax.numpy as jnp

    def _L0_gnn_ref(h, edge_index, edge_type, num_nodes, W_msg, b_msg, edge_embed, W_ih, W_hh, b_ih, b_hh):
        import jax, jax.numpy as jnp
        import numpy as np
        NUM_EDGE_TYPES = 8
        HIDDEN = 128
        N_NODES = 6250
        N_EDGES = 75000

        def _gru_cell(x, h, W_ih, W_hh, b_ih, b_hh):
            H = h.shape[-1]
            gi = x @ W_ih.T + b_ih
            gh = h @ W_hh.T + b_hh
            i_r, i_z, i_n = (gi[:, :H], gi[:, H:2 * H], gi[:, 2 * H:])
            h_r, h_z, h_n = (gh[:, :H], gh[:, H:2 * H], gh[:, 2 * H:])
            r = jax.nn.sigmoid(i_r + h_r)
            z = jax.nn.sigmoid(i_z + h_z)
            n = jnp.tanh(i_n + r * h_n)
            return (1.0 - z) * n + z * h
        src = edge_index[0]
        dst = edge_index[1]
        src_h = h[src] @ W_msg.T + b_msg
        emb = edge_embed[jnp.clip(edge_type, 0, NUM_EDGE_TYPES)]
        msg = src_h + emb
        messages = jax.ops.segment_sum(msg, dst, num_segments=num_nodes)
        h_new = _gru_cell(messages, h[:num_nodes], W_ih, W_hh, b_ih, b_hh)
        result = jnp.zeros_like(h).at[:num_nodes].set(h_new)
        return result

    def _L1_gnn_ref(x, edge_index, W, b, gamma, beta):
        import jax, jax.numpy as jnp
        import numpy as np
        N_NODES = 12500
        N_EDGES = 400000
        DIM = 128
        LN_EPS = 1e-05
        N = x.shape[0]
        loops = jnp.arange(N, dtype=edge_index.dtype)
        row = jnp.concatenate([edge_index[0], loops])
        col = jnp.concatenate([edge_index[1], loops])
        deg = jax.ops.segment_sum(jnp.ones_like(col, dtype=x.dtype), col, num_segments=N)
        deg_inv_sqrt = jnp.where(deg > 0, jax.lax.rsqrt(jnp.maximum(deg, 1.0)), 0.0)
        norm = deg_inv_sqrt[row] * deg_inv_sqrt[col]
        msg = norm[:, None] * x[row]
        agg = jax.ops.segment_sum(msg, col, num_segments=N)
        out = agg @ W.T + b
        mean = jnp.mean(out, axis=-1, keepdims=True)
        var = jnp.mean(jnp.square(out - mean), axis=-1, keepdims=True)
        out = (out - mean) * jax.lax.rsqrt(var + LN_EPS) * gamma + beta
        return out

    def _L2_gnn_ref(x, bases, comps, alpha, edge_index, edge_type):
        import jax, jax.numpy as jnp
        import numpy as np
        N_ENT = 2048
        N_REL = 50
        D = 128
        B = 4
        E = 32768
        n = x.shape[0]
        row, col = (edge_index[0], edge_index[1])
        ones = jnp.ones(row.shape, x.dtype)
        deg = jax.ops.segment_sum(ones, row, num_segments=n)
        deg_inv = jnp.where(deg > 0, jax.lax.rsqrt(jnp.maximum(deg, 1.0)), 0.0)
        norm = deg_inv[row] * deg_inv[col]
        h_j = x[col]
        c_e = comps[edge_type]
        hj_b = c_e[:, :, None] * h_j[:, None, :]
        msg = jnp.einsum('ebd,bdf->ef', hj_b, bases)
        msg = msg * alpha[edge_type] * norm[:, None]
        out = jax.ops.segment_sum(msg, row, num_segments=n)
        return out

    def _L3_gnn_ref(nfeats, efeats, src, dst, W_proj_w, W_proj_b, attn_vec, W_out_w, W_out_b, ln_gamma, ln_beta):
        import jax, jax.numpy as jnp
        import numpy as np
        N_NODES = 12500
        N_EDGES = 200000
        NDIM_IN = 128
        EDIMS = 64
        NDIM_OUT = 128
        NUM_HEADS = 4
        HEAD_DIM = NDIM_OUT // NUM_HEADS
        N = nfeats.shape[0]
        H, D = attn_vec.shape
        x = jnp.concatenate([nfeats[src], efeats], axis=1)
        x_proj = (x @ W_proj_w.T + W_proj_b).reshape(-1, H, D)
        e = jnp.sum(x_proj * attn_vec, axis=-1)
        emax = jax.ops.segment_max(e, dst, num_segments=N)
        ex = jnp.exp(e - emax[dst])
        denom = jax.ops.segment_sum(ex, dst, num_segments=N)
        alpha = ex / denom[dst]
        m = (x_proj * alpha[:, :, None]).reshape(-1, H * D)
        h_neigh = jax.ops.segment_sum(m, dst, num_segments=N)
        h = jax.nn.relu((h_neigh + nfeats) @ W_out_w.T + W_out_b)
        mu = jnp.mean(h, axis=-1, keepdims=True)
        var = jnp.mean((h - mu) ** 2, axis=-1, keepdims=True)
        return (h - mu) * jax.lax.rsqrt(var + 1e-05) * ln_gamma + ln_beta
    edge_index = jnp.stack([src, dst])
    h = jnp.maximum(_layernorm(x, axis=-1), 0.0)
    x = x + _L0_gnn_ref(h, edge_index, edge_type_9, 12500, L0_gnn_W_msg, L0_gnn_b_msg, L0_gnn_edge_embed, L0_gnn_W_ih, L0_gnn_W_hh, L0_gnn_b_ih, L0_gnn_b_hh)
    h = jnp.maximum(_layernorm(x, axis=-1), 0.0)
    x = x + _L1_gnn_ref(h, edge_index, L1_gnn_W, L1_gnn_b, L1_gnn_gamma, L1_gnn_beta)
    h = jnp.maximum(_layernorm(x, axis=-1), 0.0)
    x = x + _L2_gnn_ref(h, L2_gnn_bases, L2_gnn_comps, L2_gnn_alpha, edge_index, edge_type_50)
    h = jnp.maximum(_layernorm(x, axis=-1), 0.0)
    x = x + _L3_gnn_ref(h, edge_attr_64, src, dst, L3_gnn_W_proj_w, L3_gnn_W_proj_b, L3_gnn_attn_vec, L3_gnn_W_out_w, L3_gnn_W_out_b, L3_gnn_ln_gamma, L3_gnn_ln_beta)
    return x

_drawn_inputs = setup_inputs


def setup_inputs(seed=0):
    import zlib

    import numpy as np

    out = dict(_drawn_inputs(seed))
    spreads = {'L1_gnn_gamma': (1.0, 0.2),
     'L1_gnn_beta': (0.0, 0.1),
     'L3_gnn_W_proj_b': (0.0, 0.1),
     'L3_gnn_W_out_b': (0.0, 0.1),
     'L3_gnn_ln_gamma': (1.0, 0.2),
     'L3_gnn_ln_beta': (0.0, 0.1)}
    factors = {'L0_gnn_b_ih': 6.321, 'L0_gnn_b_hh': 7.879}
    for name, (base, spread) in spreads.items():
        noise = np.random.default_rng([zlib.crc32(name.encode()), seed]).standard_normal(out[name].shape)
        drawn = base * np.exp(spread * noise) if base else spread * noise
        out[name] = jnp.asarray(drawn.astype(out[name].dtype))
    for name, factor in factors.items():
        out[name] = (out[name] * factor).astype(out[name].dtype)
    return out
```

```python
from contextlib import ExitStack

import concourse.bass as bass
from concourse import mybir

P = 128
F = 128
J = 4
GE = P * J
W = 64
U = 4
Q = 4
COPIES = 8
T9 = 9
T50 = 50
HEADS = 4
HD = F // HEADS
ED = 64
EPS = 1e-5
FAR = -1.0e6
BIG = 1.0e30

ALU = mybir.AluOpType
ACT = mybir.ActivationFunctionType
AX_X = mybir.AxisListType.X
F32 = mybir.dt.float32
I32 = mybir.dt.int32
BF16 = mybir.dt.bfloat16
ds = bass.ds


class Link:

    def __init__(self, eng, sem, base=0):
        self.eng, self.sem, self.base, self.n = eng, sem, base, 0

    def __call__(self, ins, wait=True):
        self.n += 1
        ins.then_inc(self.sem, 1)
        if wait:
            self.eng.wait_ge(self.sem, self.base + self.n)


class Shapes:
    def __init__(self, n_nodes, n_edges):
        self.N, self.E = n_nodes, n_edges
        self.NT = -(-n_nodes // P)
        self.NP = self.NT * P
        self.NTP = -(-self.NT // Q) * Q
        self.NR = (self.NTP + 2) * P
        self.NG = -(-n_edges // GE)
        self.NGP = -(-self.NG // U) * U
        self.NB = -(-self.NGP // P)
        self.NWIN = -(-n_nodes // W)


def bcast(ap, axis, n):
    ap = ap.unsqueeze(axis)
    shape = list(ap.shape)
    shape[axis] = n
    return ap.broadcast_to(shape)


def setup_phase(nc, S, src, dst, type9, type50, t):
    NB, NGP = S.NB, S.NGP
    full, rest = S.E // GE, S.E % GE
    with ExitStack() as c:
        sb = lambda n, s, d=F32: c.enter_context(nc.sbuf_tensor(f"setup_{n}", s, d))
        sem = lambda n: c.enter_context(nc.semaphore(n))
        raw = {k: sb(f"raw_{k}", [P, NB, GE], I32) for k in ("src", "dst", "t9", "t50")}
        dst_f = sb("dst_f", [P, NB, GE])
        low = sb("low", [P, NB, GE])
        src_f = sb("src_f", [P, NB, GE])
        t9_f = sb("t9_f", [P, NB, GE])
        whole = sb("whole", [P, NB, GE], I32)
        part = sb("part", [P, NB, GE], I32)
        rows = sb("rows", [P, NB, 5, GE], BF16)
        dmin = sb("dmin", [P, NB])
        dmax = sb("dmax", [P, NB])
        span = sb("span", [P, NB])
        spanmax = sb("spanmax", [P, 1])
        wide_f = sb("wide_f", [1, 1])
        one_row = sb("one_row", [1, P])
        narrow = sb("narrow", [P, 1])
        base = sb("base", [P, NB])
        below = sb("below", [P, NGP * J])
        cols = sb("cols", [P, NGP * J])
        type9_cols = sb("type9_cols", [P, NGP * J])
        unique = sb("unique", [P, 1])
        ps_small = c.enter_context(nc.psum_tensor("ps_small", [P, 512], F32))
        ps_base = c.enter_context(nc.psum_tensor("ps_base", [P, 512], F32))
        ps_t = [c.enter_context(nc.psum_tensor(f"ps_t{k}", [P, J, P], F32)) for k in range(2)]
        padded, loaded, consts = sem("padded"), sem("loaded"), sem("setup_consts")
        step, spans, bcast_flag, bases = sem("setup_step"), sem("spans"), sem("bcast_flag"), sem("bases")
        turned, taken, stored, rows_made = sem("turned"), sem("taken"), sem("rows_stored"), sem("rows_made")
        flag_made, base_made, rel_made = sem("flag_made"), sem("base_made"), sem("rel_made")
        block = c.enter_context(nc.Block())

        parts = [(b, min(P, full - b * P)) for b in range(NB) if full > b * P]

        @block.sync
        def _(sp):
            sp.wait_ge(padded, 4)
            for k, a in (("dst", dst), ("src", src), ("t9", type9), ("t50", type50)):
                g = a[0:full * GE].rearrange("(g e) -> g e", e=GE)
                for b, n in parts:
                    sp.dma_start(raw[k][0:n, b, :], g[b * P:b * P + n, :]).then_inc(loaded, 16)
                if rest:
                    q, b = full % P, full // P
                    sp.dma_start(raw[k][q:q + 1, b, 0:rest],
                                 a[full * GE:S.E].rearrange("(g e) -> g e", g=1)).then_inc(loaded, 16)
            sp.wait_ge(rows_made, 5)
            n = 0
            for b in range(NB):
                m = min(P, NGP - b * P)
                sp.dma_start(t["rows5"][b * P:b * P + m, :, :], rows[0:m, b, :, :]).then_inc(stored, 16)
                n += 16
            sp.wait_ge(taken, 3 * NB)
            sp.dma_start(t["T9"], type9_cols[:, :]).then_inc(stored, 16)
            sp.wait_ge(stored, n + 16)

        @block.gpsimd
        def _(pool):
            pool.memset(raw["dst"][:, :, :], int(FAR)).then_inc(padded, 1)
            for k in ("src", "t9", "t50"):
                pool.memset(raw[k][:, :, :], -1).then_inc(padded, 1)
            pool.memset(t["ident"][:, :], 0.0).then_inc(consts, 1)
            pool.wait_ge(consts, 1)
            pool.affine_select(out=t["ident"][:, :], in_=t["ident"][:, :], compare_op=ALU.not_equal,
                               fill=1.0, base=0, pattern=[[-1, P]], channel_multiplier=1).then_inc(consts, 1)
            pool.iota(t["iota"][:, :], pattern=[[1, P]], base=0, channel_multiplier=0,
                      allow_small_or_imprecise_dtypes=True).then_inc(consts, 1)
            pool.iota(t["pcol"][:, :], pattern=[[0, 1]], base=0, channel_multiplier=1,
                      allow_small_or_imprecise_dtypes=True).then_inc(consts, 1)
            pool.memset(one_row[:, :], 1.0).then_inc(consts, 1)
            pool.iota(t["win0"][:, :], pattern=[[W, S.NWIN]], base=0, channel_multiplier=0,
                      allow_small_or_imprecise_dtypes=True).then_inc(consts, 1)
            pool.iota(t["win_far"][:, :], pattern=[[1024, S.NWIN]], base=0, channel_multiplier=0,
                      allow_small_or_imprecise_dtypes=True).then_inc(consts, 1)

        @block.vector
        def _(v):
            link = Link(v, step)
            v.wait_ge(loaded, 4 * 16 * (len(parts) + (1 if rest else 0)))
            v.wait_ge(consts, 7)
            link(v.tensor_copy(dst_f[:, :, :], raw["dst"][:, :, :]), False)
            link(v.tensor_copy(src_f[:, :, :], raw["src"][:, :, :]), False)
            link(v.tensor_scalar(t9_f[:, :, :], raw["t9"][:, :, :], 0.0, float(T9 - 1), ALU.max, ALU.min))
            link(v.tensor_reduce(dmax[:, :], dst_f[:, :, :], AX_X, ALU.max), False)
            link(v.tensor_scalar(low[:, :, :], dst_f[:, :, :], 0.0, -2.0 * FAR, ALU.is_lt, ALU.mult))
            link(v.tensor_tensor(low[:, :, :], low[:, :, :], dst_f[:, :, :], ALU.add))
            link(v.tensor_reduce(dmin[:, :], low[:, :, :], AX_X, ALU.min))
            link(v.tensor_tensor(span[:, :], dmax[:, :], dmin[:, :], ALU.subtract))
            link(v.tensor_reduce(spanmax[:, :], span[:, :], AX_X, ALU.max))
            v.sem_inc(spans, 1)
            v.wait_ge(bcast_flag, 1)
            link(v.tensor_reduce(wide_f[:, :], ps_small[0:1, 0:P], AX_X, ALU.max))
            link(v.tensor_scalar(wide_f[:, :], wide_f[:, :], float(W) - 0.5, None, ALU.is_gt))
            link(v.tensor_copy(t["wide"][:, :], wide_f[:, :]))
            v.sem_inc(flag_made, 1)
            v.wait_ge(bcast_flag, 2)
            link(v.tensor_scalar(narrow[:, :], ps_small[:, 256:257], -1.0, 1.0, ALU.mult, ALU.add))
            link(v.tensor_scalar(base[:, :], dmin[:, :], float(S.N - 1), narrow[:, 0:1], ALU.min, ALU.mult))
            v.sem_inc(base_made, 1)
            for b in range(NB):
                link(v.tensor_scalar(dst_f[:, b, :], dst_f[:, b, :], base[:, b:b + 1], None, ALU.subtract))
            v.sem_inc(rel_made, 1)
            v.wait_ge(bases, 1)
            link(v.tensor_copy(t["base"][0:1, 0:NB * P], ps_base[0:1, 0:NB * P]))
            for k, a in ((0, dst_f), (2, src_f)):
                link(v.tensor_copy(whole[:, :, :], a[:, :, :]))
                link(v.tensor_scalar(part[:, :, :], whole[:, :, :], ~(P - 1), None, ALU.bitwise_and))
                v.tensor_copy(rows[:, :, k, :], part[:, :, :]).then_inc(rows_made, 1)
                v.wait_ge(rows_made, k + 1)
                link(v.tensor_scalar(part[:, :, :], whole[:, :, :], P - 1, None, ALU.bitwise_and))
                v.tensor_copy(rows[:, :, k + 1, :], part[:, :, :]).then_inc(rows_made, 1)
                v.wait_ge(rows_made, k + 2)
            v.tensor_scalar(rows[:, :, 4, :], raw["t50"][:, :, :], 0.0, float(T50 - 1),
                            ALU.max, ALU.min).then_inc(rows_made, 1)
            n = 0
            for out in (t["dst_rel"], cols, type9_cols):
                for b in range(NB):
                    m = min(P, NGP - b * P)
                    v.wait_ge(turned, n + 1)
                    v.tensor_copy(out[:, b * P * J:(b * P + m) * J].rearrange("p (q j) -> p j q", j=J),
                                  ps_t[n % 2][:, :, 0:m]).then_inc(taken, 1)
                    n += 1
            v.wait_ge(taken, n)
            link(v.tensor_scalar(unique[:, :], t["pcol"][:, :], float(S.NP + 1), None, ALU.add))
            link(v.tensor_scalar(below[:, :], cols[:, :], 0.0, unique[:, 0:1], ALU.is_lt, ALU.mult))
            link(v.tensor_tensor(t["src_i"][:, :], cols[:, :], below[:, :], ALU.add))

        @block.tensor
        def _(pe):
            pe.wait_ge(consts, 7)
            pe.wait_ge(spans, 1)
            pe.transpose(ps_small[0:1, 0:P], spanmax[:, :], t["ident"][:, :]).then_inc(bcast_flag, 1)
            pe.wait_ge(flag_made, 1)
            pe.matmul(ps_small[:, 256:257], one_row[:, :], wide_f[:, :], start=True, stop=True).then_inc(bcast_flag, 1)
            pe.wait_ge(base_made, 1)
            for b in range(NB):
                mm = pe.matmul(ps_base[0:1, b * P:(b + 1) * P], base[:, b:b + 1], t["ident"][:, :],
                               start=True, stop=True)
            mm.then_inc(bases, 1)
            pe.wait_ge(rel_made, 1)
            n = 0
            for a in (dst_f, src_f, t9_f):
                for b in range(NB):
                    if n >= 2:
                        pe.wait_ge(taken, n - 1)
                    for j in range(J):
                        mm = pe.transpose(ps_t[n % 2][:, j, :], a[:, b, :].rearrange("q (p j) -> q j p", j=J)[:, j, :],
                                          t["ident"][:, :])
                    mm.then_inc(turned, 1)
                    n += 1


def norm_constants(link, v, stats, mean, var, tmp):
    link(v.tensor_tensor(mean[:, :], stats[:, :, 1], stats[:, :, 4], ALU.add), False)
    link(v.tensor_tensor(tmp[:, :], stats[:, :, 1], stats[:, :, 4], ALU.subtract), False)
    link(v.tensor_tensor(var[:, :], stats[:, :, 2], stats[:, :, 5], ALU.add))
    link(v.tensor_scalar(mean[:, :], mean[:, :], 0.5, None, ALU.mult), False)
    link(v.scalar_tensor_tensor(tmp[:, :], tmp[:, :], 0.25, tmp[:, :], ALU.mult, ALU.mult), False)
    link(v.tensor_scalar(var[:, :], var[:, :], 1.0 / F, EPS, ALU.mult, ALU.add))
    link(v.tensor_tensor(var[:, :], var[:, :], tmp[:, :], ALU.add))


def first_norm_phase(nc, S, x, t):
    NT, N = S.NT, S.N
    full, rest = N // P, N % P
    with ExitStack() as c:
        sb = lambda n, s, d=F32: c.enter_context(nc.sbuf_tensor(n, s, d))
        sem = lambda n: c.enter_context(nc.semaphore(n))
        TR = S.NR // P
        xs = sb("xs", [P, TR, F])
        hs = sb("hs", [P, TR, F])
        stats = sb("n0_stats", [P, NT, 6])
        mean, var, tmp = sb("n0_mean", [P, NT]), sb("n0_var", [P, NT]), sb("n0_tmp", [P, NT])
        cleared, loaded, step = sem("n0_cleared"), sem("n0_loaded"), sem("n0_step")
        stat, roots, ready, normed, stored = sem("n0_stat"), sem("n0_roots"), sem("n0_ready"), sem("n0_normed"), sem("n0_stored")
        block = c.enter_context(nc.Block())

        @block.sync
        def _(sp):
            sp.wait_ge(cleared, 2)
            sp.dma_start(xs[:, 0:full, :], x[0:full * P, :].rearrange("(n p) f -> p n f", p=P)).then_inc(loaded, 16)
            if rest:
                sp.dma_start(xs[0:rest, full, :], x[full * P:N, :]).then_inc(loaded, 16)
            sp.wait_ge(loaded, 16 * (1 + bool(rest)))
            sp.dma_start(t["X0"].rearrange("(n p) f -> p n f", p=P), xs[:, :, :]).then_inc(stored, 16)
            sp.wait_ge(normed, NT)
            sp.dma_start(t["H0"].rearrange("(n p) f -> p n f", p=P), hs[:, :, :]).then_inc(stored, 16)
            sp.wait_ge(stored, 32)

        @block.vector
        def _(v):
            v.memset(xs[:, full:TR, :], 0.0).then_inc(cleared, 1)
            v.memset(hs[:, NT:TR, :], 0.0).then_inc(cleared, 1)
            v.wait_ge(cleared, 2)
            v.wait_ge(loaded, 16 * (1 + bool(rest)))
            with v.Fori(0, NT) as i:
                v.bn_stats(stats[:, ds(i, 1), :], xs[:, ds(i, 1), :]).then_inc(stat, 1)
            v.wait_ge(stat, NT)
            link = Link(v, step)
            norm_constants(link, v, stats, mean, var, tmp)
            v.sem_inc(roots, 1)
            v.wait_ge(roots, 2)
            link(v.reciprocal(var[:, :], var[:, :]))
            link(v.scalar_tensor_tensor(mean[:, :], mean[:, :], -1.0, var[:, :], ALU.mult, ALU.mult))
            v.sem_inc(ready, 1)

        @block.scalar
        def _(act):
            act.wait_ge(roots, 1)
            act.activation(var[:, :], var[:, :], ACT.Sqrt).then_inc(roots, 1)
            act.wait_ge(ready, 1)
            with act.Fori(0, NT) as i:
                act.activation(hs[:, ds(i, 1), :], xs[:, ds(i, 1), :], ACT.Relu, bias=mean[:, ds(i, 1)],
                               scale=var[:, ds(i, 1)]).then_inc(normed, 1)


def forms(eng, S, t, turn, after=None, last_apart=False):
    turns = S.NGP // U
    in_loop = turns - last_apart
    wide = eng.value_load(t["wide"][0:1, 0:1], min_val=0, max_val=1)

    def run(NW, turn_i):
        if in_loop:
            with eng.Fori(0, in_loop) as i:
                turn_i(i)
        if last_apart:
            turn_i(turns - 1)
        if after is not None:
            after(turns * NW)

    def every_window(i):
        with eng.Fori(0, S.NWIN) as w:
            turn(i, w + i * S.NWIN, w)

    with eng.If(wide > 0):
        run(S.NWIN, every_window)
    with eng.Else():
        run(1, lambda i: turn(i, i, None))


def window_start(eng, S, t, g, w):
    if w is None:
        return eng.value_load(t["base"][0:1, ds(g, 1)], min_val=0, max_val=S.N - 1)
    return w * W


def one_hot(v, t, out, g, w, op=ALU.is_equal):
    rel = bcast(t["dst_rel"][:, ds(g * J, J)], 2, W)
    window = bcast(t["iota"][:, 0:W], 1, J)
    if w is None:
        return v.tensor_tensor(out, rel, window, op)
    return v.scalar_tensor_tensor(out, rel, t["win0"][:, ds(w, 1)], window, ALU.subtract, op)


def sum_phase(nc, S, t, tag, table, types):
    NGP = S.NGP
    acc, acc9 = t["big"][:, 0, :], t["big"][0:T9, 1, :]
    HI = S.NT
    per = 2 if types else 1
    hots = 4 if types else 1
    with ExitStack() as c:
        sb = lambda n, s, d=F32: c.enter_context(nc.sbuf_tensor(f"{tag}_{n}", s, d))
        sem = lambda n: c.enter_context(nc.semaphore(f"{tag}_{n}"))
        ps = lambda n, s: c.enter_context(nc.psum_tensor(f"{tag}_{n}", s, F32))
        slot = sb("slot", [P, U, J], I32)
        rows = sb("rows", [P, U, J, F])
        onehot = sb("onehot", [P, U, J, W])
        ps_sum = [ps(f"sum{k}", [P, 512]) for k in range(2)]
        idx_ready, multiplied, made, added = sem("idx_ready"), sem("multiplied"), sem("made"), sem("added")
        gathered = [sem(f"gathered{k}") for k in range(U)]
        if types:
            kind = sb("kind", [P, U, J, T9])
            type9 = sb("type9", [P, NGP * J])
            lo_i, hi_i = sb("lo_i", [P, NGP * J], I32), sb("hi_i", [P, NGP * J], I32)
            lo, hi = sb("lo", [P, NGP * J]), sb("hi", [P, NGP * J])
            lo_hot, hi_hot = sb("lo_hot", [P, U, J, P], BF16), sb("hi_hot", [P, U, J, HI], BF16)
            none = sb("none", [P, P], BF16)
            zeros = sb("zeros", [P, S.NR // 4])
            ps_kind = [ps(f"kind{k}", [P, 512]) for k in range(2)]
            ps_hist = ps("hist", [P, 512])
            start, cleared, prep, counts = sem("start"), sem("cleared"), sem("prep"), sem("counts")
        block = c.enter_context(nc.Block())

        if types:
            @block.sync
            def _(sp):
                sp.dma_start(type9[:, :], t["T9"]).then_inc(prep, 16)
                sp.wait_ge(start, 1)
                n = 0
                for k in range(COPIES):
                    flat = t["scat"][k].rearrange("(p n) f -> p (n f)", p=P)
                    for q in range(4):
                        sp.dma_start(flat[:, q * (S.NR // 4):(q + 1) * (S.NR // 4)], zeros[:, :]).then_inc(cleared, 16)
                        n += 16
                sp.wait_ge(cleared, n)

        @block.gpsimd
        def _(pool):
            def turn(i, r, w):
                for s in range(U):
                    pool.wait_ge(idx_ready, r * U + s + 1)
                    pool.nop(nofuse=True)
                    for j in range(J):
                        pool.indirect_dma_start(rows[:, s, j, :], None, table,
                                                bass.IndirectOffsetOnAxis(ap=slot[:, s, j:j + 1], axis=0)
                                                ).then_inc(gathered[s], 16)
            forms(pool, S, t, turn)

        @block.scalar
        def _(act):
            def turn(i, r, w):
                for s in range(U):
                    act.wait_ge(multiplied, r * U + s + 1)
                    act.activation(slot[:, s, :], t["src_i"][:, ds((i * U + s) * J, J)], ACT.Copy).then_inc(idx_ready, 1)
            forms(act, S, t, turn)

        @block.vector
        def _(v):
            v.memset(acc, 0.0).then_inc(added, 1)
            if types:
                v.memset(acc9, 0.0).then_inc(added, 1)
                v.memset(none[:, :], 0.0).then_inc(counts, 1)
                v.memset(zeros[:, :], 0.0).then_inc(start, 1)
                v.tensor_scalar(hi_i[:, :], t["src_i"][:, :], 7, None, ALU.arith_shift_right).then_inc(prep, 1)
                v.tensor_scalar(lo_i[:, :], t["src_i"][:, :], P - 1, None, ALU.bitwise_and).then_inc(prep, 1)
                v.wait_ge(prep, 18)
                v.tensor_copy(hi[:, :], hi_i[:, :]).then_inc(prep, 1)
                v.tensor_copy(lo[:, :], lo_i[:, :]).then_inc(prep, 1)
                v.wait_ge(prep, 20)
            v.sem_inc(added, 2 * per)

            def turn(i, r, w):
                for s in range(U):
                    n, g = r * U + s, i * U + s
                    v.wait_ge(multiplied, n + 1)
                    one_hot(v, t, onehot[:, s, :, :], g, w).then_inc(made, 1)
                    if types:
                        v.tensor_tensor(kind[:, s, :, :], bcast(type9[:, ds(g * J, J)], 2, T9),
                                        bcast(t["iota"][:, 0:T9], 1, J), ALU.is_equal).then_inc(made, 1)
                        rel, io = bcast(lo[:, ds(g * J, J)], 2, P), bcast(t["iota"][:, 0:P], 1, J)
                        if w is None:
                            v.tensor_tensor(lo_hot[:, s, :, :], rel, io, ALU.is_equal).then_inc(made, 1)
                        else:
                            v.scalar_tensor_tensor(lo_hot[:, s, :, :], rel, t["win_far"][:, ds(w, 1)], io,
                                                   ALU.add, ALU.is_equal).then_inc(made, 1)
                        v.tensor_tensor(hi_hot[:, s, :, :], bcast(hi[:, ds(g * J, J)], 2, HI),
                                        bcast(t["iota"][:, 0:HI], 1, J), ALU.is_equal).then_inc(made, 1)
                for s in range(U):
                    n, g = r * U + s, i * U + s
                    at = window_start(v, S, t, g, w)
                    v.wait_ge(multiplied, n + U + 1)
                    v.wait_ge(added, n * per + 3 * per)
                    v.tensor_tensor(acc[:, ds(at, W)], acc[:, ds(at, W)], ps_sum[s % 2][:, 0:W], ALU.add).then_inc(added, 1)
                    if types:
                        v.tensor_tensor(acc9[:, ds(at, W)], acc9[:, ds(at, W)], ps_kind[s % 2][0:T9, 0:W],
                                        ALU.add).then_inc(added, 1)
            forms(v, S, t, turn)
            if types:
                v.wait_ge(counts, 2)
                v.tensor_copy(t["deg_src"][:, :], ps_hist[:, 0:HI]).then_inc(counts, 1)

        @block.tensor
        def _(pe):
            if types:
                pe.wait_ge(counts, 1)
                pe.matmul(ps_hist[:, 0:HI], none[:, :], none[:, 0:HI], start=True, stop=False, skip_group_check=True)
            pe.sem_inc(multiplied, U)

            def turn(i, r, w):
                for s in range(U):
                    n = r * U + s
                    pe.wait_ge(made, n * hots + hots)
                    pe.wait_ge(added, n * per + 2 * per)
                    pe.wait_ge(gathered[s], r * (16 * J) + 16 * J)
                    for j in range(J):
                        mm = pe.matmul(ps_sum[s % 2][:, 0:W], rows[:, s, j, :], onehot[:, s, j, :],
                                       start=(j == 0), stop=(j == J - 1))
                    if types:
                        for j in range(J):
                            pe.matmul(ps_kind[s % 2][0:T9, 0:W], kind[:, s, j, :], onehot[:, s, j, :],
                                      start=(j == 0), stop=(j == J - 1))
                        for j in range(J):
                            mm = pe.matmul(ps_hist[:, 0:HI], lo_hot[:, s, j, :], hi_hot[:, s, j, :],
                                           start=False, stop=False, skip_group_check=True)
                    mm.then_inc(multiplied, 1)
            forms(pe, S, t, turn)
            if types:
                pe.matmul(ps_hist[:, 0:HI], none[:, :], none[:, 0:HI], start=False, stop=True,
                          skip_group_check=True).then_inc(counts, 1)


WEIGHTS = {
    "msg_wT": F, "ih_wT": 3 * F, "hh_wT": 3 * F, "gcn_wT": F, "bases": 4 * F, "node_wT": F, "edge_wT": 2 * F, "out_wT": F,
    "gate_b": 4 * F, "gcn_b": F, "gcn_gamma": F, "gcn_beta": F, "proj_b": F, "attn": F, "out_b": F,
    "out_gamma": F, "out_beta": F, "embed_b": F, "relation": 4 * F // 2, "ones": 1,
}


def weights_phase(nc, S, a, t):
    with ExitStack() as c:
        sb = lambda n, s, d=F32: c.enter_context(nc.sbuf_tensor(f"w_{n}", s, d))
        sem = lambda n: c.enter_context(nc.semaphore(f"w_{n}"))
        square = [("L0_gnn_W_msg", 0, "msg_wT", 0), ("L1_gnn_W", 0, "gcn_wT", 0), ("L3_gnn_W_out_w", 0, "out_wT", 0),
                  ("L3_gnn_W_proj_w", 0, "node_wT", 0)]
        square += [("L0_gnn_W_ih", q, "ih_wT", q) for q in range(3)] + [("L0_gnn_W_hh", q, "hh_wT", q) for q in range(3)]
        nat = sb("natural", [P, len(square), F])
        edge_nat = sb("edge_natural", [P, 2, ED])
        bias2 = sb("bias2", [P, 3 * F])
        msg_b = sb("msg_b", [T9, F])
        comps, alpha = sb("comps", [T50, 4]), sb("alpha", [T50, 1])
        ps = [c.enter_context(nc.psum_tensor(f"w_ps{k}", [P, 512], F32)) for k in range(2)]
        loaded, turned, taken, step = sem("loaded"), sem("turned"), sem("taken"), sem("step")
        block = c.enter_context(nc.Block())
        row = lambda ap, n=P: ap.rearrange("(a f) -> a f", a=1).broadcast_to([n, ap.shape[0]])
        loads = [(nat[:, m, :], a[w][q * P:(q + 1) * P, 0:F]) for m, (w, q, _, _) in enumerate(square)]
        loads += [(edge_nat[:, h, :], a["L3_gnn_W_proj_w"][:, F:F + ED]) for h in range(2)]
        loads += [(t["bases"][:, b * F:(b + 1) * F], a["L2_gnn_bases"][b]) for b in range(4)]
        loads += [(t["gate_b"][:, 0:3 * F], row(a["L0_gnn_b_ih"])), (bias2[:, :], row(a["L0_gnn_b_hh"])),
                  (msg_b[:, :], row(a["L0_gnn_b_msg"], T9)), (t["embed_b"][0:T9, :], a["L0_gnn_edge_embed"]),
                  (comps[:, :], a["L2_gnn_comps"]), (alpha[:, :], a["L2_gnn_alpha"]),
                  (t["gcn_b"][:, :], row(a["L1_gnn_b"])), (t["gcn_gamma"][:, :], row(a["L1_gnn_gamma"])),
                  (t["gcn_beta"][:, :], row(a["L1_gnn_beta"])), (t["proj_b"][:, :], row(a["L3_gnn_W_proj_b"])),
                  (t["attn"][:, :], row(a["L3_gnn_attn_vec"].rearrange("h d -> (h d)"))),
                  (t["out_b"][:, :], row(a["L3_gnn_W_out_b"])), (t["out_gamma"][:, :], row(a["L3_gnn_ln_gamma"])),
                  (t["out_beta"][:, :], row(a["L3_gnn_ln_beta"]))]

        @block.sync
        def _(sp):
            for to, of in loads:
                sp.dma_start(to, of).then_inc(loaded, 16)

        @block.tensor
        def _(pe):
            pe.wait_ge(loaded, 16 * len(loads))
            for m in range(len(square)):
                if m >= 2:
                    pe.wait_ge(taken, m - 1)
                pe.transpose(ps[m % 2][:, 0:P], nat[:, m, :], t["ident"][:, :]).then_inc(turned, 1)
            m = len(square)
            pe.wait_ge(taken, m - 1)
            pe.transpose(ps[m % 2][:, 0:P], edge_nat[:, :, :].rearrange("p h f -> p (h f)"), t["ident"][:, :]).then_inc(turned, 1)

        @block.vector
        def _(v):
            v.wait_ge(loaded, 16 * len(loads))
            link = Link(v, step)
            for m, (_, _, to, q) in enumerate(square):
                v.wait_ge(turned, m + 1)
                v.tensor_copy(t[to][:, q * F:(q + 1) * F], ps[m % 2][:, 0:P]).then_inc(taken, 1)
            link(v.memset(t["edge_wT"][:, :], 0.0))
            m = len(square)
            v.wait_ge(turned, m + 1)
            for h in range(2):
                link(v.tensor_copy(t["edge_wT"][h * ED:(h + 1) * ED, h * F:(h + 1) * F], ps[m % 2][h * ED:(h + 1) * ED, 0:P]), False)
            link(v.tensor_copy(t["gate_b"][:, 3 * F:4 * F], bias2[:, 2 * F:3 * F]), False)
            link(v.tensor_tensor(t["gate_b"][:, 0:2 * F], t["gate_b"][:, 0:2 * F], bias2[:, 0:2 * F], ALU.add), False)
            link(v.tensor_tensor(t["embed_b"][0:T9, :], t["embed_b"][0:T9, :], msg_b[:, :], ALU.add), False)
            link(v.memset(t["ones"][:, :], 1.0), False)
            link(v.tensor_scalar(comps[:, :], comps[:, :], alpha[:, 0:1], None, ALU.mult))
            link(v.tensor_copy(t["relation"][0:T50, :].rearrange("p (b n) -> p b n", b=4), bcast(comps[:, :], 2, W)), False)


def tiles_of(table, at, n):
    return table.rearrange("(n p) f -> p n f", p=P)[:, ds(at, n), :]


def gru_phase(nc, S, t):
    NT, NR, PAIRS = S.NT, S.NR, S.NTP // 2
    acc, acc9 = t["big"][:, 0, :], t["big"][0:T9, 1, :]
    with ExitStack() as c:
        sb = lambda n, s, d=F32: c.enter_context(nc.sbuf_tensor(f"gru_{n}", s, d))
        sem = lambda n: c.enter_context(nc.semaphore(f"gru_{n}"))
        ps = lambda n, s: c.enter_context(nc.psum_tensor(f"gru_{n}", s, F32))
        res = sb("res", [P, S.NTP, F])
        h_a, h_b, x_b = sb("h_a", [P, 2, F]), sb("h_b", [P, 2, F]), sb("x_b", [P, 2, F])
        aggs, kinds = sb("aggs", [P, 2 * P]), sb("kinds", [T9, 2 * P])
        msgT, hT = sb("msgT", [P, 2 * P]), sb("hT", [P, 2 * P])
        gates, rz, cand, n_out = sb("gates", [P, 2, 4 * F]), sb("rz", [P, 2, 2 * F]), sb("cand", [P, 2, F]), sb("n_out", [P, 2, F])
        stats = sb("stats", [P, S.NTP, 6])
        mean, var, tmp, deg = (sb(n, [P, S.NTP]) for n in ("mean", "var", "tmp", "deg"))
        ps_msg, ps_h, ps_g, ps_deg = ps("ps_msg", [P, 512]), ps("ps_h", [P, 512]), ps("ps_g", [P, 2, 512]), ps("ps_deg", [P, 512])
        h_in, b_in, turned, staged, messaged = sem("h_in"), sem("b_in"), sem("turned"), sem("staged"), sem("messaged")
        copied, gated, gate_free, dv, acted = sem("copied"), sem("gated"), sem("gate_free"), sem("dv"), sem("acted")
        fin, roots, normed, stored = sem("fin"), sem("roots"), sem("normed"), sem("stored")
        C = 9
        block = c.enter_context(nc.Block())

        @block.sync
        def _(sp):
            def ahead(j):
                sp.wait_ge(turned, j + 1)
                sp.dma_start(h_a[:, :, :], tiles_of(t["H0"], j * 2, 2)).then_inc(h_in, 16)
            ahead(0)
            with sp.Fori(0, PAIRS) as i:
                ahead(i + 1)
                sp.wait_ge(dv, i * C + C)
                sp.dma_start(h_b[:, :, :], tiles_of(t["H0"], i * 2, 2)).then_inc(b_in, 16)
                sp.dma_start(x_b[:, :, :], tiles_of(t["X0"], i * 2, 2)).then_inc(b_in, 16)
            sp.wait_ge(dv, PAIRS * C + C)
            sp.dma_start(tiles_of(t["X1"], 0, S.NTP), res[:, :, :]).then_inc(stored, 16)
            sp.wait_ge(normed, NT + 1)
            sp.dma_start(tiles_of(t["H1"], 0, NR // P), acc.rearrange("p (n f) -> p n f", f=F)).then_inc(stored, 16)
            sp.wait_ge(stored, 32)
            sp.wait_ge(h_in, 16 * PAIRS + 16)

        @block.tensor
        def _(pe):
            pe.sem_inc(turned, 1)
            pe.sem_inc(gated, 1)

            def ahead(j):
                pe.wait_ge(h_in, j * 16 + 16)
                pe.wait_ge(copied, j * 2 + 2)
                for k in range(2):
                    mm = pe.transpose(ps_h[:, k * P:(k + 1) * P], h_a[:, k, :], t["ident"][:, :])
                mm.then_inc(turned, 1)
                pe.wait_ge(staged, j * 2 + 2)
                pe.matmul(ps_msg[:, 0:2 * P], t["msg_wT"][:, :], aggs[:, :], start=True, stop=False)
                pe.matmul(ps_msg[:, 0:2 * P], t["embed_b"][0:T9, :], kinds[:, :], start=False, stop=True).then_inc(messaged, 1)
                pe.wait_ge(copied, j * 2 + 4)
                pe.wait_ge(gate_free, j * 2 + 2)
                for k in range(2):
                    m, h = msgT[:, k * P:(k + 1) * P], hT[:, k * P:(k + 1) * P]
                    pe.matmul(ps_g[:, k, 0:2 * F], m, t["ih_wT"][:, 0:2 * F], start=True, stop=False)
                    pe.matmul(ps_g[:, k, 0:2 * F], h, t["hh_wT"][:, 0:2 * F], start=False, stop=True)
                    pe.matmul(ps_g[:, k, 2 * F:3 * F], m, t["ih_wT"][:, 2 * F:3 * F], start=True, stop=True)
                    pe.matmul(ps_g[:, k, 3 * F:4 * F], h, t["hh_wT"][:, 2 * F:3 * F], start=True, stop=True)
                    mm = pe.matmul(ps_deg[:, k:k + 1], kinds[:, k * P:(k + 1) * P], t["ones"][0:T9, :], start=True, stop=True)
                mm.then_inc(gated, 1)
            ahead(0)
            with pe.Fori(0, PAIRS) as i:
                ahead(i + 1)

        @block.scalar
        def _(act):
            act.sem_inc(copied, 2)

            def ahead(j):
                act.wait_ge(gated, j + 1)
                act.activation(aggs[:, :], acc[:, ds(j * (2 * P), 2 * P)], ACT.Copy).then_inc(staged, 1)
                act.activation(kinds[:, :], acc9[:, ds(j * (2 * P), 2 * P)], ACT.Copy).then_inc(staged, 1)
                act.wait_ge(turned, j + 2)
                act.activation(hT[:, :], ps_h[:, 0:2 * P], ACT.Copy).then_inc(copied, 1)
                act.wait_ge(messaged, j + 1)
                act.activation(msgT[:, :], ps_msg[:, 0:2 * P], ACT.Copy).then_inc(copied, 1)
            ahead(0)
            with act.Fori(0, PAIRS) as i:
                ahead(i + 1)
                act.wait_ge(dv, i * C + C + 1)
                act.activation(rz[:, :, :], gates[:, :, 0:2 * F], ACT.Sigmoid).then_inc(acted, 1)
                act.wait_ge(dv, i * C + C + 4)
                act.activation(n_out[:, :, :], cand[:, :, :], ACT.Tanh).then_inc(acted, 1)
            act.wait_ge(roots, 1)
            act.activation(var[:, :], var[:, :], ACT.Sqrt).then_inc(roots, 1)
            act.activation(deg[:, :], deg[:, :], ACT.Sqrt).then_inc(roots, 1)
            act.wait_ge(roots, 4)
            with act.Fori(0, NT) as i:
                act.activation(acc[:, ds(i * F, F)], res[:, ds(i, 1), :], ACT.Relu, bias=mean[:, ds(i, 1)],
                               scale=var[:, ds(i, 1)]).then_inc(normed, 1)

        @block.vector
        def _(v):
            v.sem_inc(gate_free, 2)
            v.sem_inc(dv, C)
            with v.Fori(0, PAIRS) as i:
                link = Link(v, dv, i * C + C)
                v.wait_ge(gated, i + 2)
                link(v.tensor_tensor(gates[:, :, :], ps_g[:, :, :], bcast(t["gate_b"][:, :], 1, 2), ALU.add))
                v.sem_inc(gate_free, 1)
                link(v.tensor_copy(deg[:, ds(i * 2, 2)], ps_deg[:, 0:2]))
                v.sem_inc(gate_free, 1)
                v.wait_ge(acted, i * 2 + 1)
                link(v.tensor_tensor(cand[:, :, :], rz[:, :, 0:F], gates[:, :, 3 * F:4 * F], ALU.mult))
                link(v.tensor_tensor(cand[:, :, :], cand[:, :, :], gates[:, :, 2 * F:3 * F], ALU.add))
                v.wait_ge(acted, i * 2 + 2)
                v.wait_ge(b_in, i * 32 + 32)
                link(v.tensor_tensor(h_b[:, :, :], h_b[:, :, :], n_out[:, :, :], ALU.subtract))
                link(v.tensor_tensor(h_b[:, :, :], h_b[:, :, :], rz[:, :, F:2 * F], ALU.mult))
                link(v.tensor_tensor(h_b[:, :, :], h_b[:, :, :], n_out[:, :, :], ALU.add))
                x1 = res[:, ds(i * 2, 2), :]
                link(v.tensor_tensor(x1, h_b[:, :, :], x_b[:, :, :], ALU.add))
                v.bn_stats(stats[:, ds(i * 2, 1), :], res[:, ds(i * 2, 1), :])
                link(v.bn_stats(stats[:, ds(i * 2 + 1, 1), :], res[:, ds(i * 2 + 1, 1), :]), False)
                assert link.n == C
            v.wait_ge(dv, PAIRS * C + C)
            v.wait_ge(gated, PAIRS + 2)
            link = Link(v, fin)
            norm_constants(link, v, stats, mean, var, tmp)
            link(v.tensor_scalar(deg[:, :], deg[:, :], 1.0, None, ALU.add))
            v.sem_inc(roots, 1)
            v.wait_ge(roots, 3)
            link(v.reciprocal(var[:, :], var[:, :]))
            link(v.reciprocal(t["dinv_in"][:, :], deg[:, :]))
            link(v.tensor_tensor(var[:, :], var[:, :], t["dinv_in"][:, :], ALU.mult))
            link(v.scalar_tensor_tensor(mean[:, :], mean[:, :], -1.0, var[:, :], ALU.mult, ALU.mult))
            v.memset(acc[:, NT * F:NR], 0.0).then_inc(normed, 1)
            v.sem_inc(roots, 1)


def normed_sum(v, link, res, i, mean, var, gamma, beta, x_old):
    for k in range(Q):
        at = i * Q + k
        link(v.tensor_scalar(res[:, ds(at, 1), :], res[:, ds(at, 1), :], mean[:, ds(at, 1)], var[:, ds(at, 1)],
                             ALU.subtract, ALU.mult), k == Q - 1)
    four = res[:, ds(i * Q, Q), :]
    link(v.tensor_tensor(four, four, bcast(gamma[:, :], 1, Q), ALU.mult))
    link(v.tensor_tensor(four, four, bcast(beta[:, :], 1, Q), ALU.add))
    link(v.tensor_tensor(four, four, x_old, ALU.add))


def gcn_phase(nc, S, t):
    NT, TURNS = S.NT, S.NTP // Q
    acc = t["big"][:, 0, :]
    with ExitStack() as c:
        sb = lambda n, s, d=F32: c.enter_context(nc.sbuf_tensor(f"gcn_{n}", s, d))
        sem = lambda n: c.enter_context(nc.semaphore(f"gcn_{n}"))
        ps = lambda n, s: c.enter_context(nc.psum_tensor(f"gcn_{n}", s, F32))
        res = sb("res", [P, S.NTP, F])
        mean, var, tmp = (sb(n, [P, S.NTP]) for n in ("mean", "var", "tmp"))
        blocks = c.enter_context(ExitStack())
        own = lambda n, s: blocks.enter_context(nc.sbuf_tensor(f"gcn_{n}", s, F32))
        h_q, aggs, x_q = own("h_q", [P, Q, F]), own("aggs", [P, Q * P]), own("x_q", [P, Q, F])
        stats = own("stats", [P, S.NTP, 6])
        ps_h, ps_o = ps("ps_h", [P, 512]), ps("ps_o", [P, 512])
        h_in, x_in, turned, multiplied, dv = sem("h_in"), sem("x_in"), sem("turned"), sem("multiplied"), sem("dv")
        dv2, fin, roots, stored = sem("dv2"), sem("fin"), sem("roots"), sem("stored")
        C, C2 = 9, 11
        block = blocks.enter_context(nc.Block())

        @block.sync
        def _(sp):
            with sp.Fori(0, TURNS) as i:
                sp.wait_ge(turned, i + 1)
                sp.dma_start(h_q[:, :, :], tiles_of(t["H1"], i * Q, Q)).then_inc(h_in, 16)
            with sp.Fori(0, TURNS) as i:
                sp.wait_ge(dv2, i * C2 + C2)
                sp.dma_start(x_q[:, :, :], tiles_of(t["X1"], i * Q, Q)).then_inc(x_in, 16)
            sp.wait_ge(dv2, TURNS * C2 + C2)
            sp.dma_start(tiles_of(t["X2"], 0, S.NTP), res[:, :, :]).then_inc(stored, 16)
            sp.wait_ge(stored, 16)

        @block.tensor
        def _(pe):
            pe.sem_inc(turned, 1)
            with pe.Fori(0, TURNS) as i:
                pe.wait_ge(h_in, i * 16 + 16)
                pe.wait_ge(dv, i * C + C)
                for k in range(Q):
                    mm = pe.transpose(ps_h[:, k * P:(k + 1) * P], h_q[:, k, :], t["ident"][:, :])
                mm.then_inc(turned, 1)
                pe.wait_ge(dv, i * C + C + 1)
                for k in range(Q):
                    mm = pe.matmul(ps_o[:, k * P:(k + 1) * P], aggs[:, k * P:(k + 1) * P], t["gcn_wT"][:, :],
                                   start=True, stop=True)
                mm.then_inc(multiplied, 1)

        @block.vector
        def _(v):
            v.sem_inc(dv, C)
            with v.Fori(0, TURNS) as i:
                link = Link(v, dv, i * C + C)
                v.wait_ge(turned, i + 2)
                link(v.tensor_tensor(aggs[:, :], ps_h[:, :], acc[:, ds(i * (Q * P), Q * P)], ALU.add))
                v.wait_ge(multiplied, i + 1)
                for k in range(Q):
                    link(v.scalar_tensor_tensor(res[:, ds(i * Q + k, 1), :].rearrange("p a f -> p (a f)"),
                                                ps_o[:, k * P:(k + 1) * P], t["dinv_in"][:, ds(i * Q + k, 1)],
                                                t["gcn_b"][:, :], ALU.mult, ALU.add), k == Q - 1)
                for k in range(Q):
                    link(v.bn_stats(stats[:, ds(i * Q + k, 1), :], res[:, ds(i * Q + k, 1), :]), False)
                assert link.n == C
            v.wait_ge(dv, TURNS * C + C)
            link = Link(v, fin)
            norm_constants(link, v, stats, mean, var, tmp)
            v.sem_inc(roots, 1)
            v.wait_ge(roots, 2)
            link(v.reciprocal(var[:, :], var[:, :]))
            v.sem_inc(dv2, C2)
            with v.Fori(0, TURNS) as i:
                link2 = Link(v, dv2, i * C2 + C2)
                v.wait_ge(x_in, i * 16 + 16)
                normed_sum(v, link2, res, i, mean, var, t["gcn_gamma"], t["gcn_beta"], x_q[:, :, :])
                for k in range(Q):
                    link2(v.bn_stats(stats[:, ds(i * Q + k, 1), :], res[:, ds(i * Q + k, 1), :]), False)
                assert link2.n == C2
            v.wait_ge(dv2, TURNS * C2 + C2)
            norm_constants(link, v, stats, mean, var, tmp)
            link(v.tensor_scalar(tmp[:, 0:NT], t["deg_src"][:, :], 1.0, None, ALU.max))
            v.sem_inc(roots, 1)
            v.wait_ge(roots, 5)
            link(v.reciprocal(var[:, :], var[:, :]))
            link(v.reciprocal(tmp[:, 0:NT], tmp[:, 0:NT]))
            if S.NTP > NT:
                link(v.memset(t["dinv_src"][:, NT:S.NTP], 0.0))
            link(v.scalar_tensor_tensor(t["dinv_src"][:, 0:NT], t["deg_src"][:, :], 0.5, tmp[:, 0:NT], ALU.is_gt, ALU.mult))
            link(v.tensor_tensor(var[:, :], var[:, :], t["dinv_src"][:, :], ALU.mult))
            link(v.scalar_tensor_tensor(mean[:, :], mean[:, :], -1.0, var[:, :], ALU.mult, ALU.mult))

        @block.scalar
        def _(act):
            act.wait_ge(roots, 1)
            act.activation(var[:, :], var[:, :], ACT.Sqrt).then_inc(roots, 1)
            act.wait_ge(roots, 3)
            act.activation(var[:, :], var[:, :], ACT.Sqrt).then_inc(roots, 1)
            act.activation(tmp[:, 0:NT], tmp[:, 0:NT], ACT.Sqrt).then_inc(roots, 1)
        blocks.close()
        product_block(nc, S, t, "base", res, mean, var, t["bases"], 4, None, [t["HB"][b] for b in range(4)], None)


def product_block(nc, S, t, tag, res, mean, var, weight, M, bias, outs, h_table):
    TURNS = S.NTP // Q
    with ExitStack() as c:
        sb = lambda n, s, d=F32: c.enter_context(nc.sbuf_tensor(f"{tag}_{n}", s, d))
        sem = lambda n: c.enter_context(nc.semaphore(f"{tag}_{n}"))
        ps = lambda n, s: c.enter_context(nc.psum_tensor(f"{tag}_{n}", s, F32))
        h_q, hT, prod = sb("h_q", [P, Q, F]), sb("hT", [P, Q * P]), sb("prod", [P, M, Q, F])
        ps_h, ps_b = ps("ps_h", [P, 512]), ps("ps_b", [P, Q, 512])
        made, turned, taken, based, out, saved, free = (
            sem(n) for n in ("made", "turned", "taken", "based", "out", "saved", "free"))
        stores = M + bool(h_table is not None)
        extra = S.NR - S.NTP * P
        pads = c.enter_context(nc.sbuf_tensor(f"{tag}_pads", [P, extra // P, F], F32))
        padded = sem("padded")
        block = c.enter_context(nc.Block())

        @block.sync
        def _(sp):
            sp.wait_ge(padded, 1)
            for m in range(M):
                sp.dma_start(tiles_of(outs[m], S.NTP, extra // P), pads[:, :, :]).then_inc(padded, 16)
            sp.sem_inc(free, 1)
            with sp.Fori(0, TURNS) as i:
                sp.wait_ge(out, i * 2 + 4)
                for m in range(M):
                    sp.dma_start(tiles_of(outs[m], i * Q, Q), prod[:, m, :, :]).then_inc(saved, 16)
                if h_table is not None:
                    sp.wait_ge(made, i * Q + Q)
                    sp.dma_start(tiles_of(h_table, i * Q, Q), h_q[:, :, :]).then_inc(saved, 16)
                sp.wait_ge(saved, i * (16 * stores) + 16 * stores)
                sp.sem_inc(free, 1)
            sp.wait_ge(padded, 1 + 16 * M)

        @block.scalar
        def _(act):
            with act.Fori(0, TURNS) as i:
                act.wait_ge(turned, i + 1)
                if h_table is not None:
                    act.wait_ge(free, i + 1)
                for k in range(Q):
                    at = i * Q + k
                    act.activation(h_q[:, k, :], res[:, ds(at, 1), :].rearrange("p a f -> p (a f)"), ACT.Relu,
                                   bias=mean[:, ds(at, 1)], scale=var[:, ds(at, 1)]).then_inc(made, 1)
                if bias is None:
                    act.wait_ge(based, i + 1)
                    act.wait_ge(free, i + 1)
                    for k in range(Q // 2, Q):
                        cp = act.activation(prod[:, :, k, :], ps_b[:, k, 0:M * F].rearrange("p (m f) -> p m f", m=M),
                                            ACT.Copy)
                    cp.then_inc(out, 1)

        @block.tensor
        def _(pe):
            pe.sem_inc(turned, 1)
            with pe.Fori(0, TURNS) as i:
                pe.wait_ge(made, i * Q + Q)
                pe.wait_ge(taken, i + 1)
                for k in range(Q):
                    mm = pe.transpose(ps_h[:, k * P:(k + 1) * P], h_q[:, k, :], t["ident"][:, :])
                mm.then_inc(turned, 1)
                pe.wait_ge(taken, i + 2)
                pe.wait_ge(out, i * 2 + 2)
                for k in range(Q):
                    mm = pe.matmul(ps_b[:, k, 0:M * F], hT[:, k * P:(k + 1) * P], weight[:, :], start=True, stop=True)
                mm.then_inc(based, 1)

        @block.vector
        def _(v):
            v.memset(pads[:, :, :], 0.0).then_inc(padded, 1)
            v.sem_inc(out, 2)
            v.sem_inc(taken, 1)
            with v.Fori(0, TURNS) as i:
                v.wait_ge(turned, i + 2)
                v.tensor_copy(hT[:, :], ps_h[:, :]).then_inc(taken, 1)
                v.wait_ge(based, i + 1)
                v.wait_ge(free, i + 1)
                if bias is None:
                    for k in range(Q // 2):
                        cp = v.tensor_copy(prod[:, :, k, :], ps_b[:, k, 0:M * F].rearrange("p (m f) -> p m f", m=M))
                    cp.then_inc(out, 1)
                else:
                    v.tensor_tensor(prod[:, 0, 0:2, :], ps_b[:, 0:2, 0:F], bcast(bias[:, :], 1, 2), ALU.add).then_inc(out, 1)
                    v.tensor_tensor(prod[:, 0, 2:4, :], ps_b[:, 2:4, 0:F], bcast(bias[:, :], 1, 2), ALU.add).then_inc(out, 1)


def relation_norm_phase(nc, S, t):
    TURNS = S.NTP // Q
    with ExitStack() as c:
        sb = lambda n, s, d=F32: c.enter_context(nc.sbuf_tensor(f"rel_{n}", s, d))
        sem = lambda n: c.enter_context(nc.semaphore(f"rel_{n}"))
        res = sb("res", [P, S.NTP, F])
        mean, var, tmp = (sb(n, [P, S.NTP]) for n in ("mean", "var", "tmp"))
        blocks = c.enter_context(ExitStack())
        own = lambda n, s: blocks.enter_context(nc.sbuf_tensor(f"rel_{n}", s, F32))
        parts = own("parts", [P, 2, COPIES, 2 * F])
        x_q = own("x_q", [P, Q, F])
        total = own("total", [P, Q, F])
        stats = own("stats", [P, S.NTP, 6])
        part_in = [sem(f"part_in{k}") for k in range(2)]
        x_in, dv, fin, roots, stored = sem("x_in"), sem("dv"), sem("fin"), sem("roots"), sem("stored")
        C = 2 + 2 * Q
        block = blocks.enter_context(nc.Block())

        @block.sync
        def _(sp):
            with sp.Fori(0, TURNS) as i:
                for k in range(2):
                    sp.wait_ge(dv, i * C + 1 + k)
                    for q in range(COPIES):
                        sp.dma_start(parts[:, k, q, :].rearrange("p (n f) -> p n f", n=2),
                                     tiles_of(t["scat"][q], i * Q + 2 * k, 2)).then_inc(part_in[k], 16)
                    if k == 0:
                        sp.wait_ge(dv, i * C + C)
                        sp.dma_start(x_q[:, :, :], tiles_of(t["X2"], i * Q, Q)).then_inc(x_in, 16)
            sp.wait_ge(dv, TURNS * C + C)
            sp.dma_start(tiles_of(t["X3"], 0, S.NTP), res[:, :, :]).then_inc(stored, 16)
            sp.wait_ge(stored, 16)

        @block.vector
        def _(v):
            v.sem_inc(dv, C)
            with v.Fori(0, TURNS) as i:
                link = Link(v, dv, i * C + C)
                for k in range(2):
                    v.wait_ge(part_in[k], i * (16 * COPIES) + 16 * COPIES)
                    link(v.tensor_reduce(total[:, 2 * k:2 * k + 2, :].rearrange("p n f -> p (n f)"),
                                         parts[:, k, :, :].rearrange("p c f -> p f c"), AX_X, ALU.add), k == 1)
                v.wait_ge(x_in, i * 16 + 16)
                for k in range(Q):
                    link(v.scalar_tensor_tensor(res[:, ds(i * Q + k, 1), :].rearrange("p a f -> p (a f)"), total[:, k, :],
                                                t["dinv_src"][:, ds(i * Q + k, 1)], x_q[:, k, :], ALU.mult, ALU.add), k == Q - 1)
                for k in range(Q):
                    link(v.bn_stats(stats[:, ds(i * Q + k, 1), :], res[:, ds(i * Q + k, 1), :]), False)
                assert link.n == C
            v.wait_ge(dv, TURNS * C + C)
            link = Link(v, fin)
            norm_constants(link, v, stats, mean, var, tmp)
            v.sem_inc(roots, 1)
            v.wait_ge(roots, 2)
            link(v.reciprocal(var[:, :], var[:, :]))
            link(v.scalar_tensor_tensor(mean[:, :], mean[:, :], -1.0, var[:, :], ALU.mult, ALU.mult))

        @block.scalar
        def _(act):
            act.wait_ge(roots, 1)
            act.activation(var[:, :], var[:, :], ACT.Sqrt).then_inc(roots, 1)
        blocks.close()
        product_block(nc, S, t, "proj", res, mean, var, t["node_wT"], 1, t["proj_b"], [t["proj"]], t["H3"])


def relation_phase(nc, S, t):
    NGP, R2 = S.NGP, 2
    with ExitStack() as c:
        sb = lambda n, s, d=F32: c.enter_context(nc.sbuf_tensor(f"msg_{n}", s, d))
        sem = lambda n: c.enter_context(nc.semaphore(f"msg_{n}"))
        ps = lambda n, s: c.enter_context(nc.psum_tensor(f"msg_{n}", s, F32))
        src_f = sb("src_f", [P, NGP * J])
        dst_row, src_row, type_row = (sb(n, [m, R2, GE], BF16) for n, m in (("dst_row", 2), ("src_row", 2), ("type_row", 1)))
        ones2 = sb("ones2", [2, P], BF16)
        hb = sb("hb", [P, R2, 2, F])
        node = sb("node", [P, 1])
        node_w = sb("node_w", [P, S.NWIN])
        trash = sb("trash", [P, 1])
        before = sb("before", [P, P])
        dst_sp, type_hot = sb("dst_sp", [P, GE]), sb("type_hot", [T50, GE])
        lhs = sb("lhs", [P, 2, GE])
        same, same_b = sb("same", [P, J, P]), sb("same_b", [P, J, P])
        dup, off = sb("dup", [P, J]), sb("off", [P, J])
        msg = sb("msg", [P, GE])
        out = sb("out", [P, R2, J, F])
        idx = sb("idx", [P, R2, J], I32)
        ps_dst, ps_src, ps_type, ps_msg, ps_sum = (ps(n, [P, 512]) for n in ("ps_dst", "ps_src", "ps_type", "ps_msg", "ps_sum"))
        ps_c = ps("ps_c", [P, 2, 512])
        consts, rows_in, hb_in = sem("consts"), [sem(f"rows_in{k}") for k in range(R2)], [sem(f"hb_in{k}") for k in range(R2)]
        spread, dv, acted, coeff, mixed, summed, prep = (sem(n) for n in ("spread", "dv", "acted", "coeff", "mixed", "summed", "prep"))
        scattered = [sem(f"scattered{k}") for k in range(R2)]
        C, CA = 9, 3
        block = c.enter_context(nc.Block())

        def slot_free(eng, r, s, k):
            eng.wait_ge(scattered[k], r * (16 * J * (U // R2)) + 16 * J * (s // R2) + 16 * J)

        @block.sync
        def _(sp):
            def turn(i, r, w):
                for s in range(U):
                    n, g, k = r * U + s, i * U + s, s % R2
                    sp.wait_ge(mixed, n + 1)
                    for to, a, m in ((dst_row, 0, 2), (src_row, 2, 2), (type_row, 4, 1)):
                        sp.dma_start(to[:, k, :], t["rows5"][ds(g, 1), a:a + m, :].rearrange("a m e -> (a m) e")).then_inc(rows_in[k], 16)
                    at = window_start(sp, S, t, g, w)
                    for b in range(4):
                        sp.dma_start(hb[(b % 2) * W:(b % 2 + 1) * W, k, b // 2, :], t["HB"][b][ds(at, W), :]).then_inc(hb_in[k], 16)
            forms(sp, S, t, turn)

        @block.gpsimd
        def _(pool):
            pool.iota(node[:, :], pattern=[[0, 1]], base=0, channel_multiplier=1, allow_small_or_imprecise_dtypes=True).then_inc(consts, 1)
            pool.memset(before[:, :], 1.0).then_inc(consts, 1)
            pool.wait_ge(consts, 2)
            pool.affine_select(out=before[:, :], in_=before[:, :], compare_op=ALU.is_gt, fill=0.0, base=0,
                               pattern=[[-1, P]], channel_multiplier=1).then_inc(consts, 1)
            for k in range(R2):
                for j in range(J):
                    pool.dma_start(out[:, k, j, :], t["HB"][0][0:P, :]).then_inc(scattered[k], 16)

            def turn(i, r, w):
                for s in range(U):
                    n, k = r * U + s, s % R2
                    slot_free(pool, r, s, k)
                    pool.wait_ge(acted, n * CA + 2 * CA)
                    pool.wait_ge(dv, n * C + 2 * C)
                    pool.nop(nofuse=True)
                    for j in range(J):
                        pool.indirect_dma_start(t["scat"][(k * J + j) % COPIES], bass.IndirectOffsetOnAxis(ap=idx[:, k, j:j + 1], axis=0),
                                                out[:, k, j, :], None, compute_op=ALU.add).then_inc(scattered[k], 16)

            def after(turns):
                for k in range(R2):
                    pool.wait_ge(scattered[k], (turns * (U // R2) + 1) * 16 * J)
            forms(pool, S, t, turn, after)

        @block.scalar
        def _(act):
            act.sem_inc(acted, CA)

            def turn(i, r, w):
                for s in range(U):
                    n, k = r * U + s, s % R2
                    link = Link(act, acted, n * CA + CA)
                    act.wait_ge(spread, n + 1)
                    act.wait_ge(dv, n * C + C)
                    link(act.activation(dst_sp[:, :], ps_dst[:, :], ACT.Copy), False)
                    act.wait_ge(mixed, n + 3)
                    act.wait_ge(summed, n + 1)
                    link(act.activation(msg[:, :], ps_msg[:, :], ACT.Copy), False)
                    act.wait_ge(summed, n + 2)
                    slot_free(act, r, s, k)
                    link(act.activation(out[:, k, :, :].rearrange("p j f -> p (j f)"), ps_sum[:, :], ACT.Copy), False)
            forms(act, S, t, turn)


        @block.vector
        def _(v):
            v.wait_ge(consts, 3)
            v.tensor_copy(src_f[:, :], t["src_i"][:, :]).then_inc(prep, 1)
            v.tensor_scalar(trash[:, :], node[:, :], float(S.NP), None, ALU.add).then_inc(prep, 1)
            v.tensor_scalar(ones2[:, :], t["iota"][0:2, :], 0.0, 1.0, ALU.mult, ALU.add).then_inc(prep, 1)
            v.tensor_scalar(same[:, 0, 0:1], node[:, :], float(W) - 0.5, -float(W), ALU.is_gt, ALU.mult).then_inc(prep, 1)
            v.wait_ge(prep, 4)
            v.tensor_tensor(node[:, :], node[:, :], same[:, 0, 0:1], ALU.add).then_inc(prep, 1)
            v.wait_ge(prep, 5)
            v.tensor_scalar(node_w[:, :], t["win0"][:, :], node[:, 0:1], None, ALU.add).then_inc(prep, 1)
            v.wait_ge(prep, 6)
            v.sem_inc(dv, C)

            def turn(i, r, w):
                for s in range(U):
                    n, g, k = r * U + s, i * U + s, s % R2
                    link = Link(v, dv, n * C + C)
                    v.wait_ge(spread, n + 1)
                    v.wait_ge(coeff, n + 1)
                    link(v.tensor_scalar(type_hot[:, :], ps_type[0:T50, :], t["pcol"][0:T50, 0:1], None, ALU.is_equal), False)
                    v.wait_ge(summed, n + 1)
                    link(v.tensor_tensor(same[:, :, :], ps_src[:, :].rearrange("p (e j) -> p j e", j=J),
                                         bcast(src_f[:, ds(g * J, J)], 2, P), ALU.is_equal))
                    link(v.tensor_tensor(same_b[:, :, :], same[:, :, :], bcast(before[:, :], 1, J), ALU.mult))
                    link(v.tensor_reduce(dup[:, :], same_b[:, :, :], AX_X, ALU.add))
                    link(v.tensor_scalar(off[:, :], src_f[:, ds(g * J, J)], trash[:, 0:1], -1.0, ALU.subtract, ALU.mult))
                    link(v.scalar_tensor_tensor(off[:, :], dup[:, :], 0.5, off[:, :], ALU.is_gt, ALU.mult))
                    slot_free(v, r, s, k)
                    link(v.tensor_tensor(idx[:, k, :], off[:, :], src_f[:, ds(g * J, J)], ALU.add), False)
                    v.wait_ge(acted, n * CA + CA + 1)
                    v.wait_ge(coeff, n + 2)
                    v.wait_ge(mixed, n + 2)
                    col = node[:, 0:1] if w is None else node_w[:, ds(w, 1)]
                    for q in range(2):
                        link(v.scalar_tensor_tensor(lhs[:, q, :], dst_sp[:, :], col, ps_c[:, q, :], ALU.is_equal, ALU.mult), False)
                    assert link.n == C
            forms(v, S, t, turn)

        @block.tensor
        def _(pe):
            pe.wait_ge(prep, 6)
            pe.sem_inc(coeff, 1)
            pe.sem_inc(summed, 1)
            pe.sem_inc(mixed, 2)

            def turn(i, r, w):
                for s in range(U):
                    n, k = r * U + s, s % R2
                    pe.wait_ge(rows_in[k], r * (48 * (U // R2)) + 48 * (s // R2) + 48)
                    pe.wait_ge(dv, n * C + C)
                    pe.wait_ge(acted, n * CA + CA)
                    pe.matmul(ps_type[0:T50, :], ones2[0:1, 0:T50], type_row[:, k, :], start=True, stop=True)
                    pe.matmul(ps_src[:, :], ones2[:, :], src_row[:, k, :], start=True, stop=True)
                    pe.matmul(ps_dst[:, :], ones2[:, :], dst_row[:, k, :], start=True, stop=True).then_inc(spread, 1)
                    pe.wait_ge(dv, n * C + C + 1)
                    for q in range(2):
                        mm = pe.matmul(ps_c[:, q, :], t["relation"][0:T50, q * P:(q + 1) * P], type_hot[:, :], start=True, stop=True)
                    mm.then_inc(coeff, 1)
                    pe.wait_ge(dv, n * C + 2 * C)
                    pe.wait_ge(hb_in[k], r * (64 * (U // R2)) + 64 * (s // R2) + 64)
                    for j in range(J):
                        for q in range(2):
                            mm = pe.matmul(ps_msg[:, j * F:(j + 1) * F], lhs[:, q, :].rearrange("p (e j) -> p j e", j=J)[:, j, :],
                                           hb[:, k, q, :], start=(q == 0), stop=(q == 1))
                    mm.then_inc(mixed, 1)
                    pe.wait_ge(acted, n * CA + CA + 2)
                    for j in range(J):
                        mm = pe.matmul(ps_sum[:, j * F:(j + 1) * F], same[:, j, :], msg[:, j * F:(j + 1) * F], start=True, stop=True)
                    mm.then_inc(summed, 1)
            forms(pe, S, t, turn)


def logit_phase(nc, S, attr, t):
    NGP = S.NGP
    full, rest = S.E // GE, S.E % GE
    CA = 6
    with ExitStack() as c:
        sb = lambda n, s, d=F32: c.enter_context(nc.sbuf_tensor(f"log_{n}", s, d))
        sem = lambda n: c.enter_context(nc.semaphore(f"log_{n}"))
        ps = lambda n, s: c.enter_context(nc.psum_tensor(f"log_{n}", s, F32))
        most = t["big"][0:2, :, :]
        slot = sb("slot", [P, U, J], I32)
        rows = sb("rows", [P, U, J, F])
        at_in, atT = sb("at_in", [P, 2, J * ED]), sb("atT", [P, J * ED])
        xs = sb("xs", [P, 2, J * F])
        weighed, far = sb("weighed", [P, J * F]), sb("far", [P, J, W])
        val = sb("val", [P, 2, 2, J, 2, W])
        top = sb("top", [P, 2, 2])
        ps_at, ps_top = ps("ps_at", [P, 512]), ps("ps_top", [P, 512])
        ps_x = [ps(f"ps_x{k}", [P, 512]) for k in range(2)]
        ps_v = [ps(f"ps_v{k}", [P, 2, 512]) for k in range(2)]
        gathered = [sem(f"gathered{k}") for k in range(U)]
        attr_in, stored = [sem(f"attr_in{k}") for k in range(2)], [sem(f"stored{k}") for k in range(2)]
        pad_in, idx_ready, at_turned, at_copied, projected, x_copied = (
            sem(n) for n in ("pad_in", "idx_ready", "at_turned", "at_copied", "projected", "x_copied"))
        valued, val_turned, topped, top_turned, merged, saved = (
            sem(n) for n in ("valued", "val_turned", "topped", "top_turned", "merged", "saved"))
        block = c.enter_context(nc.Block())

        @block.sync
        def _(sp):
            whole = attr[0:full * GE, :].rearrange("(g p j) d -> g p (j d)", p=P, j=J)

            def turn(i, r, w):
                for s in range(U):
                    n, k = r * U + s, s % 2
                    sp.wait_ge(at_turned, n + 1)
                    if not isinstance(i, int) or i * U + s < full:
                        sp.dma_start(at_in[:, k, :], whole[ds(i * U + s, 1), :, :].rearrange("a p d -> (a p) d")
                                     ).then_inc(attr_in[k], 16)
                    elif i * U + s == full and rest:
                        m = rest // J
                        tail = attr[full * GE:S.E, :].rearrange("(p j) d -> p (j d)", j=J)
                        other = attr[0:(P - m) * J, :].rearrange("(p j) d -> p (j d)", j=J)
                        sp.dma_start(at_in[m:P, k, :], other).then_inc(pad_in, 16)
                        sp.wait_ge(pad_in, (w * 16 + 16) if w is not None else 16)
                        sp.dma_start(at_in[0:m, k, :], tail).then_inc(attr_in[k], 16)
                    else:
                        sp.dma_start(at_in[:, k, :], whole[0]).then_inc(attr_in[k], 16)

            def after(turns):
                sp.wait_ge(merged, turns * U + 2)
                sp.dma_start(t["MX"].rearrange("(a b) n -> a b n", a=2), most).then_inc(saved, 16)
                sp.wait_ge(saved, 16)
            forms(sp, S, t, turn, after, last_apart=True)

        @block.gpsimd
        def _(pool):
            def turn(i, r, w):
                for s in range(U):
                    pool.wait_ge(idx_ready, r * U + s + 1)
                    pool.nop(nofuse=True)
                    for j in range(J):
                        pool.indirect_dma_start(rows[:, s, j, :], None, t["proj"],
                                                bass.IndirectOffsetOnAxis(ap=slot[:, s, j:j + 1], axis=0)
                                                ).then_inc(gathered[s], 16)
            forms(pool, S, t, turn)

        @block.scalar
        def _(act):
            for k in range(2):
                act.dma_start(xs[:, k, :], t["proj"][0:P * J, :].rearrange("(p j) f -> p (j f)", j=J)).then_inc(stored[k], 16)
            act.sem_inc(at_copied, 1)
            act.sem_inc(x_copied, 2)
            edges = t["edges"].rearrange("(g p j) f -> g p (j f)", p=P, j=J)

            def turn(i, r, w):
                for s in range(U):
                    act.wait_ge(projected, r * U + s + 1)
                    act.activation(slot[:, s, :], t["src_i"][:, ds((i * U + s) * J, J)], ACT.Copy).then_inc(idx_ready, 1)
                for s in range(U):
                    n, g, k = r * U + s, i * U + s, s % 2
                    act.wait_ge(at_turned, n + 3)
                    act.wait_ge(projected, n + U)
                    act.activation(atT[:, :], ps_at[:, 0:J * ED], ACT.Copy).then_inc(at_copied, 1)
                    act.wait_ge(projected, n + U + 1)
                    act.wait_ge(stored[k], r * (16 * (U // 2)) + 16 * (s // 2) + 16)
                    act.wait_ge(valued, n * CA + 1)
                    act.activation(xs[:, k, :], ps_x[k][:, :], ACT.Copy).then_inc(x_copied, 1)
                    act.wait_ge(x_copied, n + 3)
                    act.dma_start(edges[ds(g, 1), :, :].rearrange("a p d -> (a p) d"), xs[:, k, :]).then_inc(stored[k], 16)

            def after(turns):
                for k in range(2):
                    act.wait_ge(stored[k], turns * (U // 2) * 16 + 16)
            forms(act, S, t, turn, after)

        @block.tensor
        def _(pe):
            pe.sem_inc(at_turned, 2)
            pe.sem_inc(projected, U)
            pe.sem_inc(val_turned, 2)
            pe.sem_inc(top_turned, 2)

            def turn(i, r, w):
                def project(s):
                    n, k = r * U + s, s % 2
                    pe.wait_ge(attr_in[k], r * (16 * (U // 2)) + 16 * (s // 2) + 16)
                    pe.wait_ge(at_copied, n + 1)
                    for q in range(2):
                        mm = pe.transpose(ps_at[:, q * P:(q + 1) * P], at_in[:, k, q * P:(q + 1) * P], t["ident"][:, :])
                    mm.then_inc(at_turned, 1)
                    pe.wait_ge(x_copied, n + 1)
                    pe.wait_ge(gathered[s], r * (16 * J) + 16 * J)
                    pe.matmul(ps_x[k][:, :], t["ident"][:, :], rows[:, s, :, :].rearrange("p j f -> p (j f)"),
                              start=True, stop=False, skip_group_check=True)
                    pe.wait_ge(at_copied, n + 2)
                    for q in range(2):
                        mm = pe.matmul(ps_x[k][:, q * 2 * F:(q + 1) * 2 * F], atT[:, q * P:(q + 1) * P],
                                       t["edge_wT"][:, :], start=False, stop=(q == 1), skip_group_check=True)
                    mm.then_inc(projected, 1)

                def turn_values(s):
                    n, k = r * U + s, s % 2
                    pe.wait_ge(valued, n * CA + 3 * CA)
                    pe.wait_ge(topped, n + 1)
                    for hp in range(2):
                        for j in range(J):
                            mm = pe.transpose(ps_v[k][:, hp, j * P:(j + 1) * P],
                                              val[:, k, hp, j, :, :].rearrange("p a n -> p (a n)"), t["ident"][:, :])
                    mm.then_inc(val_turned, 1)

                def turn_top(s):
                    n, k = r * U + s, s % 2
                    pe.wait_ge(topped, n + 3)
                    pe.wait_ge(merged, n + 2)
                    pe.transpose(ps_top[0:2, k * P:(k + 1) * P], top[:, k, :], t["ident"][:, :]).then_inc(top_turned, 1)

                for s in range(U + 2):
                    if s < U:
                        project(s)
                    if 1 <= s <= U:
                        turn_values(s - 1)
                    if s >= 2:
                        turn_top(s - 2)
            forms(pe, S, t, turn)

        @block.vector
        def _(v):
            v.memset(most, -BIG).then_inc(merged, 1)
            v.sem_inc(merged, 1)
            v.sem_inc(valued, 2 * CA)
            v.sem_inc(topped, 2)

            def turn(i, r, w):
                def values(s):
                    n, g, k = r * U + s, i * U + s, s % 2
                    link = Link(v, valued, n * CA + 2 * CA)
                    v.wait_ge(x_copied, n + 3)
                    link(v.tensor_tensor(weighed[:, :].rearrange("p (j f) -> p j f", j=J), xs[:, k, :].rearrange("p (j f) -> p j f", j=J),
                                         bcast(t["attn"][:, :], 1, J), ALU.mult))
                    e = t["logits"][:, ds(g * (J * HEADS), J * HEADS)]
                    link(v.tensor_reduce(e, weighed[:, :].rearrange("p (a d) -> p a d", d=HD), AX_X, ALU.add), False)
                    link(one_hot(v, t, far[:, :, :], g, w, ALU.not_equal))
                    link(v.tensor_scalar(far[:, :, :], far[:, :, :], -BIG, None, ALU.mult))
                    v.wait_ge(val_turned, n + 1)
                    for hp in range(2):
                        link(v.tensor_tensor(val[:, k, hp, :, :, :], bcast(far[:, :, :], 2, 2),
                                             bcast(e.rearrange("p (j h) -> p j h", j=J)[:, :, 2 * hp:2 * hp + 2], 3, W),
                                             ALU.add), False)
                    assert link.n == CA

                def tops(s):
                    n, k = r * U + s, s % 2
                    v.wait_ge(val_turned, n + 3)
                    v.wait_ge(top_turned, n + 1)
                    v.tensor_reduce(top[:, k, :], ps_v[k][:, :, :], AX_X, ALU.max).then_inc(topped, 1)

                def merge(s):
                    n, g, k = r * U + s, i * U + s, s % 2
                    at = window_start(v, S, t, g, w)
                    v.wait_ge(top_turned, n + 3)
                    v.wait_ge(merged, n + 2)
                    v.tensor_tensor(most[:, :, ds(at, W)], most[:, :, ds(at, W)],
                                    ps_top[0:2, k * P:(k + 1) * P].rearrange("p (a n) -> p a n", a=2), ALU.max).then_inc(merged, 1)

                for s in range(U + 2):
                    if s < U:
                        values(s)
                    if 1 <= s <= U:
                        tops(s - 1)
                    if s >= 2:
                        merge(s - 2)
            forms(v, S, t, turn)


def attention_phase(nc, S, t):
    with ExitStack() as c:
        sb = lambda n, s, d=F32: c.enter_context(nc.sbuf_tensor(f"att_{n}", s, d))
        sem = lambda n: c.enter_context(nc.semaphore(f"att_{n}"))
        ps = lambda n, s: c.enter_context(nc.psum_tensor(f"att_{n}", s, F32))
        xe = sb("xe", [P, U, J * F])
        ex, diff = sb("ex", [P, U * J * HEADS]), sb("diff", [P, U * J * HEADS])
        ex_f = sb("ex_f", [P, U * J * HEADS, HD])
        onehot, hotT = sb("onehot", [P, U, J, W]), sb("hotT", [W, U, J * P])
        most, mostT = sb("most", [HEADS, U, W]), sb("mostT", [W, U, HEADS])
        ps_hot = [ps(f"ps_hot{k}", [P, 512]) for k in range(2)]
        ps_most, ps_max = ps("ps_most", [P, 512]), ps("ps_max", [P, 512])
        ps_sum = [ps(f"ps_sum{k}", [P, 512]) for k in range(U)]
        x_in, m_in = [sem(f"x_in{k}") for k in range(U)], [sem(f"m_in{k}") for k in range(U)]
        hot_made, hot_turned, hot_copied, most_turned, most_copied, max_made = (
            sem(n) for n in ("hot_made", "hot_turned", "hot_copied", "most_turned", "most_copied", "max_made"))
        differed, exped, weighed, summed, added = (sem(n) for n in ("differed", "exped", "weighed", "summed", "added"))
        block = c.enter_context(nc.Block())

        @block.sync
        def _(sp):
            edges = t["edges"].rearrange("(g p j) f -> g p (j f)", p=P, j=J)

            def turn(i, r, w):
                for s in range(U):
                    n, g = r * U + s, i * U + s
                    sp.wait_ge(summed, n + 1)
                    sp.dma_start(xe[:, s, :], edges[ds(g, 1), :, :].rearrange("a p d -> (a p) d")).then_inc(x_in[s], 16)
                    at = window_start(sp, S, t, g, w)
                    sp.dma_start(most[:, s, :], t["MX"][:, ds(at, W)]).then_inc(m_in[s], 16)
            forms(sp, S, t, turn)

        @block.vector
        def _(v):
            v.memset(t["big"][:, :, :], 0.0).then_inc(added, 1)
            v.sem_inc(added, U - 1)
            v.sem_inc(most_copied, 1)
            v.sem_inc(differed, 2)

            def turn(i, r, w):
                for s in range(U):
                    v.wait_ge(summed, r * U + s + 1)
                    one_hot(v, t, onehot[:, s, :, :], i * U + s, w).then_inc(hot_made, 1)
                v.wait_ge(most_turned, r + 1)
                v.wait_ge(max_made, r + 1)
                v.tensor_copy(mostT[:, :, :].rearrange("p s h -> p (s h)"), ps_most[0:W, 0:U * HEADS]).then_inc(most_copied, 1)
                v.wait_ge(max_made, r + 2)
                v.wait_ge(exped, 2 * r + 2)
                v.tensor_tensor(diff[:, :], t["logits"][:, ds(i * (U * J * HEADS), U * J * HEADS)],
                                ps_max[:, 0:U * J * HEADS], ALU.subtract).then_inc(differed, 1)
                v.wait_ge(differed, 2 * r + 3)
                v.tensor_scalar(diff[:, :], diff[:, :], 0.0, None, ALU.min).then_inc(differed, 1)
                v.wait_ge(exped, 2 * r + 3)
                for s in range(U):
                    v.wait_ge(x_in[s], r * 16 + 16)
                    x = xe[:, s, :].rearrange("p (a d) -> p a d", d=HD)
                    v.tensor_tensor(x, x, bcast(ex[:, s * J * HEADS:(s + 1) * J * HEADS], 2, HD), ALU.mult).then_inc(weighed, 1)
                for s in range(U):
                    n, g = r * U + s, i * U + s
                    at = window_start(v, S, t, g, w)
                    v.wait_ge(summed, n + U + 1)
                    v.wait_ge(added, n + U)
                    both = t["big"][:, :, ds(at, W)]
                    v.tensor_tensor(both, both, ps_sum[s][:, 0:2 * W].rearrange("p (a n) -> p a n", a=2), ALU.add).then_inc(added, 1)
            forms(v, S, t, turn)

        @block.scalar
        def _(act):
            act.sem_inc(hot_copied, 2)
            act.sem_inc(exped, 2)

            def turn(i, r, w):
                for s in range(U):
                    act.wait_ge(hot_turned, r * U + s + 1)
                    act.wait_ge(max_made, r + 1)
                    act.activation(hotT[:, s, :], ps_hot[s % 2][0:W, :], ACT.Copy).then_inc(hot_copied, 1)
                act.wait_ge(differed, 2 * r + 4)
                act.wait_ge(weighed, r * U + U)
                act.wait_ge(summed, r * U + U)
                act.activation(ex[:, :], diff[:, :], ACT.Exp).then_inc(exped, 1)
                act.activation(ex_f[:, :, :], bcast(diff[:, :], 2, HD), ACT.Exp).then_inc(exped, 1)
            forms(act, S, t, turn)

        @block.tensor
        def _(pe):
            pe.sem_inc(summed, U)
            pe.sem_inc(max_made, 1)
            pe.sem_inc(weighed, U)

            def turn(i, r, w):
                for s in range(U):
                    n = r * U + s
                    pe.wait_ge(hot_made, n + 1)
                    pe.wait_ge(hot_copied, n + 1)
                    pe.nop(nofuse=True)
                    for j in range(J):
                        mm = pe.transpose(ps_hot[s % 2][0:W, j * P:(j + 1) * P], onehot[:, s, j, :], t["ident"][:, :])
                    mm.then_inc(hot_turned, 1)
                pe.wait_ge(most_copied, r + 1)
                for s in range(U):
                    pe.wait_ge(m_in[s], r * 16 + 16)
                    pe.nop(nofuse=True)
                    mm = pe.transpose(ps_most[0:W, s * HEADS:(s + 1) * HEADS], most[:, s, :], t["ident"][0:HEADS, 0:HEADS])
                mm.then_inc(most_turned, 1)
                pe.wait_ge(most_copied, r + 2)
                pe.wait_ge(differed, 2 * r + 1)
                for s in range(U):
                    pe.wait_ge(hot_copied, r * U + s + 3)
                    for j in range(J):
                        at = (s * J + j) * HEADS
                        mm = pe.matmul(ps_max[:, at:at + HEADS], hotT[:, s, j * P:(j + 1) * P], mostT[:, s, :], start=True, stop=True)
                mm.then_inc(max_made, 1)
                for s in range(U):
                    n = r * U + s
                    pe.wait_ge(weighed, n + U + 1)
                    pe.wait_ge(exped, 2 * r + 4)
                    pe.wait_ge(added, n + 1)
                    for j in range(J):
                        pe.matmul(ps_sum[s][:, 0:W], xe[:, s, j * F:(j + 1) * F], onehot[:, s, j, :],
                                  start=(j == 0), stop=(j == J - 1))
                    for j in range(J):
                        at = (s * J + j) * HEADS
                        mm = pe.matmul(ps_sum[s][:, W:2 * W], ex_f[:, at:at + HEADS, :].rearrange("p a d -> p (a d)"),
                                       onehot[:, s, j, :], start=(j == 0), stop=(j == J - 1))
                    mm.then_inc(summed, 1)
            forms(pe, S, t, turn)


def output_phase(nc, S, t, y):
    NT, TURNS = S.NT, S.NTP // Q
    full, rest = S.N // P, S.N % P
    acc, den = t["big"][:, 0, :], t["big"][:, 1, :]
    with ExitStack() as c:
        sb = lambda n, s, d=F32: c.enter_context(nc.sbuf_tensor(f"out_{n}", s, d))
        sem = lambda n: c.enter_context(nc.semaphore(f"out_{n}"))
        ps = lambda n, s: c.enter_context(nc.psum_tensor(f"out_{n}", s, F32))
        res = sb("res", [P, S.NTP, F])
        h_q, aggs, x_q = sb("h_q", [P, Q, F]), sb("aggs", [P, Q * P]), sb("x_q", [P, Q, F])
        stats = sb("stats", [P, S.NTP, 6])
        mean, var, tmp = (sb(n, [P, S.NTP]) for n in ("mean", "var", "tmp"))
        ps_h, ps_o = ps("ps_h", [P, 512]), ps("ps_o", [P, 512])
        h_in, x_in, turned, multiplied, dv = sem("h_in"), sem("x_in"), sem("turned"), sem("multiplied"), sem("dv")
        dv2, fin, roots, stored = sem("dv2"), sem("fin"), sem("roots"), sem("stored")
        C, C2 = 6 + Q, 7
        block = c.enter_context(nc.Block())

        @block.sync
        def _(sp):
            with sp.Fori(0, TURNS) as i:
                sp.wait_ge(turned, i + 1)
                sp.dma_start(h_q[:, :, :], tiles_of(t["H3"], i * Q, Q)).then_inc(h_in, 16)
            with sp.Fori(0, TURNS) as i:
                sp.wait_ge(dv2, i * C2 + C2)
                sp.dma_start(x_q[:, :, :], tiles_of(t["X3"], i * Q, Q)).then_inc(x_in, 16)
            sp.wait_ge(dv2, TURNS * C2 + C2)
            sp.dma_start(y[0:full * P, :].rearrange("(n p) f -> p n f", p=P), res[:, 0:full, :]).then_inc(stored, 16)
            if rest:
                sp.dma_start(y[full * P:S.N, :], res[0:rest, full, :]).then_inc(stored, 16)
            sp.wait_ge(stored, 16 * (1 + bool(rest)))

        @block.tensor
        def _(pe):
            pe.sem_inc(turned, 1)
            with pe.Fori(0, TURNS) as i:
                pe.wait_ge(h_in, i * 16 + 16)
                pe.wait_ge(dv, i * C + C)
                for k in range(Q):
                    mm = pe.transpose(ps_h[:, k * P:(k + 1) * P], h_q[:, k, :], t["ident"][:, :])
                mm.then_inc(turned, 1)
                pe.wait_ge(dv, i * C + C + 4)
                for k in range(Q):
                    mm = pe.matmul(ps_o[:, k * P:(k + 1) * P], aggs[:, k * P:(k + 1) * P], t["out_wT"][:, :], start=True, stop=True)
                mm.then_inc(multiplied, 1)

        @block.vector
        def _(v):
            v.sem_inc(dv, C)
            with v.Fori(0, TURNS) as i:
                link = Link(v, dv, i * C + C)
                cols = ds(i * (Q * P), Q * P)
                link(v.tensor_scalar(aggs[:, :], den[:, cols], 1.0e-30, None, ALU.max))
                link(v.reciprocal(aggs[:, :], aggs[:, :]))
                link(v.tensor_tensor(aggs[:, :], aggs[:, :], acc[:, cols], ALU.mult))
                v.wait_ge(turned, i + 2)
                link(v.tensor_tensor(aggs[:, :], aggs[:, :], ps_h[:, :], ALU.add))
                v.wait_ge(multiplied, i + 1)
                four = res[:, ds(i * Q, Q), :]
                link(v.tensor_tensor(four, ps_o[:, :].rearrange("p (n f) -> p n f", n=Q), bcast(t["out_b"][:, :], 1, Q), ALU.add))
                link(v.tensor_scalar(four, four, 0.0, None, ALU.max))
                for k in range(Q):
                    link(v.bn_stats(stats[:, ds(i * Q + k, 1), :], res[:, ds(i * Q + k, 1), :]), False)
                assert link.n == C
            v.wait_ge(dv, TURNS * C + C)
            link = Link(v, fin)
            norm_constants(link, v, stats, mean, var, tmp)
            v.sem_inc(roots, 1)
            v.wait_ge(roots, 2)
            link(v.reciprocal(var[:, :], var[:, :]))
            v.sem_inc(dv2, C2)
            with v.Fori(0, TURNS) as i:
                link2 = Link(v, dv2, i * C2 + C2)
                v.wait_ge(x_in, i * 16 + 16)
                normed_sum(v, link2, res, i, mean, var, t["out_gamma"], t["out_beta"], x_q[:, :, :])
                assert link2.n == C2
            v.wait_ge(dv2, TURNS * C2 + C2)

        @block.scalar
        def _(act):
            act.wait_ge(roots, 1)
            act.activation(var[:, :], var[:, :], ACT.Sqrt).then_inc(roots, 1)


NAMES = ["x", "src", "dst", "edge_attr_64", "edge_type_50", "edge_type_9", "L0_gnn_W_msg", "L0_gnn_b_msg",
         "L0_gnn_edge_embed", "L0_gnn_W_ih", "L0_gnn_W_hh", "L0_gnn_b_ih", "L0_gnn_b_hh", "L1_gnn_W", "L1_gnn_b",
         "L1_gnn_gamma", "L1_gnn_beta", "L2_gnn_bases", "L2_gnn_comps", "L2_gnn_alpha", "L3_gnn_W_proj_w",
         "L3_gnn_W_proj_b", "L3_gnn_attn_vec", "L3_gnn_W_out_w", "L3_gnn_W_out_b", "L3_gnn_ln_gamma",
         "L3_gnn_ln_beta"]


def build_program(nc, a, out, kind="Internal"):
    S = Shapes(a["x"].shape[0], a["src"].shape[0])
    dram = lambda n, s, d=F32: nc.dram_tensor(n, s, d, kind=kind).ap()
    t = {
        "T9": dram("T9", (P, S.NGP * J)),
        "rows5": dram("rows5", (S.NGP, 5, GE), BF16),
        "scat": [dram(f"scat{k}", (S.NR, F)) for k in range(COPIES)],
        "HB": dram("HB", (4, S.NR, F)),
        "MX": dram("MX", (HEADS, S.NR)),
        "proj": dram("proj", (S.NR, F)),
        "edges": dram("edges", (S.NGP * GE, F)),
    }
    for k in range(4):
        t[f"H{k}"] = dram(f"H{k}", (S.NR, F))
        t[f"X{k}"] = dram(f"X{k}", (S.NR, F))
    with ExitStack() as c:
        sb = lambda n, s, d=F32: c.enter_context(nc.sbuf_tensor(n, s, d))
        t["ident"] = sb("ident", [P, P])
        t["iota"] = sb("iota", [P, P])
        t["pcol"] = sb("pcol", [P, 1])
        t["win0"] = sb("win0", [P, S.NWIN])
        t["win_far"] = sb("win_far", [P, S.NWIN])
        t["src_i"] = sb("src_i", [P, S.NGP * J], I32)
        t["dst_rel"] = sb("dst_rel", [P, S.NGP * J])
        t["base"] = sb("base_row", [1, S.NB * P], I32)
        t["wide"] = sb("wide", [1, 1], I32)
        t["deg_src"] = sb("deg_src", [P, S.NT])
        t["dinv_in"] = sb("dinv_in", [P, S.NTP])
        t["dinv_src"] = sb("dinv_src", [P, S.NTP])
        for n, w in WEIGHTS.items():
            t[n] = sb(n, [P, w])
        setup_phase(nc, S, a["src"], a["dst"], a["edge_type_9"], a["edge_type_50"], t)
        first_norm_phase(nc, S, a["x"], t)
        with nc.sbuf_tensor("sums_a", [P, 2, S.NR], F32) as t["big"]:
            sum_phase(nc, S, t, "L0", t["H0"], True)
            weights_phase(nc, S, a, t)
            gru_phase(nc, S, t)
            sum_phase(nc, S, t, "L1", t["H1"], False)
            gcn_phase(nc, S, t)
        relation_phase(nc, S, t)
        relation_norm_phase(nc, S, t)
        with nc.sbuf_tensor("sums_b", [P, 2, S.NR], F32) as t["big"]:
            with nc.sbuf_tensor("logits", [P, S.NGP * J * HEADS], F32) as t["logits"]:
                logit_phase(nc, S, a["edge_attr_64"], t)
                attention_phase(nc, S, t)
            output_phase(nc, S, t, out)
    return S, t


def kernel(**inputs):
    import numpy as _np
    import concourse.bacc as _bacc
    from concourse import mybir as _mybir
    from concourse.bass_utils import run_bass_kernel_spmd as _run

    nc = _bacc.Bacc("TRN2", target_bir_lowering=False, num_devices=1)
    arrays, args = {}, {}
    for name in NAMES:
        a = _np.ascontiguousarray(inputs[name])
        arrays[f"in_{name}_dram"] = a
        args[name] = nc.dram_tensor(f"in_{name}_dram", a.shape, _mybir.dt.from_np(a.dtype), kind="ExternalInput").ap()
    out = nc.dram_tensor("out_0_dram", args["x"].shape, F32, kind="ExternalOutput").ap()
    build_program(nc, args, out)
    r = _run(nc, [arrays], core_ids=[0])
    return r.results[0]["out_0_dram"]
```

```python
from contextlib import ExitStack

import concourse.bass as bass
from concourse import mybir

P = 128
F = 128
J = 4
GE = P * J
W = 64
U = 4
Q = 4
COPIES = 8
T9 = 9
T50 = 50
HEADS = 4
HD = F // HEADS
ED = 64
BASES = 4
IDS = 5
EPS = 1e-5
FAR = -1.0e6
BIG = 1.0e30

ALU = mybir.AluOpType
ACT = mybir.ActivationFunctionType
AX_X = mybir.AxisListType.X
F32 = mybir.dt.float32
I32 = mybir.dt.int32
BF16 = mybir.dt.bfloat16
ds = bass.ds


class Link:

    def __init__(self, eng, sem, base=0):
        self.eng, self.sem, self.base, self.n = eng, sem, base, 0

    def __call__(self, ins, wait=True):
        self.n += 1
        ins.then_inc(self.sem, 1)
        if wait:
            self.eng.wait_ge(self.sem, self.base + self.n)


class Shapes:
    def __init__(self, n_nodes, n_edges):
        self.N, self.E = n_nodes, n_edges
        self.NT = -(-n_nodes // P)
        self.NP = self.NT * P
        self.NTP = -(-self.NT // Q) * Q
        self.NR = (self.NTP + 2) * P
        self.NG = -(-n_edges // GE)
        self.NGP = -(-self.NG // U) * U
        self.NB = -(-self.NGP // P)
        self.NWIN = -(-n_nodes // W)


def bcast(ap, axis, n):
    ap = ap.unsqueeze(axis)
    shape = list(ap.shape)
    shape[axis] = n
    return ap.broadcast_to(shape)


def setup_phase(nc, S, src, dst, type9, type50, t):
    NB, NGP = S.NB, S.NGP
    full, rest = S.E // GE, S.E % GE
    with ExitStack() as c:
        sb = lambda n, s, d=F32: c.enter_context(nc.sbuf_tensor(f"setup_{n}", s, d))
        sem = lambda n: c.enter_context(nc.semaphore(n))
        raw = {k: sb(f"raw_{k}", [P, NB, GE], I32) for k in ("src", "dst", "t9", "t50")}
        dst_f = sb("dst_f", [P, NB, GE])
        low = sb("low", [P, NB, GE])
        src_f = sb("src_f", [P, NB, GE])
        t9_f = sb("t9_f", [P, NB, GE])
        whole = sb("whole", [P, NB, GE], I32)
        part = sb("part", [P, NB, GE], I32)
        rows = sb("rows", [P, NB, IDS, GE], BF16)
        dmin = sb("dmin", [P, NB])
        dmax = sb("dmax", [P, NB])
        span = sb("span", [P, NB])
        spanmax = sb("spanmax", [P, 1])
        wide_f = sb("wide_f", [1, 1])
        one_row = sb("one_row", [1, P])
        narrow = sb("narrow", [P, 1])
        base = sb("base", [P, NB])
        below = sb("below", [P, NGP * J])
        cols = sb("cols", [P, NGP * J])
        type9_cols = sb("type9_cols", [P, NGP * J])
        unique = sb("unique", [P, 1])
        ps_small = c.enter_context(nc.psum_tensor("ps_small", [P, 512], F32))
        ps_base = c.enter_context(nc.psum_tensor("ps_base", [P, 512], F32))
        ps_t = [c.enter_context(nc.psum_tensor(f"ps_t{k}", [P, J, P], F32)) for k in range(2)]
        loaded, consts = sem("loaded"), sem("setup_consts")
        step, found, spread = sem("setup_step"), sem("found"), sem("setup_spread")
        turned, taken, stored, rows_made = sem("turned"), sem("taken"), sem("rows_stored"), sem("rows_made")
        block = c.enter_context(nc.Block())

        parts = [(b, min(P, full - b * P)) for b in range(NB) if full > b * P]

        @block.sync
        def _(sp):
            sp.wait_ge(consts, 4)
            for k, a in (("dst", dst), ("src", src), ("t9", type9), ("t50", type50)):
                g = a[0:full * GE].rearrange("(g e) -> g e", e=GE)
                for b, n in parts:
                    sp.dma_start(raw[k][0:n, b, :], g[b * P:b * P + n, :]).then_inc(loaded, 16)
                if rest:
                    q, b = full % P, full // P
                    sp.dma_start(raw[k][q:q + 1, b, 0:rest],
                                 a[full * GE:S.E].rearrange("(g e) -> g e", g=1)).then_inc(loaded, 16)
            sp.wait_ge(rows_made, 5)
            n = 0
            for b in range(NB):
                m = min(P, NGP - b * P)
                sp.dma_start(t["rows"][b * P:b * P + m, 0:IDS, :], rows[0:m, b, :, :]).then_inc(stored, 16)
                n += 16
            sp.wait_ge(taken, 3 * NB)
            sp.dma_start(t["T9"], type9_cols[:, :]).then_inc(stored, 16)
            sp.wait_ge(stored, n + 16)

        @block.gpsimd
        def _(pool):
            pool.memset(raw["dst"][:, :, :], int(FAR)).then_inc(consts, 1)
            for k in ("src", "t9", "t50"):
                pool.memset(raw[k][:, :, :], -1).then_inc(consts, 1)
            pool.memset(t["ident"][:, :], 0.0).then_inc(consts, 1)
            pool.wait_ge(consts, 5)
            pool.affine_select(out=t["ident"][:, :], in_=t["ident"][:, :], compare_op=ALU.not_equal,
                               fill=1.0, base=0, pattern=[[-1, P]], channel_multiplier=1).then_inc(consts, 1)
            pool.iota(t["iota"][:, :], pattern=[[1, P]], base=0, channel_multiplier=0,
                      allow_small_or_imprecise_dtypes=True).then_inc(consts, 1)
            pool.iota(t["pcol"][:, :], pattern=[[0, 1]], base=0, channel_multiplier=1,
                      allow_small_or_imprecise_dtypes=True).then_inc(consts, 1)
            pool.memset(one_row[:, :], 1.0).then_inc(consts, 1)
            pool.iota(t["win0"][:, :], pattern=[[W, S.NWIN]], base=0, channel_multiplier=0,
                      allow_small_or_imprecise_dtypes=True).then_inc(consts, 1)
            pool.iota(t["win_far"][:, :], pattern=[[1024, S.NWIN]], base=0, channel_multiplier=0,
                      allow_small_or_imprecise_dtypes=True).then_inc(consts, 1)

        @block.vector
        def _(v):
            link = Link(v, step)
            v.wait_ge(loaded, 4 * 16 * (len(parts) + (1 if rest else 0)))
            v.wait_ge(consts, 11)
            link(v.tensor_copy(dst_f[:, :, :], raw["dst"][:, :, :]), False)
            link(v.tensor_copy(src_f[:, :, :], raw["src"][:, :, :]), False)
            link(v.tensor_scalar(t9_f[:, :, :], raw["t9"][:, :, :], 0.0, float(T9 - 1), ALU.max, ALU.min))
            link(v.tensor_reduce(dmax[:, :], dst_f[:, :, :], AX_X, ALU.max), False)
            link(v.tensor_scalar(low[:, :, :], dst_f[:, :, :], 0.0, -2.0 * FAR, ALU.is_lt, ALU.mult))
            link(v.tensor_tensor(low[:, :, :], low[:, :, :], dst_f[:, :, :], ALU.add))
            link(v.tensor_reduce(dmin[:, :], low[:, :, :], AX_X, ALU.min))
            link(v.tensor_tensor(span[:, :], dmax[:, :], dmin[:, :], ALU.subtract))
            link(v.tensor_reduce(spanmax[:, :], span[:, :], AX_X, ALU.max))
            v.sem_inc(found, 1)
            v.wait_ge(spread, 1)
            link(v.tensor_reduce(wide_f[:, :], ps_small[0:1, 0:P], AX_X, ALU.max))
            link(v.tensor_scalar(wide_f[:, :], wide_f[:, :], float(W) - 0.5, None, ALU.is_gt))
            link(v.tensor_copy(t["wide"][:, :], wide_f[:, :]))
            v.sem_inc(found, 1)
            v.wait_ge(spread, 2)
            link(v.tensor_scalar(narrow[:, :], ps_small[:, 256:257], -1.0, 1.0, ALU.mult, ALU.add))
            link(v.tensor_scalar(base[:, :], dmin[:, :], float(S.N - 1), narrow[:, 0:1], ALU.min, ALU.mult))
            v.sem_inc(found, 1)
            for b in range(NB):
                link(v.tensor_scalar(dst_f[:, b, :], dst_f[:, b, :], base[:, b:b + 1], None, ALU.subtract))
            v.sem_inc(found, 1)
            v.wait_ge(spread, 3)
            link(v.tensor_copy(t["base"][0:1, 0:NB * P], ps_base[0:1, 0:NB * P]))
            for k, a in ((0, dst_f), (2, src_f)):
                link(v.tensor_copy(whole[:, :, :], a[:, :, :]))
                link(v.tensor_scalar(part[:, :, :], whole[:, :, :], ~(P - 1), None, ALU.bitwise_and))
                v.tensor_copy(rows[:, :, k, :], part[:, :, :]).then_inc(rows_made, 1)
                v.wait_ge(rows_made, k + 1)
                link(v.tensor_scalar(part[:, :, :], whole[:, :, :], P - 1, None, ALU.bitwise_and))
                v.tensor_copy(rows[:, :, k + 1, :], part[:, :, :]).then_inc(rows_made, 1)
                v.wait_ge(rows_made, k + 2)
            v.tensor_scalar(rows[:, :, 4, :], raw["t50"][:, :, :], 0.0, float(T50 - 1),
                            ALU.max, ALU.min).then_inc(rows_made, 1)
            n = 0
            for out in (t["dst_rel"], cols, type9_cols):
                for b in range(NB):
                    m = min(P, NGP - b * P)
                    v.wait_ge(turned, n + 1)
                    v.tensor_copy(out[:, b * P * J:(b * P + m) * J].rearrange("p (q j) -> p j q", j=J),
                                  ps_t[n % 2][:, :, 0:m]).then_inc(taken, 1)
                    n += 1
            v.wait_ge(taken, n)
            link(v.tensor_scalar(unique[:, :], t["pcol"][:, :], float(S.NP + 1), None, ALU.add))
            link(v.tensor_scalar(below[:, :], cols[:, :], 0.0, unique[:, 0:1], ALU.is_lt, ALU.mult))
            link(v.tensor_tensor(t["src_i"][:, :], cols[:, :], below[:, :], ALU.add))

        @block.tensor
        def _(pe):
            pe.wait_ge(consts, 11)
            pe.wait_ge(found, 1)
            pe.transpose(ps_small[0:1, 0:P], spanmax[:, :], t["ident"][:, :]).then_inc(spread, 1)
            pe.wait_ge(found, 2)
            pe.matmul(ps_small[:, 256:257], one_row[:, :], wide_f[:, :], start=True, stop=True).then_inc(spread, 1)
            pe.wait_ge(found, 3)
            for b in range(NB):
                mm = pe.matmul(ps_base[0:1, b * P:(b + 1) * P], base[:, b:b + 1], t["ident"][:, :],
                               start=True, stop=True)
            mm.then_inc(spread, 1)
            pe.wait_ge(found, 4)
            n = 0
            for a in (dst_f, src_f, t9_f):
                for b in range(NB):
                    if n >= 2:
                        pe.wait_ge(taken, n - 1)
                    for j in range(J):
                        mm = pe.transpose(ps_t[n % 2][:, j, :], a[:, b, :].rearrange("q (p j) -> q j p", j=J)[:, j, :],
                                          t["ident"][:, :])
                    mm.then_inc(turned, 1)
                    n += 1


def norm_constants(link, v, stats, mean, var, tmp):
    link(v.tensor_tensor(mean[:, :], stats[:, :, 1], stats[:, :, 4], ALU.add), False)
    link(v.tensor_tensor(tmp[:, :], stats[:, :, 1], stats[:, :, 4], ALU.subtract), False)
    link(v.tensor_tensor(var[:, :], stats[:, :, 2], stats[:, :, 5], ALU.add))
    link(v.tensor_scalar(mean[:, :], mean[:, :], 0.5, None, ALU.mult), False)
    link(v.scalar_tensor_tensor(tmp[:, :], tmp[:, :], 0.25, tmp[:, :], ALU.mult, ALU.mult), False)
    link(v.tensor_scalar(var[:, :], var[:, :], 1.0 / F, EPS, ALU.mult, ALU.add))
    link(v.tensor_tensor(var[:, :], var[:, :], tmp[:, :], ALU.add))


def first_norm_phase(nc, S, x, t):
    NT, N = S.NT, S.N
    full, rest = N // P, N % P
    with ExitStack() as c:
        sb = lambda n, s, d=F32: c.enter_context(nc.sbuf_tensor(n, s, d))
        sem = lambda n: c.enter_context(nc.semaphore(n))
        TR = S.NR // P
        xs = sb("xs", [P, TR, F])
        hs = sb("hs", [P, TR, F])
        stats = sb("n0_stats", [P, NT, 6])
        mean, var, tmp = sb("n0_mean", [P, NT]), sb("n0_var", [P, NT]), sb("n0_tmp", [P, NT])
        cleared, loaded, step = sem("n0_cleared"), sem("n0_loaded"), sem("n0_step")
        stat, roots, normed, stored = sem("n0_stat"), sem("n0_roots"), sem("n0_normed"), sem("n0_stored")
        block = c.enter_context(nc.Block())

        @block.sync
        def _(sp):
            sp.wait_ge(cleared, 2)
            sp.dma_start(xs[:, 0:full, :], x[0:full * P, :].rearrange("(n p) f -> p n f", p=P)).then_inc(loaded, 16)
            if rest:
                sp.dma_start(xs[0:rest, full, :], x[full * P:N, :]).then_inc(loaded, 16)
            sp.wait_ge(loaded, 16 * (1 + bool(rest)))
            sp.dma_start(t["X0"].rearrange("(n p) f -> p n f", p=P), xs[:, :, :]).then_inc(stored, 16)
            sp.wait_ge(normed, NT)
            sp.dma_start(t["H0"].rearrange("(n p) f -> p n f", p=P), hs[:, :, :]).then_inc(stored, 16)
            sp.wait_ge(stored, 32)

        @block.vector
        def _(v):
            v.memset(xs[:, full:TR, :], 0.0).then_inc(cleared, 1)
            v.memset(hs[:, NT:TR, :], 0.0).then_inc(cleared, 1)
            v.wait_ge(cleared, 2)
            v.wait_ge(loaded, 16 * (1 + bool(rest)))
            with v.Fori(0, NT) as i:
                v.bn_stats(stats[:, ds(i, 1), :], xs[:, ds(i, 1), :]).then_inc(stat, 1)
            v.wait_ge(stat, NT)
            link = Link(v, step)
            norm_constants(link, v, stats, mean, var, tmp)
            v.sem_inc(roots, 1)
            v.wait_ge(roots, 2)
            link(v.reciprocal(var[:, :], var[:, :]))
            link(v.scalar_tensor_tensor(mean[:, :], mean[:, :], -1.0, var[:, :], ALU.mult, ALU.mult))
            v.sem_inc(roots, 1)

        @block.scalar
        def _(act):
            act.wait_ge(roots, 1)
            act.activation(var[:, :], var[:, :], ACT.Sqrt).then_inc(roots, 1)
            act.wait_ge(roots, 3)
            with act.Fori(0, NT) as i:
                act.activation(hs[:, ds(i, 1), :], xs[:, ds(i, 1), :], ACT.Relu, bias=mean[:, ds(i, 1)],
                               scale=var[:, ds(i, 1)]).then_inc(normed, 1)


def forms(eng, S, t, turn, after=None, last_apart=False):
    turns = S.NGP // U
    in_loop = turns - last_apart
    wide = eng.value_load(t["wide"][0:1, 0:1], min_val=0, max_val=1)

    def run(NW, turn_i):
        if in_loop:
            with eng.Fori(0, in_loop) as i:
                turn_i(i)
        if last_apart:
            turn_i(turns - 1)
        if after is not None:
            after(turns * NW)

    def every_window(i):
        with eng.Fori(0, S.NWIN) as w:
            turn(i, w + i * S.NWIN, w)

    with eng.If(wide > 0):
        run(S.NWIN, every_window)
    with eng.Else():
        run(1, lambda i: turn(i, i, None))


def pipelined(eng, S, t, stages, in_order=None, after=None):
    turns = S.NGP // U
    wide = eng.value_load(t["wide"][0:1, 0:1], min_val=0, max_val=1)

    def step(i, s, last):
        for ahead, stage in stages:
            n = s + ahead
            if i is None:
                if n >= 0:
                    stage(n // U, n // U, None, n % U)
            elif not last or n < U:
                stage(i + n // U, i + n // U, None, n % U)

    with eng.If(wide > 0):
        with eng.Fori(0, turns) as i:
            with eng.Fori(0, S.NWIN) as w:
                for s in range(U):
                    for stage in in_order or [stage for _, stage in stages]:
                        stage(i, w + i * S.NWIN, w, s)
        if after is not None:
            after(turns * S.NWIN)
    with eng.Else():
        for s in range(-max(ahead for ahead, _ in stages), 0):
            step(None, s, False)
        with eng.Fori(0, turns - 1) as i:
            for s in range(U):
                step(i, s, False)
        for s in range(U):
            step(turns - 1, s, True)
        if after is not None:
            after(turns)


def window_start(eng, S, t, g, w):
    if w is None:
        return eng.value_load(t["base"][0:1, ds(g, 1)], min_val=0, max_val=S.N - 1)
    return w * W


def one_hot(v, t, out, g, w, op=ALU.is_equal):
    rel = bcast(t["dst_rel"][:, ds(g * J, J)], 2, W)
    window = bcast(t["iota"][:, 0:W], 1, J)
    if w is None:
        return v.tensor_tensor(out, rel, window, op)
    return v.scalar_tensor_tensor(out, rel, t["win0"][:, ds(w, 1)], window, ALU.subtract, op)


def sum_phase(nc, S, t, tag, table, types):
    NGP = S.NGP
    acc, acc9 = t["big"][:, 0, :], t["big"][0:T9, 1, :]
    HI = S.NT
    per = 2 if types else 1
    hots = 4 if types else 1
    with ExitStack() as c:
        sb = lambda n, s, d=F32: c.enter_context(nc.sbuf_tensor(f"{tag}_{n}", s, d))
        sem = lambda n: c.enter_context(nc.semaphore(f"{tag}_{n}"))
        ps = lambda n, s: c.enter_context(nc.psum_tensor(f"{tag}_{n}", s, F32))
        slot = sb("slot", [P, U, J], I32)
        rows = sb("rows", [P, U, J, F])
        onehot = sb("onehot", [P, U, J, W])
        ps_sum = [ps(f"sum{k}", [P, 512]) for k in range(2)]
        idx_ready, multiplied, made, added = sem("idx_ready"), sem("multiplied"), sem("made"), sem("added")
        gathered = [sem(f"gathered{k}") for k in range(U)]
        if types:
            kind = sb("kind", [P, U, J, T9])
            type9 = sb("type9", [P, NGP * J])
            lo_i, hi_i = sb("lo_i", [P, NGP * J], I32), sb("hi_i", [P, NGP * J], I32)
            lo, hi = sb("lo", [P, NGP * J]), sb("hi", [P, NGP * J])
            lo_hot, hi_hot = sb("lo_hot", [P, U, J, P], BF16), sb("hi_hot", [P, U, J, HI], BF16)
            none = sb("none", [P, P], BF16)
            zeros = sb("zeros", [P, S.NR // 4])
            ps_kind = [ps(f"kind{k}", [P, 512]) for k in range(2)]
            ps_hist = ps("hist", [P, 512])
            start, cleared, prep, counts = sem("start"), sem("cleared"), sem("prep"), sem("counts")
        else:
            src_f = sb("src_f", [P, NGP * J])
            before = sb("before", [P, P])
            trash = sb("trash", [P, 1])
            dup, off, idx = sb("dup", [P, NGP * J]), sb("off", [P, NGP * J]), sb("idx", [P, NGP * J], I32)
            id_rows = sb("id_rows", [IDS, 2, GE], BF16)
            type_hot, coef = sb("type_hot", [T50, 2, GE], BF16), sb("coef", [3 * BASES, 2, GE], BF16)
            same, same_b = sb("same", [P, J, P]), sb("same_b", [P, J, P])
            ps_src, ps_type, ps_coef = ps("ps_src", [P, 512]), ps("ps_type", [P, 512]), ps("ps_coef", [P, 512])
            PREP = 12
            idx_out = sem("idx_out")
            consts, prep, spread, hot, coeffed, copied, dv = (
                sem(n) for n in ("consts", "prep", "spread", "hot", "coeffed", "copied", "dv"))
            ids_in, coef_out = [sem(f"ids_in{k}") for k in range(2)], [sem(f"coef_out{k}") for k in range(2)]
        block = c.enter_context(nc.Block())

        if types:
            @block.sync
            def _(sp):
                sp.dma_start(type9[:, :], t["T9"]).then_inc(prep, 16)
                sp.wait_ge(start, 1)
                n = 0
                for k in range(COPIES):
                    flat = t["scat"][k].rearrange("(p n) f -> p (n f)", p=P)
                    for q in range(4):
                        sp.dma_start(flat[:, q * (S.NR // 4):(q + 1) * (S.NR // 4)], zeros[:, :]).then_inc(cleared, 16)
                        n += 16
                sp.wait_ge(cleared, n)
        else:
            @block.sync
            def _(sp):
                def turn(i, r, w):
                    for s in range(U):
                        n, k = r * U + s, s % 2
                        sp.wait_ge(spread, n + 1)
                        sp.dma_start(id_rows[:, k, :], t["rows"][ds(i * U + s, 1), 0:IDS, :].rearrange("a m e -> (a m) e")
                                     ).then_inc(ids_in[k], 16)
                forms(sp, S, t, turn)
                sp.wait_ge(prep, PREP)
                sp.dma_start(t["IDX"], idx[:, :]).then_inc(idx_out, 16)
                sp.wait_ge(idx_out, 16)

        @block.gpsimd
        def _(pool):
            if not types:
                pool.memset(before[:, :], 1.0).then_inc(consts, 1)
                pool.wait_ge(consts, 1)
                pool.affine_select(out=before[:, :], in_=before[:, :], compare_op=ALU.is_gt, fill=0.0, base=0,
                                   pattern=[[-1, P]], channel_multiplier=1).then_inc(consts, 1)

            def turn(i, r, w):
                for s in range(U):
                    pool.wait_ge(idx_ready, r * U + s + 1)
                    pool.nop(nofuse=True)
                    for j in range(J):
                        pool.indirect_dma_start(rows[:, s, j, :], None, table,
                                                bass.IndirectOffsetOnAxis(ap=slot[:, s, j:j + 1], axis=0)
                                                ).then_inc(gathered[s], 16)
            forms(pool, S, t, turn)

        @block.scalar
        def _(act):
            if not types:
                for k in range(2):
                    act.dma_start(coef[:, k, :], t["rows"][0, 0:1, :].broadcast_to([3 * BASES, GE])).then_inc(coef_out[k], 16)

            def turn(i, r, w):
                for s in range(U):
                    act.wait_ge(multiplied, r * U + s + 1)
                    act.activation(slot[:, s, :], t["src_i"][:, ds((i * U + s) * J, J)], ACT.Copy).then_inc(idx_ready, 1)
                    if not types:
                        coefficients(i, r, s)

            def coefficients(i, r, s):
                n, k = r * U + s, s % 2
                act.wait_ge(coeffed, n + 2)
                act.wait_ge(coef_out[k], r * (16 * (U // 2)) + 16 * (s // 2) + 16)
                act.activation(coef[:, k, :], ps_coef[0:3 * BASES, :], ACT.Copy).then_inc(copied, 1)
                act.wait_ge(copied, n + 2)
                act.dma_start(t["rows"][ds(i * U + s, 1), IDS:, :].rearrange("a m e -> (a m) e"), coef[:, k, :]).then_inc(coef_out[k], 16)

            def after(turns):
                for k in range(2):
                    act.wait_ge(coef_out[k], turns * (U // 2) * 16 + 16)
            forms(act, S, t, turn, None if types else after)

        @block.vector
        def _(v):
            v.memset(acc, 0.0).then_inc(added, 1)
            if types:
                v.memset(acc9, 0.0).then_inc(added, 1)
                v.memset(none[:, :], 0.0).then_inc(counts, 1)
                v.memset(zeros[:, :], 0.0).then_inc(start, 1)
                v.tensor_scalar(hi_i[:, :], t["src_i"][:, :], 7, None, ALU.arith_shift_right).then_inc(prep, 1)
                v.tensor_scalar(lo_i[:, :], t["src_i"][:, :], P - 1, None, ALU.bitwise_and).then_inc(prep, 1)
                v.wait_ge(prep, 18)
                v.tensor_copy(hi[:, :], hi_i[:, :]).then_inc(prep, 1)
                v.tensor_copy(lo[:, :], lo_i[:, :]).then_inc(prep, 1)
                v.wait_ge(prep, 20)
            else:
                prepare = Link(v, prep)
                prepare(v.tensor_copy(src_f[:, :], t["src_i"][:, :]), False)
                prepare(v.tensor_scalar(trash[:, :], t["pcol"][:, :], float(S.NP), None, ALU.add), False)
                M17, id17 = IDS + 3 * BASES, t["ident"][0:IDS + 3 * BASES, :]
                for k in range(2):
                    prepare(v.tensor_tensor(t["select"][:, k, :], id17[:, 2 * k:2 * k + 1].broadcast_to([M17, P]),
                                            id17[:, 2 * k + 1:2 * k + 2].broadcast_to([M17, P]), ALU.add), False)
                prepare(v.tensor_copy(t["select"][:, 2, :], id17[:, 4:5].broadcast_to([M17, P])), False)
                for q in range(2):
                    at = lambda part: bcast(id17[:, IDS + part * BASES + 2 * q:IDS + part * BASES + 2 * q + 2], 1, W)
                    both = t["select"][:, 3 + q, :].rearrange("r (n c) -> r n c", c=2)
                    prepare(v.tensor_tensor(both, at(0), at(1), ALU.add))
                    prepare(v.tensor_tensor(both, both, at(2), ALU.add))
                v.wait_ge(consts, 2)
                v.sem_inc(dv, 3)
            v.sem_inc(added, 2 * per)

            def turn(i, r, w):
                for s in range(U):
                    n, g = r * U + s, i * U + s
                    v.wait_ge(multiplied, n + 1)
                    one_hot(v, t, onehot[:, s, :, :], g, w).then_inc(made, 1)
                    if types:
                        v.tensor_tensor(kind[:, s, :, :], bcast(type9[:, ds(g * J, J)], 2, T9),
                                        bcast(t["iota"][:, 0:T9], 1, J), ALU.is_equal).then_inc(made, 1)
                        rel, io = bcast(lo[:, ds(g * J, J)], 2, P), bcast(t["iota"][:, 0:P], 1, J)
                        if w is None:
                            v.tensor_tensor(lo_hot[:, s, :, :], rel, io, ALU.is_equal).then_inc(made, 1)
                        else:
                            v.scalar_tensor_tensor(lo_hot[:, s, :, :], rel, t["win_far"][:, ds(w, 1)], io,
                                                   ALU.add, ALU.is_equal).then_inc(made, 1)
                        v.tensor_tensor(hi_hot[:, s, :, :], bcast(hi[:, ds(g * J, J)], 2, HI),
                                        bcast(t["iota"][:, 0:HI], 1, J), ALU.is_equal).then_inc(made, 1)
                for s in range(U):
                    n, g = r * U + s, i * U + s
                    if not types:
                        repeats(n, g, s)
                    at = window_start(v, S, t, g, w)
                    v.wait_ge(multiplied, n + U + 1)
                    v.wait_ge(added, n * per + 3 * per)
                    v.tensor_tensor(acc[:, ds(at, W)], acc[:, ds(at, W)], ps_sum[s % 2][:, 0:W], ALU.add).then_inc(added, 1)
                    if types:
                        v.tensor_tensor(acc9[:, ds(at, W)], acc9[:, ds(at, W)], ps_kind[s % 2][0:T9, 0:W],
                                        ALU.add).then_inc(added, 1)
            def repeats(n, g, s):
                link = Link(v, dv, n * 3 + 3)
                v.wait_ge(spread, n + 3)
                v.wait_ge(coeffed, n)
                v.tensor_scalar(type_hot[:, s % 2, :], ps_type[0:T50, :], t["pcol"][0:T50, 0:1], None, ALU.is_equal).then_inc(hot, 1)
                link(v.tensor_tensor(same[:, :, :], ps_src[:, :].rearrange("p (e j) -> p j e", j=J),
                                     bcast(src_f[:, ds(g * J, J)], 2, P), ALU.is_equal))
                link(v.tensor_tensor(same_b[:, :, :], same[:, :, :], bcast(before[:, :], 1, J), ALU.mult))
                link(v.tensor_reduce(dup[:, ds(g * J, J)], same_b[:, :, :], AX_X, ALU.add))
            forms(v, S, t, turn)
            if not types:
                assert prepare.n == PREP - 3
                prepare(v.tensor_scalar(off[:, :], src_f[:, :], trash[:, 0:1], -1.0, ALU.subtract, ALU.mult))
                prepare(v.scalar_tensor_tensor(off[:, :], dup[:, :], 0.5, off[:, :], ALU.is_gt, ALU.mult))
                prepare(v.tensor_tensor(idx[:, :], off[:, :], src_f[:, :], ALU.add), False)
            if types:
                v.wait_ge(counts, 2)
                v.tensor_copy(t["deg_src"][:, :], ps_hist[:, 0:HI]).then_inc(counts, 1)

        @block.tensor
        def _(pe):
            if types:
                pe.wait_ge(counts, 1)
                pe.matmul(ps_hist[:, 0:HI], none[:, :], none[:, 0:HI], start=True, stop=False, skip_group_check=True)
            else:
                pe.wait_ge(dv, 3)
                pe.sem_inc(spread, 2)
                pe.sem_inc(coeffed, 1)
                pe.sem_inc(copied, 1)
            pe.sem_inc(multiplied, U)

            def spread_ids(r, s):
                n, k = r * U + s, s % 2
                pe.wait_ge(ids_in[k], r * (16 * (U // 2)) + 16 * (s // 2) + 16)
                pe.wait_ge(dv, n * 3 + 3)
                pe.matmul(ps_type[0:T50, :], t["select"][0:IDS, 2, 0:T50], id_rows[:, k, :], start=True, stop=True)
                pe.matmul(ps_src[:, :], t["select"][0:IDS, 1, :], id_rows[:, k, :], start=True, stop=True).then_inc(spread, 1)

            def coefficients(r, s):
                n, k = r * U + s, s % 2
                pe.wait_ge(hot, n + 1)
                pe.wait_ge(copied, n + 1)
                pe.nop(nofuse=True)
                pe.matmul(ps_coef[0:3 * BASES, :], t["relation"][0:T50, :], type_hot[:, k, :], start=True, stop=True).then_inc(coeffed, 1)

            def turn(i, r, w):
                for s in range(U):
                    n = r * U + s
                    if not types:
                        spread_ids(r, s)
                    pe.wait_ge(made, n * hots + hots)
                    pe.wait_ge(added, n * per + 2 * per)
                    pe.wait_ge(gathered[s], r * (16 * J) + 16 * J)
                    for j in range(J):
                        mm = pe.matmul(ps_sum[s % 2][:, 0:W], rows[:, s, j, :], onehot[:, s, j, :],
                                       start=(j == 0), stop=(j == J - 1))
                    if types:
                        for j in range(J):
                            pe.matmul(ps_kind[s % 2][0:T9, 0:W], kind[:, s, j, :], onehot[:, s, j, :],
                                      start=(j == 0), stop=(j == J - 1))
                        for j in range(J):
                            mm = pe.matmul(ps_hist[:, 0:HI], lo_hot[:, s, j, :], hi_hot[:, s, j, :],
                                           start=False, stop=False, skip_group_check=True)
                    mm.then_inc(multiplied, 1)
                    if not types:
                        coefficients(r, s)
            forms(pe, S, t, turn)
            if types:
                pe.matmul(ps_hist[:, 0:HI], none[:, :], none[:, 0:HI], start=False, stop=True,
                          skip_group_check=True).then_inc(counts, 1)


WEIGHTS = {
    "msg_wT": F, "ih_wT": 3 * F, "hh_wT": 3 * F, "gcn_wT": F, "bases": BASES * F, "node_wT": F, "edge_wT": 2 * F, "out_wT": F,
    "gate_b": 4 * F, "gcn_b": F, "gcn_gamma": F, "gcn_beta": F, "proj_b": F, "attn": F, "out_b": F,
    "out_gamma": F, "out_beta": F, "embed_b": F, "ones": 1,
}


def weights_phase(nc, S, a, t):
    with ExitStack() as c:
        sb = lambda n, s, d=F32: c.enter_context(nc.sbuf_tensor(f"w_{n}", s, d))
        sem = lambda n: c.enter_context(nc.semaphore(f"w_{n}"))
        square = [("L0_gnn_W_msg", 0, "msg_wT", 0), ("L1_gnn_W", 0, "gcn_wT", 0), ("L3_gnn_W_out_w", 0, "out_wT", 0),
                  ("L3_gnn_W_proj_w", 0, "node_wT", 0)]
        square += [("L0_gnn_W_ih", q, "ih_wT", q) for q in range(3)] + [("L0_gnn_W_hh", q, "hh_wT", q) for q in range(3)]
        nat = sb("natural", [P, len(square), F])
        edge_nat = sb("edge_natural", [P, 2, ED])
        bias2 = sb("bias2", [P, 3 * F])
        msg_b = sb("msg_b", [T9, F])
        comps, alpha = sb("comps", [T50, BASES]), sb("alpha", [T50, 1])
        ps = [c.enter_context(nc.psum_tensor(f"w_ps{k}", [P, 512], F32)) for k in range(2)]
        loaded, turned, taken, step = sem("loaded"), sem("turned"), sem("taken"), sem("step")
        block = c.enter_context(nc.Block())
        row = lambda ap, n=P: ap.rearrange("(a f) -> a f", a=1).broadcast_to([n, ap.shape[0]])
        loads = [(nat[:, m, :], a[w][q * P:(q + 1) * P, 0:F]) for m, (w, q, _, _) in enumerate(square)]
        loads += [(edge_nat[:, h, :], a["L3_gnn_W_proj_w"][:, F:F + ED]) for h in range(2)]
        loads += [(t["bases"][:, (b % 2 * 2 + b // 2) * F:(b % 2 * 2 + b // 2 + 1) * F], a["L2_gnn_bases"][b])
                  for b in range(BASES)]
        loads += [(t["gate_b"][:, 0:3 * F], row(a["L0_gnn_b_ih"])), (bias2[:, :], row(a["L0_gnn_b_hh"])),
                  (msg_b[:, :], row(a["L0_gnn_b_msg"], T9)), (t["embed_b"][0:T9, :], a["L0_gnn_edge_embed"]),
                  (comps[:, :], a["L2_gnn_comps"]), (alpha[:, :], a["L2_gnn_alpha"]),
                  (t["gcn_b"][:, :], row(a["L1_gnn_b"])), (t["gcn_gamma"][:, :], row(a["L1_gnn_gamma"])),
                  (t["gcn_beta"][:, :], row(a["L1_gnn_beta"])), (t["proj_b"][:, :], row(a["L3_gnn_W_proj_b"])),
                  (t["attn"][:, :], row(a["L3_gnn_attn_vec"].rearrange("h d -> (h d)"))),
                  (t["out_b"][:, :], row(a["L3_gnn_W_out_b"])), (t["out_gamma"][:, :], row(a["L3_gnn_ln_gamma"])),
                  (t["out_beta"][:, :], row(a["L3_gnn_ln_beta"]))]

        @block.sync
        def _(sp):
            for to, of in loads:
                sp.dma_start(to, of).then_inc(loaded, 16)

        @block.tensor
        def _(pe):
            pe.wait_ge(loaded, 16 * len(loads))
            for m in range(len(square)):
                if m >= 2:
                    pe.wait_ge(taken, m - 1)
                pe.transpose(ps[m % 2][:, 0:P], nat[:, m, :], t["ident"][:, :]).then_inc(turned, 1)
            m = len(square)
            pe.wait_ge(taken, m - 1)
            pe.transpose(ps[m % 2][:, 0:P], edge_nat[:, :, :].rearrange("p h f -> p (h f)"), t["ident"][:, :]).then_inc(turned, 1)

        @block.vector
        def _(v):
            v.wait_ge(loaded, 16 * len(loads))
            link = Link(v, step)
            for m, (_, _, to, q) in enumerate(square):
                v.wait_ge(turned, m + 1)
                v.tensor_copy(t[to][:, q * F:(q + 1) * F], ps[m % 2][:, 0:P]).then_inc(taken, 1)
            link(v.memset(t["edge_wT"][:, :], 0.0))
            m = len(square)
            v.wait_ge(turned, m + 1)
            for h in range(2):
                link(v.tensor_copy(t["edge_wT"][h * ED:(h + 1) * ED, h * F:(h + 1) * F], ps[m % 2][h * ED:(h + 1) * ED, 0:P]), False)
            link(v.tensor_copy(t["gate_b"][:, 3 * F:4 * F], bias2[:, 2 * F:3 * F]), False)
            link(v.tensor_tensor(t["gate_b"][:, 0:2 * F], t["gate_b"][:, 0:2 * F], bias2[:, 0:2 * F], ALU.add), False)
            link(v.tensor_tensor(t["embed_b"][0:T9, :], t["embed_b"][0:T9, :], msg_b[:, :], ALU.add), False)
            link(v.memset(t["ones"][:, :], 1.0), False)
            link(v.tensor_scalar(comps[:, :], comps[:, :], alpha[:, 0:1], None, ALU.mult))
            for k in range(3):
                part = t["relation"][0:T50, k * BASES:(k + 1) * BASES]
                link(v.tensor_copy(part, comps[:, :]))
                if k < 2:
                    link(v.tensor_tensor(comps[:, :], comps[:, :], part, ALU.subtract))


def tiles_of(table, at, n):
    return table.rearrange("(n p) f -> p n f", p=P)[:, ds(at, n), :]


def gru_phase(nc, S, t):
    NT, NR, PAIRS = S.NT, S.NR, S.NTP // 2
    acc, acc9 = t["big"][:, 0, :], t["big"][0:T9, 1, :]
    with ExitStack() as c:
        sb = lambda n, s, d=F32: c.enter_context(nc.sbuf_tensor(f"gru_{n}", s, d))
        sem = lambda n: c.enter_context(nc.semaphore(f"gru_{n}"))
        ps = lambda n, s: c.enter_context(nc.psum_tensor(f"gru_{n}", s, F32))
        res = sb("res", [P, S.NTP, F])
        h_a, h_b, x_b = sb("h_a", [P, 2, F]), sb("h_b", [P, 2, F]), sb("x_b", [P, 2, F])
        aggs, kinds = sb("aggs", [P, 2 * P]), sb("kinds", [T9, 2 * P])
        msgT, hT = sb("msgT", [P, 2 * P]), sb("hT", [P, 2 * P])
        gates, rz, cand, n_out = sb("gates", [P, 2, 4 * F]), sb("rz", [P, 2, 2 * F]), sb("cand", [P, 2, F]), sb("n_out", [P, 2, F])
        stats = sb("stats", [P, S.NTP, 6])
        mean, var, tmp, deg = (sb(n, [P, S.NTP]) for n in ("mean", "var", "tmp", "deg"))
        ps_msg, ps_h, ps_g, ps_deg = ps("ps_msg", [P, 512]), ps("ps_h", [P, 512]), ps("ps_g", [P, 2, 512]), ps("ps_deg", [P, 512])
        h_in, b_in, turned, staged, messaged = sem("h_in"), sem("b_in"), sem("turned"), sem("staged"), sem("messaged")
        copied, gated, gate_free, dv, acted = sem("copied"), sem("gated"), sem("gate_free"), sem("dv"), sem("acted")
        fin, roots, normed, stored = sem("fin"), sem("roots"), sem("normed"), sem("stored")
        C = 9
        block = c.enter_context(nc.Block())

        @block.sync
        def _(sp):
            def ahead(j):
                sp.wait_ge(turned, j + 1)
                sp.dma_start(h_a[:, :, :], tiles_of(t["H0"], j * 2, 2)).then_inc(h_in, 16)
            ahead(0)
            with sp.Fori(0, PAIRS) as i:
                ahead(i + 1)
                sp.wait_ge(dv, i * C + C)
                sp.dma_start(h_b[:, :, :], tiles_of(t["H0"], i * 2, 2)).then_inc(b_in, 16)
                sp.dma_start(x_b[:, :, :], tiles_of(t["X0"], i * 2, 2)).then_inc(b_in, 16)
            sp.wait_ge(dv, PAIRS * C + C)
            sp.dma_start(tiles_of(t["X1"], 0, S.NTP), res[:, :, :]).then_inc(stored, 16)
            sp.wait_ge(normed, NT + 1)
            sp.dma_start(tiles_of(t["H1"], 0, NR // P), acc.rearrange("p (n f) -> p n f", f=F)).then_inc(stored, 16)
            sp.wait_ge(stored, 32)
            sp.wait_ge(h_in, 16 * PAIRS + 16)

        @block.tensor
        def _(pe):
            pe.sem_inc(turned, 1)
            pe.sem_inc(gated, 1)

            def ahead(j):
                pe.wait_ge(h_in, j * 16 + 16)
                pe.wait_ge(copied, j * 2 + 2)
                for k in range(2):
                    mm = pe.transpose(ps_h[:, k * P:(k + 1) * P], h_a[:, k, :], t["ident"][:, :])
                mm.then_inc(turned, 1)
                pe.wait_ge(staged, j * 2 + 2)
                pe.matmul(ps_msg[:, 0:2 * P], t["msg_wT"][:, :], aggs[:, :], start=True, stop=False)
                pe.matmul(ps_msg[:, 0:2 * P], t["embed_b"][0:T9, :], kinds[:, :], start=False, stop=True).then_inc(messaged, 1)
                pe.wait_ge(copied, j * 2 + 4)
                pe.wait_ge(gate_free, j * 2 + 2)
                for k in range(2):
                    m, h = msgT[:, k * P:(k + 1) * P], hT[:, k * P:(k + 1) * P]
                    pe.matmul(ps_g[:, k, 0:2 * F], m, t["ih_wT"][:, 0:2 * F], start=True, stop=False)
                    pe.matmul(ps_g[:, k, 0:2 * F], h, t["hh_wT"][:, 0:2 * F], start=False, stop=True)
                    pe.matmul(ps_g[:, k, 2 * F:3 * F], m, t["ih_wT"][:, 2 * F:3 * F], start=True, stop=True)
                    pe.matmul(ps_g[:, k, 3 * F:4 * F], h, t["hh_wT"][:, 2 * F:3 * F], start=True, stop=True)
                    mm = pe.matmul(ps_deg[:, k:k + 1], kinds[:, k * P:(k + 1) * P], t["ones"][0:T9, :], start=True, stop=True)
                mm.then_inc(gated, 1)
            ahead(0)
            with pe.Fori(0, PAIRS) as i:
                ahead(i + 1)

        @block.scalar
        def _(act):
            act.sem_inc(copied, 2)

            def ahead(j):
                act.wait_ge(gated, j + 1)
                act.activation(aggs[:, :], acc[:, ds(j * (2 * P), 2 * P)], ACT.Copy).then_inc(staged, 1)
                act.activation(kinds[:, :], acc9[:, ds(j * (2 * P), 2 * P)], ACT.Copy).then_inc(staged, 1)
                act.wait_ge(turned, j + 2)
                act.activation(hT[:, :], ps_h[:, 0:2 * P], ACT.Copy).then_inc(copied, 1)
                act.wait_ge(messaged, j + 1)
                act.activation(msgT[:, :], ps_msg[:, 0:2 * P], ACT.Copy).then_inc(copied, 1)
            ahead(0)
            with act.Fori(0, PAIRS) as i:
                ahead(i + 1)
                act.wait_ge(dv, i * C + C + 1)
                act.activation(rz[:, :, :], gates[:, :, 0:2 * F], ACT.Sigmoid).then_inc(acted, 1)
                act.wait_ge(dv, i * C + C + 4)
                act.activation(n_out[:, :, :], cand[:, :, :], ACT.Tanh).then_inc(acted, 1)
            act.wait_ge(roots, 1)
            act.activation(var[:, :], var[:, :], ACT.Sqrt).then_inc(roots, 1)
            act.activation(deg[:, :], deg[:, :], ACT.Sqrt).then_inc(roots, 1)
            act.wait_ge(roots, 4)
            with act.Fori(0, NT) as i:
                act.activation(acc[:, ds(i * F, F)], res[:, ds(i, 1), :], ACT.Relu, bias=mean[:, ds(i, 1)],
                               scale=var[:, ds(i, 1)]).then_inc(normed, 1)

        @block.vector
        def _(v):
            v.sem_inc(gate_free, 2)
            v.sem_inc(dv, C)
            with v.Fori(0, PAIRS) as i:
                link = Link(v, dv, i * C + C)
                v.wait_ge(gated, i + 2)
                link(v.tensor_tensor(gates[:, :, :], ps_g[:, :, :], bcast(t["gate_b"][:, :], 1, 2), ALU.add))
                v.sem_inc(gate_free, 1)
                link(v.tensor_copy(deg[:, ds(i * 2, 2)], ps_deg[:, 0:2]))
                v.sem_inc(gate_free, 1)
                v.wait_ge(acted, i * 2 + 1)
                link(v.tensor_tensor(cand[:, :, :], rz[:, :, 0:F], gates[:, :, 3 * F:4 * F], ALU.mult))
                link(v.tensor_tensor(cand[:, :, :], cand[:, :, :], gates[:, :, 2 * F:3 * F], ALU.add))
                v.wait_ge(acted, i * 2 + 2)
                v.wait_ge(b_in, i * 32 + 32)
                link(v.tensor_tensor(h_b[:, :, :], h_b[:, :, :], n_out[:, :, :], ALU.subtract))
                link(v.tensor_tensor(h_b[:, :, :], h_b[:, :, :], rz[:, :, F:2 * F], ALU.mult))
                link(v.tensor_tensor(h_b[:, :, :], h_b[:, :, :], n_out[:, :, :], ALU.add))
                x1 = res[:, ds(i * 2, 2), :]
                link(v.tensor_tensor(x1, h_b[:, :, :], x_b[:, :, :], ALU.add))
                v.bn_stats(stats[:, ds(i * 2, 1), :], res[:, ds(i * 2, 1), :])
                link(v.bn_stats(stats[:, ds(i * 2 + 1, 1), :], res[:, ds(i * 2 + 1, 1), :]), False)
                assert link.n == C
            v.wait_ge(dv, PAIRS * C + C)
            v.wait_ge(gated, PAIRS + 2)
            link = Link(v, fin)
            norm_constants(link, v, stats, mean, var, tmp)
            link(v.tensor_scalar(deg[:, :], deg[:, :], 1.0, None, ALU.add))
            v.sem_inc(roots, 1)
            v.wait_ge(roots, 3)
            link(v.reciprocal(var[:, :], var[:, :]))
            link(v.reciprocal(t["dinv_in"][:, :], deg[:, :]))
            link(v.tensor_tensor(var[:, :], var[:, :], t["dinv_in"][:, :], ALU.mult))
            link(v.scalar_tensor_tensor(mean[:, :], mean[:, :], -1.0, var[:, :], ALU.mult, ALU.mult))
            v.memset(acc[:, NT * F:NR], 0.0).then_inc(normed, 1)
            v.sem_inc(roots, 1)


def normed_sum(v, link, res, i, mean, var, gamma, beta, x_old):
    for k in range(Q):
        at = i * Q + k
        link(v.tensor_scalar(res[:, ds(at, 1), :], res[:, ds(at, 1), :], mean[:, ds(at, 1)], var[:, ds(at, 1)],
                             ALU.subtract, ALU.mult), k == Q - 1)
    four = res[:, ds(i * Q, Q), :]
    link(v.tensor_tensor(four, four, bcast(gamma[:, :], 1, Q), ALU.mult))
    link(v.tensor_tensor(four, four, bcast(beta[:, :], 1, Q), ALU.add))
    link(v.tensor_tensor(four, four, x_old, ALU.add))


def gcn_phase(nc, S, t):
    NT, TURNS = S.NT, S.NTP // Q
    acc = t["big"][:, 0, :]
    with ExitStack() as c:
        sb = lambda n, s, d=F32: c.enter_context(nc.sbuf_tensor(f"gcn_{n}", s, d))
        sem = lambda n: c.enter_context(nc.semaphore(f"gcn_{n}"))
        ps = lambda n, s: c.enter_context(nc.psum_tensor(f"gcn_{n}", s, F32))
        res = sb("res", [P, S.NTP, F])
        mean, var, tmp = (sb(n, [P, S.NTP]) for n in ("mean", "var", "tmp"))
        blocks = c.enter_context(ExitStack())
        own = lambda n, s: blocks.enter_context(nc.sbuf_tensor(f"gcn_{n}", s, F32))
        h_q, aggs, x_q = own("h_q", [P, Q, F]), own("aggs", [P, Q * P]), own("x_q", [P, Q, F])
        stats = own("stats", [P, S.NTP, 6])
        ps_h, ps_o = ps("ps_h", [P, 512]), ps("ps_o", [P, 512])
        h_in, turned, multiplied, dv = sem("h_in"), sem("turned"), sem("multiplied"), sem("dv")
        dv2, fin, roots, stored = sem("dv2"), sem("fin"), sem("roots"), sem("stored")
        C, C2 = 9, 11
        block = blocks.enter_context(nc.Block())

        @block.sync
        def _(sp):
            with sp.Fori(0, TURNS) as i:
                sp.wait_ge(turned, i + 1)
                sp.dma_start(h_q[:, :, :], tiles_of(t["H1"], i * Q, Q)).then_inc(h_in, 16)
            with sp.Fori(0, TURNS) as i:
                sp.wait_ge(dv2, i * C2 + C2)
                sp.dma_start(x_q[:, :, :], tiles_of(t["X1"], i * Q, Q)).then_inc(h_in, 16)
            sp.wait_ge(dv2, TURNS * C2 + C2)
            sp.dma_start(tiles_of(t["X2"], 0, S.NTP), res[:, :, :]).then_inc(stored, 16)
            sp.wait_ge(stored, 16)

        @block.tensor
        def _(pe):
            pe.sem_inc(turned, 1)
            with pe.Fori(0, TURNS) as i:
                pe.wait_ge(h_in, i * 16 + 16)
                pe.wait_ge(dv, i * C + C)
                for k in range(Q):
                    mm = pe.transpose(ps_h[:, k * P:(k + 1) * P], h_q[:, k, :], t["ident"][:, :])
                mm.then_inc(turned, 1)
                pe.wait_ge(dv, i * C + C + 1)
                for k in range(Q):
                    mm = pe.matmul(ps_o[:, k * P:(k + 1) * P], aggs[:, k * P:(k + 1) * P], t["gcn_wT"][:, :],
                                   start=True, stop=True)
                mm.then_inc(multiplied, 1)

        @block.vector
        def _(v):
            v.sem_inc(dv, C)
            with v.Fori(0, TURNS) as i:
                link = Link(v, dv, i * C + C)
                v.wait_ge(turned, i + 2)
                link(v.tensor_tensor(aggs[:, :], ps_h[:, :], acc[:, ds(i * (Q * P), Q * P)], ALU.add))
                v.wait_ge(multiplied, i + 1)
                for k in range(Q):
                    link(v.scalar_tensor_tensor(res[:, ds(i * Q + k, 1), :].rearrange("p a f -> p (a f)"),
                                                ps_o[:, k * P:(k + 1) * P], t["dinv_in"][:, ds(i * Q + k, 1)],
                                                t["gcn_b"][:, :], ALU.mult, ALU.add), k == Q - 1)
                for k in range(Q):
                    link(v.bn_stats(stats[:, ds(i * Q + k, 1), :], res[:, ds(i * Q + k, 1), :]), False)
                assert link.n == C
            v.wait_ge(dv, TURNS * C + C)
            link = Link(v, fin)
            norm_constants(link, v, stats, mean, var, tmp)
            v.sem_inc(roots, 1)
            v.wait_ge(roots, 2)
            link(v.reciprocal(var[:, :], var[:, :]))
            v.sem_inc(dv2, C2)
            with v.Fori(0, TURNS) as i:
                link2 = Link(v, dv2, i * C2 + C2)
                v.wait_ge(h_in, i * 16 + 16 * TURNS + 16)
                normed_sum(v, link2, res, i, mean, var, t["gcn_gamma"], t["gcn_beta"], x_q[:, :, :])
                for k in range(Q):
                    link2(v.bn_stats(stats[:, ds(i * Q + k, 1), :], res[:, ds(i * Q + k, 1), :]), False)
                assert link2.n == C2
            v.wait_ge(dv2, TURNS * C2 + C2)
            norm_constants(link, v, stats, mean, var, tmp)
            link(v.tensor_scalar(tmp[:, 0:NT], t["deg_src"][:, :], 1.0, None, ALU.max))
            v.sem_inc(roots, 1)
            v.wait_ge(roots, 5)
            link(v.reciprocal(var[:, :], var[:, :]))
            link(v.reciprocal(tmp[:, 0:NT], tmp[:, 0:NT]))
            if S.NTP > NT:
                link(v.memset(t["dinv_src"][:, NT:S.NTP], 0.0))
            link(v.scalar_tensor_tensor(t["dinv_src"][:, 0:NT], t["deg_src"][:, :], 0.5, tmp[:, 0:NT], ALU.is_gt, ALU.mult))
            link(v.tensor_tensor(var[:, :], var[:, :], t["dinv_src"][:, :], ALU.mult))
            link(v.scalar_tensor_tensor(mean[:, :], mean[:, :], -1.0, var[:, :], ALU.mult, ALU.mult))

        @block.scalar
        def _(act):
            act.wait_ge(roots, 1)
            act.activation(var[:, :], var[:, :], ACT.Sqrt).then_inc(roots, 1)
            act.wait_ge(roots, 3)
            act.activation(var[:, :], var[:, :], ACT.Sqrt).then_inc(roots, 1)
            act.activation(tmp[:, 0:NT], tmp[:, 0:NT], ACT.Sqrt).then_inc(roots, 1)
        blocks.close()
        product_block(nc, S, t, "mixes", res, mean, var, t["bases"], BASES, None, t["HB"], None)


def product_block(nc, S, t, tag, res, mean, var, weight, M, bias, table, h_table):
    TURNS = S.NTP // Q
    with ExitStack() as c:
        sb = lambda n, s, d=F32: c.enter_context(nc.sbuf_tensor(f"{tag}_{n}", s, d))
        sem = lambda n: c.enter_context(nc.semaphore(f"{tag}_{n}"))
        ps = lambda n, s: c.enter_context(nc.psum_tensor(f"{tag}_{n}", s, F32))
        h_q, hT, prod = sb("h_q", [P, Q, F]), sb("hT", [P, Q * P]), sb("prod", [P, Q, M * F])
        ps_h, ps_b = ps("ps_h", [P, 512]), ps("ps_b", [P, Q, 512])
        made, turned, taken, based, out, saved, free = (
            sem(n) for n in ("made", "turned", "taken", "based", "out", "saved", "free"))
        stores = 1 + (h_table is not None)
        extra = S.NR - S.NTP * P
        pads = c.enter_context(nc.sbuf_tensor(f"{tag}_pads", [P, extra // P, M * F], F32))
        padded = sem("padded")
        block = c.enter_context(nc.Block())

        @block.sync
        def _(sp):
            sp.wait_ge(padded, 1)
            sp.dma_start(tiles_of(table, S.NTP, extra // P), pads[:, :, :]).then_inc(padded, 16)
            sp.sem_inc(free, 1)
            with sp.Fori(0, TURNS) as i:
                sp.wait_ge(out, i * 2 + 4)
                sp.dma_start(tiles_of(table, i * Q, Q), prod[:, :, :]).then_inc(saved, 16)
                if h_table is not None:
                    sp.wait_ge(made, i * Q + Q)
                    sp.dma_start(tiles_of(h_table, i * Q, Q), h_q[:, :, :]).then_inc(saved, 16)
                sp.wait_ge(saved, i * (16 * stores) + 16 * stores)
                sp.sem_inc(free, 1)
            sp.wait_ge(padded, 17)

        @block.scalar
        def _(act):
            with act.Fori(0, TURNS) as i:
                act.wait_ge(turned, i + 1)
                if h_table is not None:
                    act.wait_ge(free, i + 1)
                for k in range(Q):
                    at = i * Q + k
                    act.activation(h_q[:, k, :], res[:, ds(at, 1), :].rearrange("p a f -> p (a f)"), ACT.Relu,
                                   bias=mean[:, ds(at, 1)], scale=var[:, ds(at, 1)]).then_inc(made, 1)
                if bias is None:
                    act.wait_ge(based, i + 1)
                    act.wait_ge(free, i + 1)
                    for k in range(Q // 2, Q):
                        cp = act.activation(prod[:, k, :], ps_b[:, k, 0:M * F], ACT.Copy)
                    cp.then_inc(out, 1)

        @block.tensor
        def _(pe):
            pe.sem_inc(turned, 1)
            with pe.Fori(0, TURNS) as i:
                pe.wait_ge(made, i * Q + Q)
                pe.wait_ge(taken, i + 1)
                for k in range(Q):
                    mm = pe.transpose(ps_h[:, k * P:(k + 1) * P], h_q[:, k, :], t["ident"][:, :])
                mm.then_inc(turned, 1)
                pe.wait_ge(taken, i + 2)
                pe.wait_ge(out, i * 2 + 2)
                for k in range(Q):
                    mm = pe.matmul(ps_b[:, k, 0:M * F], hT[:, k * P:(k + 1) * P], weight[:, :], start=True, stop=True)
                mm.then_inc(based, 1)

        @block.vector
        def _(v):
            v.memset(pads[:, :, :], 0.0).then_inc(padded, 1)
            v.sem_inc(out, 2)
            v.sem_inc(taken, 1)
            with v.Fori(0, TURNS) as i:
                v.wait_ge(turned, i + 2)
                v.tensor_copy(hT[:, :], ps_h[:, :]).then_inc(taken, 1)
                v.wait_ge(based, i + 1)
                v.wait_ge(free, i + 1)
                if bias is None:
                    for k in range(Q // 2):
                        cp = v.tensor_copy(prod[:, k, :], ps_b[:, k, 0:M * F])
                    cp.then_inc(out, 1)
                else:
                    v.tensor_tensor(prod[:, 0:2, :], ps_b[:, 0:2, 0:F], bcast(bias[:, :], 1, 2), ALU.add).then_inc(out, 1)
                    v.tensor_tensor(prod[:, 2:4, :], ps_b[:, 2:4, 0:F], bcast(bias[:, :], 1, 2), ALU.add).then_inc(out, 1)


def relation_norm_phase(nc, S, t):
    TURNS = S.NTP // Q
    with ExitStack() as c:
        sb = lambda n, s, d=F32: c.enter_context(nc.sbuf_tensor(f"rel_{n}", s, d))
        sem = lambda n: c.enter_context(nc.semaphore(f"rel_{n}"))
        res = sb("res", [P, S.NTP, F])
        mean, var, tmp = (sb(n, [P, S.NTP]) for n in ("mean", "var", "tmp"))
        blocks = c.enter_context(ExitStack())
        own = lambda n, s: blocks.enter_context(nc.sbuf_tensor(f"rel_{n}", s, F32))
        parts = own("parts", [P, 2, COPIES, 2 * F])
        x_q = own("x_q", [P, Q, F])
        total = own("total", [P, Q, F])
        stats = own("stats", [P, S.NTP, 6])
        part_in = [sem(f"part_in{k}") for k in range(2)]
        x_in, dv, fin, roots, stored = sem("x_in"), sem("dv"), sem("fin"), sem("roots"), sem("stored")
        C = 2 + 2 * Q
        block = blocks.enter_context(nc.Block())

        @block.sync
        def _(sp):
            with sp.Fori(0, TURNS) as i:
                for k in range(2):
                    sp.wait_ge(dv, i * C + 1 + k)
                    for q in range(COPIES):
                        sp.dma_start(parts[:, k, q, :].rearrange("p (n f) -> p n f", n=2),
                                     tiles_of(t["scat"][q], i * Q + 2 * k, 2)).then_inc(part_in[k], 16)
                    if k == 0:
                        sp.wait_ge(dv, i * C + C)
                        sp.dma_start(x_q[:, :, :], tiles_of(t["X2"], i * Q, Q)).then_inc(x_in, 16)
            sp.wait_ge(dv, TURNS * C + C)
            sp.dma_start(tiles_of(t["X3"], 0, S.NTP), res[:, :, :]).then_inc(stored, 16)
            sp.wait_ge(stored, 16)

        @block.vector
        def _(v):
            v.sem_inc(dv, C)
            with v.Fori(0, TURNS) as i:
                link = Link(v, dv, i * C + C)
                for k in range(2):
                    v.wait_ge(part_in[k], i * (16 * COPIES) + 16 * COPIES)
                    link(v.tensor_reduce(total[:, 2 * k:2 * k + 2, :].rearrange("p n f -> p (n f)"),
                                         parts[:, k, :, :].rearrange("p c f -> p f c"), AX_X, ALU.add), k == 1)
                v.wait_ge(x_in, i * 16 + 16)
                for k in range(Q):
                    link(v.scalar_tensor_tensor(res[:, ds(i * Q + k, 1), :].rearrange("p a f -> p (a f)"), total[:, k, :],
                                                t["dinv_src"][:, ds(i * Q + k, 1)], x_q[:, k, :], ALU.mult, ALU.add), k == Q - 1)
                for k in range(Q):
                    link(v.bn_stats(stats[:, ds(i * Q + k, 1), :], res[:, ds(i * Q + k, 1), :]), False)
                assert link.n == C
            v.wait_ge(dv, TURNS * C + C)
            link = Link(v, fin)
            norm_constants(link, v, stats, mean, var, tmp)
            v.sem_inc(roots, 1)
            v.wait_ge(roots, 2)
            link(v.reciprocal(var[:, :], var[:, :]))
            link(v.scalar_tensor_tensor(mean[:, :], mean[:, :], -1.0, var[:, :], ALU.mult, ALU.mult))

        @block.scalar
        def _(act):
            act.wait_ge(roots, 1)
            act.activation(var[:, :], var[:, :], ACT.Sqrt).then_inc(roots, 1)
        blocks.close()
        product_block(nc, S, t, "proj", res, mean, var, t["node_wT"], 1, t["proj_b"], t["proj"], t["H3"])


def relation_phase(nc, S, t):
    NGP, R2, R4 = S.NGP, 2, 4
    ROWS = IDS + 3 * BASES
    with ExitStack() as c:
        sb = lambda n, s, d=F32: c.enter_context(nc.sbuf_tensor(f"msg_{n}", s, d))
        sem = lambda n: c.enter_context(nc.semaphore(f"msg_{n}"))
        ps = lambda n, s: c.enter_context(nc.psum_tensor(f"msg_{n}", s, F32))
        src_f = sb("src_f", [P, NGP * J])
        rows = sb("rows", [ROWS, R4, GE], BF16)
        hb = sb("hb", [P, R4, 2, F])
        node = sb("node", [P, 1])
        node_i = sb("node_i", [P, 1], I32)
        node_w = sb("node_w", [P, S.NWIN])
        dst_sp = sb("dst_sp", [P, R2, GE])
        lhs = sb("lhs", [P, R2, 2, GE])
        same = sb("same", [P, R4, J, P])
        msg = sb("msg", [P, R2, GE])
        out = sb("out", [P, R2, J, F])
        idx, idx_all = sb("idx", [P, R2, J], I32), sb("idx_all", [P, NGP * J], I32)
        ps_dst, ps_src, ps_c = ps("ps_dst", [P, 512]), ps("ps_src", [P, 512]), ps("ps_c", [P, 2, 512])
        ps_msg, ps_sum = [ps(f"ps_msg{k}", [P, 512]) for k in range(R2)], [ps(f"ps_sum{k}", [P, 512]) for k in range(R2)]
        loaded = [sem(f"loaded{k}") for k in range(R4)]
        scattered = [sem(f"scattered{k}") for k in range(R2)]
        src_spread, dst_spread, prep, idx_in = sem("src_spread"), sem("dst_spread"), sem("prep"), sem("idx_in")
        spread, mixed, summed = sem("spread"), sem("mixed"), sem("summed")
        same_made, dst_copied = sem("same_made"), sem("dst_copied")
        lhs_made, msg_copied, out_copied = sem("lhs_made"), sem("msg_copied"), sem("out_copied")
        block = c.enter_context(nc.Block())

        @block.sync
        def _(sp):
            def load(i, r, w, s):
                n, g = r * U + s, i * U + s
                sp.wait_ge(spread, n + 1)
                sp.dma_start(rows[:, s, :], t["rows"][ds(g, 1), :, :].rearrange("a m e -> (a m) e")).then_inc(loaded[s], 16)
                at = window_start(sp, S, t, g, w)
                sp.wait_ge(mixed, n + 1)
                sp.dma_start(hb[:, s, :, :].rearrange("p q f -> p (q f)"),
                             t["HB"][ds(at, W), :].rearrange("n (c f) -> (n c) f", c=2)).then_inc(loaded[s], 16)
            pipelined(sp, S, t, [(0, load)])

        @block.gpsimd
        def _(pool):
            for k in range(R2):
                for j in range(J):
                    pool.dma_start(out[:, k, j, :], t["HB"][0:P, 0:F]).then_inc(scattered[k], 16)

            def scatter(i, r, w, s):
                k = s % R2
                pool.wait_ge(out_copied, r * U + s + 1 + R2)
                pool.nop(nofuse=True)
                for j in range(J):
                    pool.indirect_dma_start(t["scat"][(k * J + j) % COPIES], bass.IndirectOffsetOnAxis(ap=idx[:, k, j:j + 1], axis=0),
                                            out[:, k, j, :], None, compute_op=ALU.add).then_inc(scattered[k], 16)

            def after(turns):
                for k in range(R2):
                    pool.wait_ge(scattered[k], (turns * (U // R2) + 1) * 16 * J)
            pipelined(pool, S, t, [(0, scatter)], after=after)

        @block.scalar
        def _(act):
            act.dma_start(idx_all[:, :], t["IDX"]).then_inc(idx_in, 16)
            act.wait_ge(idx_in, 16)
            act.sem_inc(dst_copied, 1)
            act.sem_inc(msg_copied, R2)
            act.sem_inc(out_copied, R2)

            def copy_dst(i, r, w, s):
                n = r * U + s
                act.wait_ge(dst_spread, n + 1)
                act.wait_ge(lhs_made, n + 1)
                act.activation(dst_sp[:, s % R2, :], ps_dst[:, :], ACT.Copy).then_inc(dst_copied, 1)

            def copy_msg(i, r, w, s):
                n = r * U + s
                act.wait_ge(mixed, n + 1 + R4)
                act.wait_ge(summed, n + 1 + R4 - R2)
                act.activation(msg[:, s % R2, :], ps_msg[s % R2][:, :], ACT.Copy).then_inc(msg_copied, 1)

            def copy_out(i, r, w, s):
                n, k = r * U + s, s % R2
                act.wait_ge(scattered[k], r * (16 * J * (U // R2)) + 16 * J * (s // R2) + 16 * J)
                act.activation(idx[:, k, :], idx_all[:, ds((i * U + s) * J, J)], ACT.Copy)
                act.wait_ge(summed, n + 1 + R4)
                act.activation(out[:, k, :, :].rearrange("p j f -> p (j f)"), ps_sum[k][:, :], ACT.Copy).then_inc(out_copied, 1)
            pipelined(act, S, t, [(2, copy_dst), (1, copy_msg), (0, copy_out)])

        @block.vector
        def _(v):
            link = Link(v, prep)
            link(v.tensor_copy(src_f[:, :], t["src_i"][:, :]), False)
            link(v.tensor_copy(node_i[:, :], t["pcol"][:, :]))
            link(v.tensor_scalar(node_i[:, :], node_i[:, :], 1, None, ALU.arith_shift_right))
            link(v.tensor_copy(node[:, :], node_i[:, :]))
            link(v.tensor_scalar(node_w[:, :], t["win0"][:, :], node[:, 0:1], None, ALU.add))
            v.sem_inc(same_made, 1)
            v.sem_inc(lhs_made, R2)

            def find_same(i, r, w, s):
                n, g = r * U + s, i * U + s
                v.wait_ge(src_spread, n + 1)
                v.wait_ge(summed, n + 1)
                v.tensor_tensor(same[:, s, :, :], ps_src[:, :].rearrange("p (e j) -> p j e", j=J),
                                bcast(src_f[:, ds(g * J, J)], 2, P), ALU.is_equal).then_inc(same_made, 1)

            def make_lhs(i, r, w, s):
                n = r * U + s
                v.wait_ge(dst_copied, n + 2)
                v.wait_ge(spread, n + 1 + R4)
                v.wait_ge(mixed, n + 1 + R4 - R2)
                col = node[:, 0:1] if w is None else node_w[:, ds(w, 1)]
                for q in range(2):
                    make = v.scalar_tensor_tensor(lhs[:, s % R2, q, :], dst_sp[:, s % R2, :], col, ps_c[:, q, :], ALU.is_equal, ALU.mult)
                make.then_inc(lhs_made, 1)
            pipelined(v, S, t, [(0, find_same), (0, make_lhs)])

        @block.tensor
        def _(pe):
            pe.sem_inc(spread, R4)
            pe.sem_inc(mixed, R4)
            pe.sem_inc(summed, R4)

            def spread_rows(i, r, w, s):
                n = r * U + s
                pe.wait_ge(loaded[s], r * 32 + 32)
                pe.wait_ge(same_made, n + 1)
                pe.matmul(ps_src[:, :], t["select"][:, 1, :], rows[:, s, :], start=True, stop=True).then_inc(src_spread, 1)
                pe.wait_ge(dst_copied, n + 1)
                pe.matmul(ps_dst[:, :], t["select"][:, 0, :], rows[:, s, :], start=True, stop=True).then_inc(dst_spread, 1)
                pe.wait_ge(lhs_made, n + 1 + R2 - 1)
                pe.matmul(ps_c[:, 0, :], t["select"][:, 3, :], rows[:, s, :], start=True, stop=True)
                pe.matmul(ps_c[:, 1, :], t["select"][:, 4, :], rows[:, s, :], start=True, stop=True).then_inc(spread, 1)

            def mix(i, r, w, s):
                n = r * U + s
                pe.wait_ge(lhs_made, n + 1 + R2)
                pe.wait_ge(msg_copied, n + 1)
                for j in range(J):
                    for q in range(2):
                        mm = pe.matmul(ps_msg[s % R2][:, j * F:(j + 1) * F], lhs[:, s % R2, q, :].rearrange("p (e j) -> p j e", j=J)[:, j, :],
                                       hb[:, s, q, :], start=(q == 0), stop=(q == 1))
                mm.then_inc(mixed, 1)

            def sum_same(i, r, w, s):
                n = r * U + s
                pe.wait_ge(msg_copied, n + 1 + R2)
                pe.wait_ge(same_made, n + 2)
                pe.wait_ge(out_copied, n + 1)
                for j in range(J):
                    mm = pe.matmul(ps_sum[s % R2][:, j * F:(j + 1) * F], same[:, s, j, :], msg[:, s % R2, j * F:(j + 1) * F],
                                   start=True, stop=True)
                mm.then_inc(summed, 1)
            pipelined(pe, S, t, [(2, spread_rows), (1, mix), (0, sum_same)])


def logit_phase(nc, S, attr, t):
    NGP = S.NGP
    full, rest = S.E // GE, S.E % GE
    CA = 6
    with ExitStack() as c:
        sb = lambda n, s, d=F32: c.enter_context(nc.sbuf_tensor(f"log_{n}", s, d))
        sem = lambda n: c.enter_context(nc.semaphore(f"log_{n}"))
        ps = lambda n, s: c.enter_context(nc.psum_tensor(f"log_{n}", s, F32))
        most = t["big"][0:2, :, :]
        slot = sb("slot", [P, U, J], I32)
        rows = sb("rows", [P, U, J, F])
        at_in, atT = sb("at_in", [P, 2, J * ED]), sb("atT", [P, J * ED])
        xs = sb("xs", [P, 2, J * F])
        weighed, far = sb("weighed", [P, J * F]), sb("far", [P, J, W])
        val = sb("val", [P, 2, 2, J, 2, W])
        top = sb("top", [P, 2, 2])
        ps_at, ps_top = ps("ps_at", [P, 512]), ps("ps_top", [P, 512])
        ps_x = [ps(f"ps_x{k}", [P, 512]) for k in range(2)]
        ps_v = [ps(f"ps_v{k}", [P, 2, 512]) for k in range(2)]
        gathered = [sem(f"gathered{k}") for k in range(U)]
        attr_in, stored = [sem(f"attr_in{k}") for k in range(2)], [sem(f"stored{k}") for k in range(2)]
        pad_in, idx_ready, at_turned, at_copied, projected, x_copied = (
            sem(n) for n in ("pad_in", "idx_ready", "at_turned", "at_copied", "projected", "x_copied"))
        valued, val_turned, topped, top_turned, merged, saved = (
            sem(n) for n in ("valued", "val_turned", "topped", "top_turned", "merged", "saved"))
        block = c.enter_context(nc.Block())

        @block.sync
        def _(sp):
            whole = attr[0:full * GE, :].rearrange("(g p j) d -> g p (j d)", p=P, j=J)

            def turn(i, r, w):
                for s in range(U):
                    n, k = r * U + s, s % 2
                    sp.wait_ge(at_turned, n + 1)
                    if not isinstance(i, int) or i * U + s < full:
                        sp.dma_start(at_in[:, k, :], whole[ds(i * U + s, 1), :, :].rearrange("a p d -> (a p) d")
                                     ).then_inc(attr_in[k], 16)
                    elif i * U + s == full and rest:
                        m = rest // J
                        tail = attr[full * GE:S.E, :].rearrange("(p j) d -> p (j d)", j=J)
                        other = attr[0:(P - m) * J, :].rearrange("(p j) d -> p (j d)", j=J)
                        sp.dma_start(at_in[m:P, k, :], other).then_inc(pad_in, 16)
                        sp.wait_ge(pad_in, (w * 16 + 16) if w is not None else 16)
                        sp.dma_start(at_in[0:m, k, :], tail).then_inc(attr_in[k], 16)
                    else:
                        sp.dma_start(at_in[:, k, :], whole[0]).then_inc(attr_in[k], 16)

            def after(turns):
                sp.wait_ge(merged, turns * U + 2)
                sp.dma_start(t["MX"].rearrange("(a b) n -> a b n", a=2), most).then_inc(saved, 16)
                sp.wait_ge(saved, 16)
            forms(sp, S, t, turn, after, last_apart=True)

        @block.gpsimd
        def _(pool):
            def turn(i, r, w):
                for s in range(U):
                    pool.wait_ge(idx_ready, r * U + s + 1)
                    pool.nop(nofuse=True)
                    for j in range(J):
                        pool.indirect_dma_start(rows[:, s, j, :], None, t["proj"],
                                                bass.IndirectOffsetOnAxis(ap=slot[:, s, j:j + 1], axis=0)
                                                ).then_inc(gathered[s], 16)
            forms(pool, S, t, turn)

        @block.scalar
        def _(act):
            for k in range(2):
                act.dma_start(xs[:, k, :], t["proj"][0:P * J, :].rearrange("(p j) f -> p (j f)", j=J)).then_inc(stored[k], 16)
            act.sem_inc(at_copied, 1)
            act.sem_inc(x_copied, 2)
            edges = t["edges"].rearrange("(g p j) f -> g p (j f)", p=P, j=J)

            def turn(i, r, w):
                for s in range(U):
                    act.wait_ge(projected, r * U + s + 1)
                    act.activation(slot[:, s, :], t["src_i"][:, ds((i * U + s) * J, J)], ACT.Copy).then_inc(idx_ready, 1)
                for s in range(U):
                    n, g, k = r * U + s, i * U + s, s % 2
                    act.wait_ge(at_turned, n + 3)
                    act.wait_ge(projected, n + U)
                    act.activation(atT[:, :], ps_at[:, 0:J * ED], ACT.Copy).then_inc(at_copied, 1)
                    act.wait_ge(projected, n + U + 1)
                    act.wait_ge(stored[k], r * (16 * (U // 2)) + 16 * (s // 2) + 16)
                    act.wait_ge(valued, n * CA + 1)
                    act.activation(xs[:, k, :], ps_x[k][:, :], ACT.Copy).then_inc(x_copied, 1)
                    act.wait_ge(x_copied, n + 3)
                    act.dma_start(edges[ds(g, 1), :, :].rearrange("a p d -> (a p) d"), xs[:, k, :]).then_inc(stored[k], 16)

            def after(turns):
                for k in range(2):
                    act.wait_ge(stored[k], turns * (U // 2) * 16 + 16)
            forms(act, S, t, turn, after)

        @block.tensor
        def _(pe):
            pe.sem_inc(at_turned, 2)
            pe.sem_inc(projected, U)
            pe.sem_inc(val_turned, 2)
            pe.sem_inc(top_turned, 2)

            def turn(i, r, w):
                def project(s):
                    n, k = r * U + s, s % 2
                    pe.wait_ge(attr_in[k], r * (16 * (U // 2)) + 16 * (s // 2) + 16)
                    pe.wait_ge(at_copied, n + 1)
                    for q in range(2):
                        mm = pe.transpose(ps_at[:, q * P:(q + 1) * P], at_in[:, k, q * P:(q + 1) * P], t["ident"][:, :])
                    mm.then_inc(at_turned, 1)
                    pe.wait_ge(x_copied, n + 1)
                    pe.wait_ge(gathered[s], r * (16 * J) + 16 * J)
                    pe.matmul(ps_x[k][:, :], t["ident"][:, :], rows[:, s, :, :].rearrange("p j f -> p (j f)"),
                              start=True, stop=False, skip_group_check=True)
                    pe.wait_ge(at_copied, n + 2)
                    for q in range(2):
                        mm = pe.matmul(ps_x[k][:, q * 2 * F:(q + 1) * 2 * F], atT[:, q * P:(q + 1) * P],
                                       t["edge_wT"][:, :], start=False, stop=(q == 1), skip_group_check=True)
                    mm.then_inc(projected, 1)

                def turn_values(s):
                    n, k = r * U + s, s % 2
                    pe.wait_ge(valued, n * CA + 3 * CA)
                    pe.wait_ge(topped, n + 1)
                    for hp in range(2):
                        for j in range(J):
                            mm = pe.transpose(ps_v[k][:, hp, j * P:(j + 1) * P],
                                              val[:, k, hp, j, :, :].rearrange("p a n -> p (a n)"), t["ident"][:, :])
                    mm.then_inc(val_turned, 1)

                def turn_top(s):
                    n, k = r * U + s, s % 2
                    pe.wait_ge(topped, n + 3)
                    pe.wait_ge(merged, n + 2)
                    pe.transpose(ps_top[0:2, k * P:(k + 1) * P], top[:, k, :], t["ident"][:, :]).then_inc(top_turned, 1)

                for s in range(U + 2):
                    if s < U:
                        project(s)
                    if 1 <= s <= U:
                        turn_values(s - 1)
                    if s >= 2:
                        turn_top(s - 2)
            forms(pe, S, t, turn)

        @block.vector
        def _(v):
            v.memset(most, -BIG).then_inc(merged, 1)
            v.sem_inc(merged, 1)
            v.sem_inc(valued, 2 * CA)
            v.sem_inc(topped, 2)

            def turn(i, r, w):
                def values(s):
                    n, g, k = r * U + s, i * U + s, s % 2
                    link = Link(v, valued, n * CA + 2 * CA)
                    v.wait_ge(x_copied, n + 3)
                    link(v.tensor_tensor(weighed[:, :].rearrange("p (j f) -> p j f", j=J), xs[:, k, :].rearrange("p (j f) -> p j f", j=J),
                                         bcast(t["attn"][:, :], 1, J), ALU.mult))
                    e = t["logits"][:, ds(g * (J * HEADS), J * HEADS)]
                    link(v.tensor_reduce(e, weighed[:, :].rearrange("p (a d) -> p a d", d=HD), AX_X, ALU.add), False)
                    link(one_hot(v, t, far[:, :, :], g, w, ALU.not_equal))
                    link(v.tensor_scalar(far[:, :, :], far[:, :, :], -BIG, None, ALU.mult))
                    v.wait_ge(val_turned, n + 1)
                    for hp in range(2):
                        link(v.tensor_tensor(val[:, k, hp, :, :, :], bcast(far[:, :, :], 2, 2),
                                             bcast(e.rearrange("p (j h) -> p j h", j=J)[:, :, 2 * hp:2 * hp + 2], 3, W),
                                             ALU.add), False)
                    assert link.n == CA

                def tops(s):
                    n, k = r * U + s, s % 2
                    v.wait_ge(val_turned, n + 3)
                    v.wait_ge(top_turned, n + 1)
                    v.tensor_reduce(top[:, k, :], ps_v[k][:, :, :], AX_X, ALU.max).then_inc(topped, 1)

                def merge(s):
                    n, g, k = r * U + s, i * U + s, s % 2
                    at = window_start(v, S, t, g, w)
                    v.wait_ge(top_turned, n + 3)
                    v.wait_ge(merged, n + 2)
                    v.tensor_tensor(most[:, :, ds(at, W)], most[:, :, ds(at, W)],
                                    ps_top[0:2, k * P:(k + 1) * P].rearrange("p (a n) -> p a n", a=2), ALU.max).then_inc(merged, 1)

                for s in range(U + 2):
                    if s < U:
                        values(s)
                    if 1 <= s <= U:
                        tops(s - 1)
                    if s >= 2:
                        merge(s - 2)
            forms(v, S, t, turn)


def attention_phase(nc, S, t):
    H4 = J * HEADS
    with ExitStack() as c:
        sb = lambda n, s, d=F32: c.enter_context(nc.sbuf_tensor(f"att_{n}", s, d))
        sem = lambda n: c.enter_context(nc.semaphore(f"att_{n}"))
        ps = lambda n: [c.enter_context(nc.psum_tensor(f"att_{n}{k}", [P, 512], F32)) for k in range(2)]
        xe, xw = sb("xe", [P, U, J * F]), sb("xw", [P, 2, J * F])
        ex, diff, ex_f = sb("ex", [P, U, H4]), sb("diff", [P, U, H4]), sb("ex_f", [P, U, H4, HD])
        onehot, hotT = sb("onehot", [P, U, J, W]), sb("hotT", [W, 2, J * P])
        most, mostT = sb("most", [HEADS, U, W]), sb("mostT", [W, 2, HEADS])
        ps_hot, ps_most, ps_max, ps_sum = ps("ps_hot"), ps("ps_most"), ps("ps_max"), ps("ps_sum")
        x_in = [sem(f"x_in{k}") for k in range(U)]
        hot_made, hot_turned = sem("hot_made"), sem("hot_turned")
        exped, weighed, summed, maxed = sem("exped"), sem("weighed"), sem("summed"), sem("maxed")
        hot_copied, added = sem("hot_copied"), sem("added")
        differed = sem("differed")
        block = c.enter_context(nc.Block())

        @block.sync
        def _(sp):
            edges = t["edges"].rearrange("(g p j) f -> g p (j f)", p=P, j=J)

            def load(i, r, w, s):
                sp.wait_ge(weighed, r * U + s + 1)
                sp.dma_start(xe[:, s, :], edges[ds(i * U + s, 1), :, :].rearrange("a p d -> (a p) d")).then_inc(x_in[s], 16)
                at = window_start(sp, S, t, i * U + s, w)
                sp.dma_start(most[:, s, :], t["MX"][:, ds(at, W)]).then_inc(x_in[s], 16)
            pipelined(sp, S, t, [(0, load)])

        @block.vector
        def _(v):
            v.memset(t["big"][:, :, :], 0.0).then_inc(added, 1)
            v.sem_inc(added, 1)
            v.sem_inc(weighed, U)
            v.sem_inc(differed, 4)

            def weigh(i, r, w, s):
                n = r * U + s
                v.wait_ge(x_in[s], r * 32 + 32)
                v.wait_ge(exped, n + 1 + U)
                v.wait_ge(summed, n + 1 + U - 2)
                v.tensor_tensor(xw[:, s % 2, :].rearrange("p (a d) -> p a d", d=HD), xe[:, s, :].rearrange("p (a d) -> p a d", d=HD),
                                bcast(ex[:, s, :], 2, HD), ALU.mult).then_inc(weighed, 1)

            def differ(i, r, w, s):
                n = r * U + s
                v.wait_ge(maxed, n + 1 + U)
                v.wait_ge(exped, n + 1)
                v.tensor_tensor(diff[:, s, :], t["logits"][:, ds((i * U + s) * H4, H4)], ps_max[s % 2][:, 0:H4],
                                ALU.subtract).then_inc(differed, 1)
                v.wait_ge(differed, n * 2 + 5)
                v.tensor_scalar(diff[:, s, :], diff[:, s, :], 0.0, None, ALU.min).then_inc(differed, 1)

            def hot(i, r, w, s):
                v.wait_ge(summed, r * U + s + 1)
                one_hot(v, t, onehot[:, s, :, :], i * U + s, w).then_inc(hot_made, 1)

            def add(i, r, w, s):
                n = r * U + s
                at = window_start(v, S, t, i * U + s, w)
                v.wait_ge(summed, n + 1 + U)
                v.wait_ge(added, n + 2)
                both = t["big"][:, :, ds(at, W)]
                v.tensor_tensor(both, both, ps_sum[s % 2][:, 0:2 * W].rearrange("p (a n) -> p a n", a=2), ALU.add).then_inc(added, 1)

            pipelined(v, S, t, [(1, weigh), (2, differ), (4, hot), (0, add)], (hot, differ, weigh, add))

        @block.scalar
        def _(act):
            act.sem_inc(hot_copied, 2)
            act.sem_inc(exped, U)

            def copy_hot(i, r, w, s):
                n, k = r * U + s, s % 2
                act.wait_ge(hot_turned, n + 1)
                act.wait_ge(maxed, n + 1 + U - 2)
                act.activation(mostT[:, k, :], ps_most[k][0:W, 0:HEADS], ACT.Copy)
                act.activation(hotT[:, k, :], ps_hot[k][0:W, :], ACT.Copy).then_inc(hot_copied, 1)

            def exps(i, r, w, s):
                n = r * U + s
                act.wait_ge(differed, n * 2 + 6)
                act.wait_ge(weighed, n + 1)
                act.wait_ge(summed, n + 1)
                act.activation(ex[:, s, :], diff[:, s, :], ACT.Exp)
                act.activation(ex_f[:, s, :, :], bcast(diff[:, s, :], 2, HD), ACT.Exp).then_inc(exped, 1)
            pipelined(act, S, t, [(2, exps), (4, copy_hot)], (copy_hot, exps))

        @block.tensor
        def _(pe):
            pe.sem_inc(summed, U)
            pe.sem_inc(maxed, U)

            def sums(i, r, w, s):
                n = r * U + s
                pe.wait_ge(weighed, n + 1 + U)
                pe.wait_ge(added, n + 1)
                for j in range(J):
                    pe.matmul(ps_sum[s % 2][:, 0:W], xw[:, s % 2, j * F:(j + 1) * F], onehot[:, s, j, :],
                              start=(j == 0), stop=(j == J - 1))
                for j in range(J):
                    mm = pe.matmul(ps_sum[s % 2][:, W:2 * W], ex_f[:, s, j * HEADS:(j + 1) * HEADS, :].rearrange("p a d -> p (a d)"),
                                   onehot[:, s, j, :], start=(j == 0), stop=(j == J - 1))
                mm.then_inc(summed, 1)

            def find_max(i, r, w, s):
                n = r * U + s
                pe.wait_ge(hot_copied, n + 3)
                pe.wait_ge(differed, n * 2 + 1)
                for j in range(J):
                    mm = pe.matmul(ps_max[s % 2][:, j * HEADS:(j + 1) * HEADS], hotT[:, s % 2, j * P:(j + 1) * P], mostT[:, s % 2, :],
                                   start=True, stop=True)
                mm.then_inc(maxed, 1)

            def turn_hot(i, r, w, s):
                n = r * U + s
                pe.wait_ge(x_in[s], r * 32 + 32)
                pe.wait_ge(hot_made, n + 1)
                pe.wait_ge(hot_copied, n + 1)
                pe.nop(nofuse=True)
                pe.transpose(ps_most[s % 2][0:W, 0:HEADS], most[:, s, :], t["ident"][0:HEADS, 0:HEADS])
                for j in range(J):
                    mm = pe.transpose(ps_hot[s % 2][0:W, j * P:(j + 1) * P], onehot[:, s, j, :], t["ident"][:, :])
                mm.then_inc(hot_turned, 1)
            pipelined(pe, S, t, [(0, sums), (3, find_max), (4, turn_hot)], (turn_hot, find_max, sums))


def output_phase(nc, S, t, y):
    NT, TURNS = S.NT, S.NTP // Q
    full, rest = S.N // P, S.N % P
    acc, den = t["big"][:, 0, :], t["big"][:, 1, :]
    with ExitStack() as c:
        sb = lambda n, s, d=F32: c.enter_context(nc.sbuf_tensor(f"out_{n}", s, d))
        sem = lambda n: c.enter_context(nc.semaphore(f"out_{n}"))
        ps = lambda n, s: c.enter_context(nc.psum_tensor(f"out_{n}", s, F32))
        res = sb("res", [P, S.NTP, F])
        h_q, aggs, x_q = sb("h_q", [P, Q, F]), sb("aggs", [P, Q * P]), sb("x_q", [P, Q, F])
        stats = sb("stats", [P, S.NTP, 6])
        mean, var, tmp = (sb(n, [P, S.NTP]) for n in ("mean", "var", "tmp"))
        ps_h, ps_o = ps("ps_h", [P, 512]), ps("ps_o", [P, 512])
        h_in, turned, multiplied, dv = sem("h_in"), sem("turned"), sem("multiplied"), sem("dv")
        dv2, fin, roots, stored = sem("dv2"), sem("fin"), sem("roots"), sem("stored")
        C, C2 = 6 + Q, 7
        block = c.enter_context(nc.Block())

        @block.sync
        def _(sp):
            with sp.Fori(0, TURNS) as i:
                sp.wait_ge(turned, i + 1)
                sp.dma_start(h_q[:, :, :], tiles_of(t["H3"], i * Q, Q)).then_inc(h_in, 16)
            with sp.Fori(0, TURNS) as i:
                sp.wait_ge(dv2, i * C2 + C2)
                sp.dma_start(x_q[:, :, :], tiles_of(t["X3"], i * Q, Q)).then_inc(h_in, 16)
            sp.wait_ge(dv2, TURNS * C2 + C2)
            sp.dma_start(y[0:full * P, :].rearrange("(n p) f -> p n f", p=P), res[:, 0:full, :]).then_inc(stored, 16)
            if rest:
                sp.dma_start(y[full * P:S.N, :], res[0:rest, full, :]).then_inc(stored, 16)
            sp.wait_ge(stored, 16 * (1 + bool(rest)))

        @block.tensor
        def _(pe):
            pe.sem_inc(turned, 1)
            with pe.Fori(0, TURNS) as i:
                pe.wait_ge(h_in, i * 16 + 16)
                pe.wait_ge(dv, i * C + C)
                for k in range(Q):
                    mm = pe.transpose(ps_h[:, k * P:(k + 1) * P], h_q[:, k, :], t["ident"][:, :])
                mm.then_inc(turned, 1)
                pe.wait_ge(dv, i * C + C + 4)
                for k in range(Q):
                    mm = pe.matmul(ps_o[:, k * P:(k + 1) * P], aggs[:, k * P:(k + 1) * P], t["out_wT"][:, :], start=True, stop=True)
                mm.then_inc(multiplied, 1)

        @block.vector
        def _(v):
            v.sem_inc(dv, C)
            with v.Fori(0, TURNS) as i:
                link = Link(v, dv, i * C + C)
                cols = ds(i * (Q * P), Q * P)
                link(v.tensor_scalar(aggs[:, :], den[:, cols], 1.0e-30, None, ALU.max))
                link(v.reciprocal(aggs[:, :], aggs[:, :]))
                link(v.tensor_tensor(aggs[:, :], aggs[:, :], acc[:, cols], ALU.mult))
                v.wait_ge(turned, i + 2)
                link(v.tensor_tensor(aggs[:, :], aggs[:, :], ps_h[:, :], ALU.add))
                v.wait_ge(multiplied, i + 1)
                four = res[:, ds(i * Q, Q), :]
                link(v.tensor_tensor(four, ps_o[:, :].rearrange("p (n f) -> p n f", n=Q), bcast(t["out_b"][:, :], 1, Q), ALU.add))
                link(v.tensor_scalar(four, four, 0.0, None, ALU.max))
                for k in range(Q):
                    link(v.bn_stats(stats[:, ds(i * Q + k, 1), :], res[:, ds(i * Q + k, 1), :]), False)
                assert link.n == C
            v.wait_ge(dv, TURNS * C + C)
            link = Link(v, fin)
            norm_constants(link, v, stats, mean, var, tmp)
            v.sem_inc(roots, 1)
            v.wait_ge(roots, 2)
            link(v.reciprocal(var[:, :], var[:, :]))
            v.sem_inc(dv2, C2)
            with v.Fori(0, TURNS) as i:
                link2 = Link(v, dv2, i * C2 + C2)
                v.wait_ge(h_in, i * 16 + 16 * TURNS + 16)
                normed_sum(v, link2, res, i, mean, var, t["out_gamma"], t["out_beta"], x_q[:, :, :])
                assert link2.n == C2
            v.wait_ge(dv2, TURNS * C2 + C2)

        @block.scalar
        def _(act):
            act.wait_ge(roots, 1)
            act.activation(var[:, :], var[:, :], ACT.Sqrt).then_inc(roots, 1)


NAMES = ["x", "src", "dst", "edge_attr_64", "edge_type_50", "edge_type_9", "L0_gnn_W_msg", "L0_gnn_b_msg",
         "L0_gnn_edge_embed", "L0_gnn_W_ih", "L0_gnn_W_hh", "L0_gnn_b_ih", "L0_gnn_b_hh", "L1_gnn_W", "L1_gnn_b",
         "L1_gnn_gamma", "L1_gnn_beta", "L2_gnn_bases", "L2_gnn_comps", "L2_gnn_alpha", "L3_gnn_W_proj_w",
         "L3_gnn_W_proj_b", "L3_gnn_attn_vec", "L3_gnn_W_out_w", "L3_gnn_W_out_b", "L3_gnn_ln_gamma",
         "L3_gnn_ln_beta"]


def build_program(nc, a, out, kind="Internal"):
    S = Shapes(a["x"].shape[0], a["src"].shape[0])
    dram = lambda n, s, d=F32: nc.dram_tensor(n, s, d, kind=kind).ap()
    t = {
        "T9": dram("T9", (P, S.NGP * J)),
        "IDX": dram("IDX", (P, S.NGP * J), I32),
        "rows": dram("rows", (S.NGP, IDS + 3 * BASES, GE), BF16),
        "scat": [dram(f"scat{k}", (S.NR, F)) for k in range(COPIES)],
        "HB": dram("HB", (S.NR, BASES * F)),
        "MX": dram("MX", (HEADS, S.NR)),
        "proj": dram("proj", (S.NR, F)),
        "edges": dram("edges", (S.NGP * GE, F)),
    }
    for k in range(4):
        t[f"H{k}"] = dram(f"H{k}", (S.NR, F))
        t[f"X{k}"] = dram(f"X{k}", (S.NR, F))
    with ExitStack() as c:
        sb = lambda n, s, d=F32: c.enter_context(nc.sbuf_tensor(n, s, d))
        t["ident"] = sb("ident", [P, P])
        t["iota"] = sb("iota", [P, P])
        t["pcol"] = sb("pcol", [P, 1])
        t["win0"] = sb("win0", [P, S.NWIN])
        t["win_far"] = sb("win_far", [P, S.NWIN])
        t["src_i"] = sb("src_i", [P, S.NGP * J], I32)
        t["dst_rel"] = sb("dst_rel", [P, S.NGP * J])
        t["base"] = sb("base_row", [1, S.NB * P], I32)
        t["wide"] = sb("wide", [1, 1], I32)
        t["deg_src"] = sb("deg_src", [P, S.NT])
        t["dinv_in"] = sb("dinv_in", [P, S.NTP])
        t["dinv_src"] = sb("dinv_src", [P, S.NTP])
        t["relation"] = sb("relation", [P, 3 * BASES], BF16)
        t["select"] = sb("select", [IDS + 3 * BASES, 5, P], BF16)
        for n, w in WEIGHTS.items():
            t[n] = sb(n, [P, w])
        setup_phase(nc, S, a["src"], a["dst"], a["edge_type_9"], a["edge_type_50"], t)
        first_norm_phase(nc, S, a["x"], t)
        with nc.sbuf_tensor("sums_a", [P, 2, S.NR], F32) as t["big"]:
            sum_phase(nc, S, t, "L0", t["H0"], True)
            weights_phase(nc, S, a, t)
            gru_phase(nc, S, t)
            sum_phase(nc, S, t, "L1", t["H1"], False)
            gcn_phase(nc, S, t)
        relation_phase(nc, S, t)
        relation_norm_phase(nc, S, t)
        with nc.sbuf_tensor("sums_b", [P, 2, S.NR], F32) as t["big"]:
            with nc.sbuf_tensor("logits", [P, S.NGP * J * HEADS], F32) as t["logits"]:
                logit_phase(nc, S, a["edge_attr_64"], t)
                attention_phase(nc, S, t)
            output_phase(nc, S, t, out)
    return S, t


def kernel(**inputs):
    import numpy as _np
    import concourse.bacc as _bacc
    from concourse import mybir as _mybir
    from concourse.bass_utils import run_bass_kernel_spmd as _run

    nc = _bacc.Bacc("TRN2", target_bir_lowering=False, num_devices=1)
    arrays, args = {}, {}
    for name in NAMES:
        a = _np.ascontiguousarray(inputs[name])
        arrays[f"in_{name}_dram"] = a
        args[name] = nc.dram_tensor(f"in_{name}_dram", a.shape, _mybir.dt.from_np(a.dtype), kind="ExternalInput").ap()
    out = nc.dram_tensor("out_0_dram", args["x"].shape, F32, kind="ExternalOutput").ap()
    build_program(nc, args, out)
    r = _run(nc, [arrays], core_ids=[0])
    return r.results[0]["out_0_dram"]
```

```python
from contextlib import ExitStack

import concourse.bass as bass
from concourse import mybir

P = 128
F = 128
J = 4
GE = P * J
W = 64
U = 4
Q = 4
COPIES = 8
T9 = 9
T50 = 50
HEADS = 4
HD = F // HEADS
ED = 64
BASES = 4
IDS = 5
EPS = 1e-5
FAR = -1.0e6
BIG = 1.0e30

ALU = mybir.AluOpType
ACT = mybir.ActivationFunctionType
AX_X = mybir.AxisListType.X
F32 = mybir.dt.float32
I32 = mybir.dt.int32
BF16 = mybir.dt.bfloat16
ds = bass.ds


class Link:

    def __init__(self, eng, sem, base=0):
        self.eng, self.sem, self.base, self.n = eng, sem, base, 0

    def __call__(self, ins, wait=True):
        self.n += 1
        ins.then_inc(self.sem, 1)
        if wait:
            self.eng.wait_ge(self.sem, self.base + self.n)


class Shapes:
    def __init__(self, n_nodes, n_edges):
        self.N, self.E = n_nodes, n_edges
        self.NT = -(-n_nodes // P)
        self.NP = self.NT * P
        self.NTP = -(-self.NT // Q) * Q
        self.NR = (self.NTP + 2) * P
        self.NG = -(-n_edges // GE)
        self.NGP = -(-self.NG // U) * U
        self.NB = -(-self.NGP // P)
        self.NWIN = -(-n_nodes // W)


def bcast(ap, axis, n):
    ap = ap.unsqueeze(axis)
    shape = list(ap.shape)
    shape[axis] = n
    return ap.broadcast_to(shape)


def setup_phase(nc, S, src, dst, type9, type50, t):
    NB, NGP = S.NB, S.NGP
    full, rest = S.E // GE, S.E % GE
    with ExitStack() as c:
        sb = lambda n, s, d=F32: c.enter_context(nc.sbuf_tensor(f"setup_{n}", s, d))
        sem = lambda n: c.enter_context(nc.semaphore(n))
        raw = {k: sb(f"raw_{k}", [P, NB, GE], I32) for k in ("src", "dst", "t9", "t50")}
        dst_f = sb("dst_f", [P, NB, GE])
        low = sb("low", [P, NB, GE])
        src_f = sb("src_f", [P, NB, GE])
        t9_f = sb("t9_f", [P, NB, GE])
        whole = sb("whole", [P, NB, GE], I32)
        part = sb("part", [P, NB, GE], I32)
        rows = sb("rows", [P, NB, IDS, GE], BF16)
        dmin = sb("dmin", [P, NB])
        dmax = sb("dmax", [P, NB])
        span = sb("span", [P, NB])
        spanmax = sb("spanmax", [P, 1])
        wide_f = sb("wide_f", [1, 1])
        one_row = sb("one_row", [1, P])
        narrow = sb("narrow", [P, 1])
        base = sb("base", [P, NB])
        below = sb("below", [P, NGP * J])
        cols = sb("cols", [P, NGP * J])
        type9_cols = sb("type9_cols", [P, NGP * J])
        unique = sb("unique", [P, 1])
        ps_small = c.enter_context(nc.psum_tensor("ps_small", [P, 512], F32))
        ps_base = c.enter_context(nc.psum_tensor("ps_base", [P, 512], F32))
        ps_t = [c.enter_context(nc.psum_tensor(f"ps_t{k}", [P, J, P], F32)) for k in range(2)]
        loaded, consts = sem("loaded"), sem("setup_consts")
        step, found, spread = sem("setup_step"), sem("found"), sem("setup_spread")
        turned, taken, stored, rows_made = sem("turned"), sem("taken"), sem("rows_stored"), sem("rows_made")
        block = c.enter_context(nc.Block())

        parts = [(b, min(P, full - b * P)) for b in range(NB) if full > b * P]

        @block.sync
        def _(sp):
            sp.wait_ge(consts, 4)
            for k, a in (("dst", dst), ("src", src), ("t9", type9), ("t50", type50)):
                g = a[0:full * GE].rearrange("(g e) -> g e", e=GE)
                for b, n in parts:
                    sp.dma_start(raw[k][0:n, b, :], g[b * P:b * P + n, :]).then_inc(loaded, 16)
                if rest:
                    q, b = full % P, full // P
                    sp.dma_start(raw[k][q:q + 1, b, 0:rest],
                                 a[full * GE:S.E].rearrange("(g e) -> g e", g=1)).then_inc(loaded, 16)
            sp.wait_ge(rows_made, 5)
            n = 0
            for b in range(NB):
                m = min(P, NGP - b * P)
                sp.dma_start(t["rows"][b * P:b * P + m, 0:IDS, :], rows[0:m, b, :, :]).then_inc(stored, 16)
                n += 16
            sp.wait_ge(taken, 3 * NB)
            sp.dma_start(t["T9"], type9_cols[:, :]).then_inc(stored, 16)
            sp.wait_ge(stored, n + 16)

        @block.gpsimd
        def _(pool):
            pool.memset(raw["dst"][:, :, :], int(FAR)).then_inc(consts, 1)
            for k in ("src", "t9", "t50"):
                pool.memset(raw[k][:, :, :], -1).then_inc(consts, 1)
            pool.memset(t["ident"][:, :], 0.0).then_inc(consts, 1)
            pool.wait_ge(consts, 5)
            pool.affine_select(out=t["ident"][:, :], in_=t["ident"][:, :], compare_op=ALU.not_equal,
                               fill=1.0, base=0, pattern=[[-1, P]], channel_multiplier=1).then_inc(consts, 1)
            pool.iota(t["iota"][:, :], pattern=[[1, P]], base=0, channel_multiplier=0,
                      allow_small_or_imprecise_dtypes=True).then_inc(consts, 1)
            pool.iota(t["pcol"][:, :], pattern=[[0, 1]], base=0, channel_multiplier=1,
                      allow_small_or_imprecise_dtypes=True).then_inc(consts, 1)
            pool.memset(one_row[:, :], 1.0).then_inc(consts, 1)
            pool.iota(t["win0"][:, :], pattern=[[W, S.NWIN]], base=0, channel_multiplier=0,
                      allow_small_or_imprecise_dtypes=True).then_inc(consts, 1)
            pool.iota(t["win_far"][:, :], pattern=[[1024, S.NWIN]], base=0, channel_multiplier=0,
                      allow_small_or_imprecise_dtypes=True).then_inc(consts, 1)

        @block.vector
        def _(v):
            link = Link(v, step)
            v.wait_ge(loaded, 4 * 16 * (len(parts) + (1 if rest else 0)))
            v.wait_ge(consts, 11)
            link(v.tensor_copy(dst_f[:, :, :], raw["dst"][:, :, :]), False)
            link(v.tensor_copy(src_f[:, :, :], raw["src"][:, :, :]), False)
            link(v.tensor_scalar(t9_f[:, :, :], raw["t9"][:, :, :], 0.0, float(T9 - 1), ALU.max, ALU.min))
            link(v.tensor_reduce(dmax[:, :], dst_f[:, :, :], AX_X, ALU.max), False)
            link(v.tensor_scalar(low[:, :, :], dst_f[:, :, :], 0.0, -2.0 * FAR, ALU.is_lt, ALU.mult))
            link(v.tensor_tensor(low[:, :, :], low[:, :, :], dst_f[:, :, :], ALU.add))
            link(v.tensor_reduce(dmin[:, :], low[:, :, :], AX_X, ALU.min))
            link(v.tensor_tensor(span[:, :], dmax[:, :], dmin[:, :], ALU.subtract))
            link(v.tensor_reduce(spanmax[:, :], span[:, :], AX_X, ALU.max))
            v.sem_inc(found, 1)
            v.wait_ge(spread, 1)
            link(v.tensor_reduce(wide_f[:, :], ps_small[0:1, 0:P], AX_X, ALU.max))
            link(v.tensor_scalar(wide_f[:, :], wide_f[:, :], float(W) - 0.5, None, ALU.is_gt))
            link(v.tensor_copy(t["wide"][:, :], wide_f[:, :]))
            v.sem_inc(found, 1)
            v.wait_ge(spread, 2)
            link(v.tensor_scalar(narrow[:, :], ps_small[:, 256:257], -1.0, 1.0, ALU.mult, ALU.add))
            link(v.tensor_scalar(base[:, :], dmin[:, :], float(S.N - 1), narrow[:, 0:1], ALU.min, ALU.mult))
            v.sem_inc(found, 1)
            for b in range(NB):
                link(v.tensor_scalar(dst_f[:, b, :], dst_f[:, b, :], base[:, b:b + 1], None, ALU.subtract))
            v.sem_inc(found, 1)
            v.wait_ge(spread, 3)
            link(v.tensor_copy(t["base"][0:1, 0:NB * P], ps_base[0:1, 0:NB * P]))
            for k, a in ((0, dst_f), (2, src_f)):
                link(v.tensor_copy(whole[:, :, :], a[:, :, :]))
                link(v.tensor_scalar(part[:, :, :], whole[:, :, :], ~(P - 1), None, ALU.bitwise_and))
                v.tensor_copy(rows[:, :, k, :], part[:, :, :]).then_inc(rows_made, 1)
                v.wait_ge(rows_made, k + 1)
                link(v.tensor_scalar(part[:, :, :], whole[:, :, :], P - 1, None, ALU.bitwise_and))
                v.tensor_copy(rows[:, :, k + 1, :], part[:, :, :]).then_inc(rows_made, 1)
                v.wait_ge(rows_made, k + 2)
            v.tensor_scalar(rows[:, :, 4, :], raw["t50"][:, :, :], 0.0, float(T50 - 1),
                            ALU.max, ALU.min).then_inc(rows_made, 1)
            n = 0
            for out in (t["dst_rel"], cols, type9_cols):
                for b in range(NB):
                    m = min(P, NGP - b * P)
                    v.wait_ge(turned, n + 1)
                    v.tensor_copy(out[:, b * P * J:(b * P + m) * J].rearrange("p (q j) -> p j q", j=J),
                                  ps_t[n % 2][:, :, 0:m]).then_inc(taken, 1)
                    n += 1
            v.wait_ge(taken, n)
            link(v.tensor_scalar(unique[:, :], t["pcol"][:, :], float(S.NP + 1), None, ALU.add))
            link(v.tensor_scalar(below[:, :], cols[:, :], 0.0, unique[:, 0:1], ALU.is_lt, ALU.mult))
            link(v.tensor_tensor(t["src_i"][:, :], cols[:, :], below[:, :], ALU.add))

        @block.tensor
        def _(pe):
            pe.wait_ge(consts, 11)
            pe.wait_ge(found, 1)
            pe.transpose(ps_small[0:1, 0:P], spanmax[:, :], t["ident"][:, :]).then_inc(spread, 1)
            pe.wait_ge(found, 2)
            pe.matmul(ps_small[:, 256:257], one_row[:, :], wide_f[:, :], start=True, stop=True).then_inc(spread, 1)
            pe.wait_ge(found, 3)
            for b in range(NB):
                mm = pe.matmul(ps_base[0:1, b * P:(b + 1) * P], base[:, b:b + 1], t["ident"][:, :],
                               start=True, stop=True)
            mm.then_inc(spread, 1)
            pe.wait_ge(found, 4)
            n = 0
            for a in (dst_f, src_f, t9_f):
                for b in range(NB):
                    if n >= 2:
                        pe.wait_ge(taken, n - 1)
                    for j in range(J):
                        mm = pe.transpose(ps_t[n % 2][:, j, :], a[:, b, :].rearrange("q (p j) -> q j p", j=J)[:, j, :],
                                          t["ident"][:, :])
                    mm.then_inc(turned, 1)
                    n += 1


def norm_constants(link, v, stats, mean, var, tmp):
    link(v.tensor_tensor(mean[:, :], stats[:, :, 1], stats[:, :, 4], ALU.add), False)
    link(v.tensor_tensor(tmp[:, :], stats[:, :, 1], stats[:, :, 4], ALU.subtract), False)
    link(v.tensor_tensor(var[:, :], stats[:, :, 2], stats[:, :, 5], ALU.add))
    link(v.tensor_scalar(mean[:, :], mean[:, :], 0.5, None, ALU.mult), False)
    link(v.scalar_tensor_tensor(tmp[:, :], tmp[:, :], 0.25, tmp[:, :], ALU.mult, ALU.mult), False)
    link(v.tensor_scalar(var[:, :], var[:, :], 1.0 / F, EPS, ALU.mult, ALU.add))
    link(v.tensor_tensor(var[:, :], var[:, :], tmp[:, :], ALU.add))


def first_norm_phase(nc, S, x, t):
    NT, N = S.NT, S.N
    full, rest = N // P, N % P
    with ExitStack() as c:
        sb = lambda n, s, d=F32: c.enter_context(nc.sbuf_tensor(n, s, d))
        sem = lambda n: c.enter_context(nc.semaphore(n))
        TR = S.NR // P
        xs = sb("xs", [P, TR, F])
        hs = sb("hs", [P, TR, F])
        stats = sb("n0_stats", [P, NT, 6])
        mean, var, tmp = sb("n0_mean", [P, NT]), sb("n0_var", [P, NT]), sb("n0_tmp", [P, NT])
        cleared, loaded, step = sem("n0_cleared"), sem("n0_loaded"), sem("n0_step")
        stat, roots, normed = sem("n0_stat"), sem("n0_roots"), sem("n0_normed")
        block = c.enter_context(nc.Block())

        @block.sync
        def _(sp):
            sp.wait_ge(cleared, 2)
            sp.dma_start(xs[:, 0:full, :], x[0:full * P, :].rearrange("(n p) f -> p n f", p=P)).then_inc(loaded, 16)
            if rest:
                sp.dma_start(xs[0:rest, full, :], x[full * P:N, :]).then_inc(loaded, 16)
            sp.wait_ge(loaded, 16 * (1 + bool(rest)))
            sp.dma_start(t["X0"].rearrange("(n p) f -> p n f", p=P), xs[:, :, :]).then_inc(loaded, 16)
            sp.wait_ge(normed, NT)
            sp.dma_start(t["H0"].rearrange("(n p) f -> p n f", p=P), hs[:, :, :]).then_inc(loaded, 16)
            sp.wait_ge(loaded, 16 * (3 + bool(rest)))

        @block.vector
        def _(v):
            v.memset(xs[:, full:TR, :], 0.0).then_inc(cleared, 1)
            v.memset(hs[:, NT:TR, :], 0.0).then_inc(cleared, 1)
            v.wait_ge(cleared, 2)
            v.wait_ge(loaded, 16 * (1 + bool(rest)))
            with v.Fori(0, NT) as i:
                v.bn_stats(stats[:, ds(i, 1), :], xs[:, ds(i, 1), :]).then_inc(stat, 1)
            v.wait_ge(stat, NT)
            link = Link(v, step)
            norm_constants(link, v, stats, mean, var, tmp)
            v.sem_inc(roots, 1)
            v.wait_ge(roots, 2)
            link(v.reciprocal(var[:, :], var[:, :]))
            link(v.scalar_tensor_tensor(mean[:, :], mean[:, :], -1.0, var[:, :], ALU.mult, ALU.mult))
            v.sem_inc(roots, 1)

        @block.scalar
        def _(act):
            act.wait_ge(roots, 1)
            act.activation(var[:, :], var[:, :], ACT.Sqrt).then_inc(roots, 1)
            act.wait_ge(roots, 3)
            with act.Fori(0, NT) as i:
                act.activation(hs[:, ds(i, 1), :], xs[:, ds(i, 1), :], ACT.Relu, bias=mean[:, ds(i, 1)],
                               scale=var[:, ds(i, 1)]).then_inc(normed, 1)


def forms(eng, S, t, turn, after=None, last_apart=False):
    turns = S.NGP // U
    in_loop = turns - last_apart
    wide = eng.value_load(t["wide"][0:1, 0:1], min_val=0, max_val=1)

    def run(NW, turn_i):
        if in_loop:
            with eng.Fori(0, in_loop) as i:
                turn_i(i)
        if last_apart:
            turn_i(turns - 1)
        if after is not None:
            after(turns * NW)

    def every_window(i):
        with eng.Fori(0, S.NWIN) as w:
            turn(i, w + i * S.NWIN, w)

    with eng.If(wide > 0):
        run(S.NWIN, every_window)
    with eng.Else():
        run(1, lambda i: turn(i, i, None))


def pipelined(eng, S, t, stages, in_order=None, after=None):
    turns = S.NGP // U
    wide = eng.value_load(t["wide"][0:1, 0:1], min_val=0, max_val=1)

    last = max(1, -(-max(ahead for ahead, _ in stages) // U))
    last = min(last, turns)

    def step(i, s):
        for ahead, stage in stages:
            n = s + ahead
            if not isinstance(i, int) or 0 <= i * U + n < turns * U:
                stage(i + n // U, i + n // U, None, n % U)

    with eng.If(wide > 0):
        with eng.Fori(0, turns) as i:
            with eng.Fori(0, S.NWIN) as w:
                for s in range(U):
                    for stage in in_order or [stage for _, stage in stages]:
                        stage(i, w + i * S.NWIN, w, s)
        if after is not None:
            after(turns * S.NWIN)
    with eng.Else():
        for s in range(-max(ahead for ahead, _ in stages), 0):
            step(0, s)
        if turns > last:
            with eng.Fori(0, turns - last) as i:
                for s in range(U):
                    step(i, s)
        for i in range(turns - last, turns):
            for s in range(U):
                step(i, s)
        if after is not None:
            after(turns)


def window_start(eng, S, t, g, w):
    if w is None:
        return eng.value_load(t["base"][0:1, ds(g, 1)], min_val=0, max_val=S.N - 1)
    return w * W


def one_hot(v, t, out, g, w, op=ALU.is_equal):
    rel = bcast(t["dst_rel"][:, ds(g * J, J)], 2, W)
    window = bcast(t["iota"][:, 0:W], 1, J)
    if w is None:
        return v.tensor_tensor(out, rel, window, op)
    return v.scalar_tensor_tensor(out, rel, t["win0"][:, ds(w, 1)], window, ALU.subtract, op)


def sum_phase(nc, S, t, tag, table, types):
    NGP = S.NGP
    acc, acc9 = t["big"][:, 0, :], t["big"][0:T9, 1, :]
    HI = S.NT
    per = 2 if types else 1
    hots = 4 if types else 1
    with ExitStack() as c:
        sb = lambda n, s, d=F32: c.enter_context(nc.sbuf_tensor(f"{tag}_{n}", s, d))
        sem = lambda n: c.enter_context(nc.semaphore(f"{tag}_{n}"))
        ps = lambda n, s: c.enter_context(nc.psum_tensor(f"{tag}_{n}", s, F32))
        slot = sb("slot", [P, U, J], I32)
        rows = sb("rows", [P, U, J, F])
        onehot = sb("onehot", [P, U, J, W])
        ps_sum = [ps(f"sum{k}", [P, 512]) for k in range(2)]
        idx_ready, multiplied, made, added = sem("idx_ready"), sem("multiplied"), sem("made"), sem("added")
        gathered = [sem(f"gathered{k}") for k in range(U)]
        if types:
            kind = sb("kind", [P, U, J, T9])
            type9 = sb("type9", [P, NGP * J])
            lo_i, hi_i = sb("lo_i", [P, NGP * J], I32), sb("hi_i", [P, NGP * J], I32)
            lo, hi = sb("lo", [P, NGP * J]), sb("hi", [P, NGP * J])
            lo_hot, hi_hot = sb("lo_hot", [P, U, J, P], BF16), sb("hi_hot", [P, U, J, HI], BF16)
            none = sb("none", [P, P], BF16)
            zeros = sb("zeros", [P, S.NR // 4])
            ps_kind = [ps(f"kind{k}", [P, 512]) for k in range(2)]
            ps_hist = ps("hist", [P, 512])
            start, cleared, prep, counts = sem("start"), sem("cleared"), sem("prep"), sem("counts")
        else:
            src_f = sb("src_f", [P, NGP * J])
            before = sb("before", [P, P])
            trash = sb("trash", [P, 1])
            dup, off, idx = sb("dup", [P, NGP * J]), sb("off", [P, NGP * J]), sb("idx", [P, NGP * J], I32)
            id_rows = sb("id_rows", [IDS, 2, GE], BF16)
            type_hot, coef = sb("type_hot", [T50, 2, GE], BF16), sb("coef", [3 * BASES, 2, GE], BF16)
            same, same_b = sb("same", [P, J, P]), sb("same_b", [P, J, P])
            ps_src, ps_type, ps_coef = ps("ps_src", [P, 512]), ps("ps_type", [P, 512]), ps("ps_coef", [P, 512])
            PREP = 12
            idx_out = sem("idx_out")
            consts, prep, spread, hot, coeffed, copied, dv = (
                sem(n) for n in ("consts", "prep", "spread", "hot", "coeffed", "copied", "dv"))
            ids_in, coef_out = [sem(f"ids_in{k}") for k in range(2)], [sem(f"coef_out{k}") for k in range(2)]
        block = c.enter_context(nc.Block())

        if types:
            @block.sync
            def _(sp):
                sp.dma_start(type9[:, :], t["T9"]).then_inc(prep, 16)
                sp.wait_ge(start, 1)
                n = 0
                for k in range(COPIES):
                    flat = t["scat"][k].rearrange("(p n) f -> p (n f)", p=P)
                    for q in range(4):
                        sp.dma_start(flat[:, q * (S.NR // 4):(q + 1) * (S.NR // 4)], zeros[:, :]).then_inc(cleared, 16)
                        n += 16
                sp.wait_ge(cleared, n)
        else:
            @block.sync
            def _(sp):
                def load_ids(i, r, w, s):
                    sp.wait_ge(spread, r * U + s + 1)
                    sp.nop(nofuse=True)
                    sp.dma_start(id_rows[:, s % 2, :], t["rows"][ds(i * U + s, 1), 0:IDS, :].rearrange("a m e -> (a m) e")
                                 ).then_inc(ids_in[s % 2], 16)
                pipelined(sp, S, t, [(0, load_ids)])
                sp.wait_ge(prep, PREP)
                sp.dma_start(t["IDX"], idx[:, :]).then_inc(idx_out, 16)
                sp.wait_ge(idx_out, 16)

        @block.gpsimd
        def _(pool):
            if not types:
                pool.memset(before[:, :], 1.0).then_inc(consts, 1)
                pool.wait_ge(consts, 1)
                pool.affine_select(out=before[:, :], in_=before[:, :], compare_op=ALU.is_gt, fill=0.0, base=0,
                                   pattern=[[-1, P]], channel_multiplier=1).then_inc(consts, 1)

            def gather(i, r, w, s):
                pool.wait_ge(idx_ready, r * U + s + 1)
                pool.nop(nofuse=True)
                for j in range(J):
                    pool.indirect_dma_start(rows[:, s, j, :], None, table,
                                            bass.IndirectOffsetOnAxis(ap=slot[:, s, j:j + 1], axis=0)
                                            ).then_inc(gathered[s], 16)
            pipelined(pool, S, t, [(0, gather)])

        @block.scalar
        def _(act):
            if not types:
                for k in range(2):
                    act.dma_start(coef[:, k, :], t["rows"][0, 0:1, :].broadcast_to([3 * BASES, GE])).then_inc(coef_out[k], 16)

            def give_indices(i, r, w, s):
                act.wait_ge(multiplied, r * U + s + 1)
                act.activation(slot[:, s, :], t["src_i"][:, ds((i * U + s) * J, J)], ACT.Copy).then_inc(idx_ready, 1)

            def store_coefficients(i, r, w, s):
                n, k = r * U + s, s % 2
                act.wait_ge(coeffed, n + 3)
                act.wait_ge(coef_out[k], r * (16 * (U // 2)) + 16 * (s // 2) + 16)
                act.activation(coef[:, k, :], ps_coef[0:3 * BASES, :], ACT.Copy).then_inc(copied, 1)
                act.wait_ge(copied, n + 2)
                act.dma_start(t["rows"][ds(i * U + s, 1), IDS:, :].rearrange("a m e -> (a m) e"), coef[:, k, :]).then_inc(coef_out[k], 16)

            def after(turns):
                for k in range(2):
                    act.wait_ge(coef_out[k], turns * (U // 2) * 16 + 16)
            if types:
                pipelined(act, S, t, [(U, give_indices)])
            else:
                pipelined(act, S, t, [(U, give_indices), (0, store_coefficients)], after=after)

        @block.vector
        def _(v):
            v.memset(acc, 0.0).then_inc(added, 1)
            if types:
                v.memset(acc9, 0.0).then_inc(added, 1)
                v.memset(none[:, :], 0.0).then_inc(counts, 1)
                v.memset(zeros[:, :], 0.0).then_inc(start, 1)
                v.tensor_scalar(hi_i[:, :], t["src_i"][:, :], 7, None, ALU.arith_shift_right).then_inc(prep, 1)
                v.tensor_scalar(lo_i[:, :], t["src_i"][:, :], P - 1, None, ALU.bitwise_and).then_inc(prep, 1)
                v.wait_ge(prep, 18)
                v.tensor_copy(hi[:, :], hi_i[:, :]).then_inc(prep, 1)
                v.tensor_copy(lo[:, :], lo_i[:, :]).then_inc(prep, 1)
                v.wait_ge(prep, 20)
            else:
                prepare = Link(v, prep)
                prepare(v.tensor_copy(src_f[:, :], t["src_i"][:, :]), False)
                prepare(v.tensor_scalar(trash[:, :], t["pcol"][:, :], float(S.NP), None, ALU.add), False)
                M17, id17 = IDS + 3 * BASES, t["ident"][0:IDS + 3 * BASES, :]
                for k in range(2):
                    prepare(v.tensor_tensor(t["select"][:, k, :], id17[:, 2 * k:2 * k + 1].broadcast_to([M17, P]),
                                            id17[:, 2 * k + 1:2 * k + 2].broadcast_to([M17, P]), ALU.add), False)
                prepare(v.tensor_copy(t["select"][:, 2, :], id17[:, 4:5].broadcast_to([M17, P])), False)
                for q in range(2):
                    at = lambda part: bcast(id17[:, IDS + part * BASES + 2 * q:IDS + part * BASES + 2 * q + 2], 1, W)
                    both = t["select"][:, 3 + q, :].rearrange("r (n c) -> r n c", c=2)
                    prepare(v.tensor_tensor(both, at(0), at(1), ALU.add))
                    prepare(v.tensor_tensor(both, both, at(2), ALU.add))
                v.wait_ge(consts, 2)
                v.sem_inc(dv, 3)
            v.sem_inc(added, 2 * per)

            def make_hots(i, r, w, s):
                n, g = r * U + s, i * U + s
                v.wait_ge(multiplied, n + 1)
                one_hot(v, t, onehot[:, s, :, :], g, w).then_inc(made, 1)
                if types:
                    v.tensor_tensor(kind[:, s, :, :], bcast(type9[:, ds(g * J, J)], 2, T9),
                                    bcast(t["iota"][:, 0:T9], 1, J), ALU.is_equal).then_inc(made, 1)
                    rel, io = bcast(lo[:, ds(g * J, J)], 2, P), bcast(t["iota"][:, 0:P], 1, J)
                    if w is None:
                        v.tensor_tensor(lo_hot[:, s, :, :], rel, io, ALU.is_equal).then_inc(made, 1)
                    else:
                        v.scalar_tensor_tensor(lo_hot[:, s, :, :], rel, t["win_far"][:, ds(w, 1)], io,
                                               ALU.add, ALU.is_equal).then_inc(made, 1)
                    v.tensor_tensor(hi_hot[:, s, :, :], bcast(hi[:, ds(g * J, J)], 2, HI),
                                    bcast(t["iota"][:, 0:HI], 1, J), ALU.is_equal).then_inc(made, 1)

            def find_repeats(i, r, w, s):
                n, g = r * U + s, i * U + s
                link = Link(v, dv, n * 3 + 3)
                v.wait_ge(spread, n + 3)
                v.wait_ge(coeffed, n + 1)
                v.tensor_scalar(type_hot[:, s % 2, :], ps_type[0:T50, :], t["pcol"][0:T50, 0:1], None, ALU.is_equal).then_inc(hot, 1)
                link(v.tensor_tensor(same[:, :, :], ps_src[:, :].rearrange("p (e j) -> p j e", j=J),
                                     bcast(src_f[:, ds(g * J, J)], 2, P), ALU.is_equal))
                link(v.tensor_tensor(same_b[:, :, :], same[:, :, :], bcast(before[:, :], 1, J), ALU.mult))
                link(v.tensor_reduce(dup[:, ds(g * J, J)], same_b[:, :, :], AX_X, ALU.add), False)

            def add(i, r, w, s):
                n = r * U + s
                at = window_start(v, S, t, i * U + s, w)
                v.wait_ge(multiplied, n + U + 1)
                v.wait_ge(added, n * per + 3 * per)
                v.tensor_tensor(acc[:, ds(at, W)], acc[:, ds(at, W)], ps_sum[s % 2][:, 0:W], ALU.add).then_inc(added, 1)
                if types:
                    v.tensor_tensor(acc9[:, ds(at, W)], acc9[:, ds(at, W)], ps_kind[s % 2][0:T9, 0:W],
                                    ALU.add).then_inc(added, 1)
            if types:
                pipelined(v, S, t, [(3, make_hots), (0, add)])
            else:
                pipelined(v, S, t, [(3, make_hots), (1, find_repeats), (0, add)],
                          after=lambda turns: v.wait_ge(dv, turns * (3 * U) + 3))
            if not types:
                assert prepare.n == PREP - 3
                prepare(v.tensor_scalar(off[:, :], src_f[:, :], trash[:, 0:1], -1.0, ALU.subtract, ALU.mult))
                prepare(v.scalar_tensor_tensor(off[:, :], dup[:, :], 0.5, off[:, :], ALU.is_gt, ALU.mult))
                prepare(v.tensor_tensor(idx[:, :], off[:, :], src_f[:, :], ALU.add), False)
            if types:
                v.wait_ge(counts, 2)
                v.tensor_copy(t["deg_src"][:, :], ps_hist[:, 0:HI]).then_inc(counts, 1)

        @block.tensor
        def _(pe):
            if types:
                pe.wait_ge(counts, 1)
                pe.matmul(ps_hist[:, 0:HI], none[:, :], none[:, 0:HI], start=True, stop=False, skip_group_check=True)
            else:
                pe.wait_ge(dv, 3)
                pe.sem_inc(spread, 2)
                pe.sem_inc(coeffed, 2)
                pe.sem_inc(copied, 1)
            pe.sem_inc(multiplied, U)

            def spread_ids(i, r, w, s):
                n, k = r * U + s, s % 2
                pe.wait_ge(ids_in[k], r * (16 * (U // 2)) + 16 * (s // 2) + 16)
                pe.wait_ge(dv, n * 3 + 3)
                pe.matmul(ps_type[0:T50, :], t["select"][0:IDS, 2, 0:T50], id_rows[:, k, :], start=True, stop=True)
                pe.matmul(ps_src[:, :], t["select"][0:IDS, 1, :], id_rows[:, k, :], start=True, stop=True).then_inc(spread, 1)

            def find_coefficients(i, r, w, s):
                n = r * U + s
                pe.wait_ge(hot, n + 1)
                pe.wait_ge(copied, n + 1)
                pe.nop(nofuse=True)
                pe.matmul(ps_coef[0:3 * BASES, :], t["relation"][0:T50, :], type_hot[:, s % 2, :], start=True, stop=True).then_inc(coeffed, 1)

            def multiply(i, r, w, s):
                n = r * U + s
                pe.wait_ge(made, n * hots + hots)
                pe.wait_ge(added, n * per + 2 * per)
                pe.wait_ge(gathered[s], r * (16 * J) + 16 * J)
                for j in range(J):
                    mm = pe.matmul(ps_sum[s % 2][:, 0:W], rows[:, s, j, :], onehot[:, s, j, :],
                                   start=(j == 0), stop=(j == J - 1))
                if types:
                    for j in range(J):
                        pe.matmul(ps_kind[s % 2][0:T9, 0:W], kind[:, s, j, :], onehot[:, s, j, :],
                                  start=(j == 0), stop=(j == J - 1))
                    for j in range(J):
                        mm = pe.matmul(ps_hist[:, 0:HI], lo_hot[:, s, j, :], hi_hot[:, s, j, :],
                                       start=False, stop=False, skip_group_check=True)
                mm.then_inc(multiplied, 1)
            if types:
                pipelined(pe, S, t, [(0, multiply)])
            else:
                pipelined(pe, S, t, [(1, spread_ids), (0, find_coefficients), (0, multiply)])
            if types:
                pe.matmul(ps_hist[:, 0:HI], none[:, :], none[:, 0:HI], start=False, stop=True,
                          skip_group_check=True).then_inc(counts, 1)


WEIGHTS = {
    "msg_wT": F, "ih_wT": 3 * F, "hh_wT": 3 * F, "gcn_wT": F, "bases": BASES * F, "node_wT": F, "edge_wT": 2 * F, "out_wT": F,
    "gate_b": 4 * F, "gcn_b": F, "gcn_gamma": F, "gcn_beta": F, "proj_b": F, "attn": F, "out_b": F,
    "out_gamma": F, "out_beta": F, "embed_b": F, "ones": 1,
}


def weights_phase(nc, S, a, t):
    with ExitStack() as c:
        sb = lambda n, s, d=F32: c.enter_context(nc.sbuf_tensor(f"w_{n}", s, d))
        sem = lambda n: c.enter_context(nc.semaphore(f"w_{n}"))
        square = [("L0_gnn_W_msg", 0, "msg_wT", 0), ("L1_gnn_W", 0, "gcn_wT", 0), ("L3_gnn_W_out_w", 0, "out_wT", 0),
                  ("L3_gnn_W_proj_w", 0, "node_wT", 0)]
        square += [("L0_gnn_W_ih", q, "ih_wT", q) for q in range(3)] + [("L0_gnn_W_hh", q, "hh_wT", q) for q in range(3)]
        nat = sb("natural", [P, len(square), F])
        edge_nat = sb("edge_natural", [P, 2, ED])
        bias2 = sb("bias2", [P, 3 * F])
        msg_b = sb("msg_b", [T9, F])
        comps, alpha = sb("comps", [T50, BASES]), sb("alpha", [T50, 1])
        ps = [c.enter_context(nc.psum_tensor(f"w_ps{k}", [P, 512], F32)) for k in range(2)]
        loaded, turned, taken, step = sem("loaded"), sem("turned"), sem("taken"), sem("step")
        block = c.enter_context(nc.Block())
        row = lambda ap, n=P: ap.rearrange("(a f) -> a f", a=1).broadcast_to([n, ap.shape[0]])
        loads = [(nat[:, m, :], a[w][q * P:(q + 1) * P, 0:F]) for m, (w, q, _, _) in enumerate(square)]
        loads += [(edge_nat[:, h, :], a["L3_gnn_W_proj_w"][:, F:F + ED]) for h in range(2)]
        loads += [(t["bases"][:, (b % 2 * 2 + b // 2) * F:(b % 2 * 2 + b // 2 + 1) * F], a["L2_gnn_bases"][b])
                  for b in range(BASES)]
        loads += [(t["gate_b"][:, 0:3 * F], row(a["L0_gnn_b_ih"])), (bias2[:, :], row(a["L0_gnn_b_hh"])),
                  (msg_b[:, :], row(a["L0_gnn_b_msg"], T9)), (t["embed_b"][0:T9, :], a["L0_gnn_edge_embed"]),
                  (comps[:, :], a["L2_gnn_comps"]), (alpha[:, :], a["L2_gnn_alpha"]),
                  (t["gcn_b"][:, :], row(a["L1_gnn_b"])), (t["gcn_gamma"][:, :], row(a["L1_gnn_gamma"])),
                  (t["gcn_beta"][:, :], row(a["L1_gnn_beta"])), (t["proj_b"][:, :], row(a["L3_gnn_W_proj_b"])),
                  (t["attn"][:, :], row(a["L3_gnn_attn_vec"].rearrange("h d -> (h d)"))),
                  (t["out_b"][:, :], row(a["L3_gnn_W_out_b"])), (t["out_gamma"][:, :], row(a["L3_gnn_ln_gamma"])),
                  (t["out_beta"][:, :], row(a["L3_gnn_ln_beta"]))]

        @block.sync
        def _(sp):
            for to, of in loads:
                sp.dma_start(to, of).then_inc(loaded, 16)

        @block.tensor
        def _(pe):
            pe.wait_ge(loaded, 16 * len(loads))
            for m in range(len(square)):
                if m >= 2:
                    pe.wait_ge(taken, m - 1)
                pe.transpose(ps[m % 2][:, 0:P], nat[:, m, :], t["ident"][:, :]).then_inc(turned, 1)
            m = len(square)
            pe.wait_ge(taken, m - 1)
            pe.transpose(ps[m % 2][:, 0:P], edge_nat[:, :, :].rearrange("p h f -> p (h f)"), t["ident"][:, :]).then_inc(turned, 1)

        @block.vector
        def _(v):
            v.wait_ge(loaded, 16 * len(loads))
            link = Link(v, step)
            for m, (_, _, to, q) in enumerate(square):
                v.wait_ge(turned, m + 1)
                v.tensor_copy(t[to][:, q * F:(q + 1) * F], ps[m % 2][:, 0:P]).then_inc(taken, 1)
            link(v.memset(t["edge_wT"][:, :], 0.0))
            m = len(square)
            v.wait_ge(turned, m + 1)
            for h in range(2):
                link(v.tensor_copy(t["edge_wT"][h * ED:(h + 1) * ED, h * F:(h + 1) * F], ps[m % 2][h * ED:(h + 1) * ED, 0:P]), False)
            link(v.tensor_copy(t["gate_b"][:, 3 * F:4 * F], bias2[:, 2 * F:3 * F]), False)
            link(v.tensor_tensor(t["gate_b"][:, 0:2 * F], t["gate_b"][:, 0:2 * F], bias2[:, 0:2 * F], ALU.add), False)
            link(v.tensor_tensor(t["embed_b"][0:T9, :], t["embed_b"][0:T9, :], msg_b[:, :], ALU.add), False)
            link(v.memset(t["ones"][:, :], 1.0), False)
            link(v.tensor_scalar(comps[:, :], comps[:, :], alpha[:, 0:1], None, ALU.mult))
            for k in range(3):
                part = t["relation"][0:T50, k * BASES:(k + 1) * BASES]
                link(v.tensor_copy(part, comps[:, :]))
                if k < 2:
                    link(v.tensor_tensor(comps[:, :], comps[:, :], part, ALU.subtract))


def tiles_of(table, at, n):
    return table.rearrange("(n p) f -> p n f", p=P)[:, ds(at, n), :]


def gru_phase(nc, S, t):
    NT, NR, PAIRS = S.NT, S.NR, S.NTP // 2
    acc, acc9 = t["big"][:, 0, :], t["big"][0:T9, 1, :]
    with ExitStack() as c:
        sb = lambda n, s, d=F32: c.enter_context(nc.sbuf_tensor(f"gru_{n}", s, d))
        sem = lambda n: c.enter_context(nc.semaphore(f"gru_{n}"))
        ps = lambda n, s: c.enter_context(nc.psum_tensor(f"gru_{n}", s, F32))
        res = sb("res", [P, S.NTP, F])
        h_a, h_b, x_b = sb("h_a", [P, 2, F]), sb("h_b", [P, 2, F]), sb("x_b", [P, 2, F])
        aggs, kinds = sb("aggs", [P, 2 * P]), sb("kinds", [T9, 2 * P])
        msgT, hT = sb("msgT", [P, 2 * P]), sb("hT", [P, 2 * P])
        gates, rz, cand, n_out = sb("gates", [P, 2, 4 * F]), sb("rz", [P, 2, 2 * F]), sb("cand", [P, 2, F]), sb("n_out", [P, 2, F])
        stats = sb("stats", [P, S.NTP, 6])
        mean, var, tmp, deg = (sb(n, [P, S.NTP]) for n in ("mean", "var", "tmp", "deg"))
        ps_msg, ps_h, ps_g, ps_deg = ps("ps_msg", [P, 512]), ps("ps_h", [P, 512]), ps("ps_g", [P, 2, 512]), ps("ps_deg", [P, 512])
        h_in, b_in, turned, staged, messaged = sem("h_in"), sem("b_in"), sem("turned"), sem("staged"), sem("messaged")
        copied, gated, gate_free, dv, acted = sem("copied"), sem("gated"), sem("gate_free"), sem("dv"), sem("acted")
        fin, roots, normed, stored = sem("fin"), sem("roots"), sem("normed"), sem("stored")
        C = 9
        block = c.enter_context(nc.Block())

        @block.sync
        def _(sp):
            def ahead(j):
                sp.wait_ge(turned, j + 1)
                sp.dma_start(h_a[:, :, :], tiles_of(t["H0"], j * 2, 2)).then_inc(h_in, 16)
            ahead(0)
            with sp.Fori(0, PAIRS) as i:
                ahead(i + 1)
                sp.wait_ge(dv, i * C + C)
                sp.dma_start(h_b[:, :, :], tiles_of(t["H0"], i * 2, 2)).then_inc(b_in, 16)
                sp.dma_start(x_b[:, :, :], tiles_of(t["X0"], i * 2, 2)).then_inc(b_in, 16)
            sp.wait_ge(dv, PAIRS * C + C)
            sp.dma_start(tiles_of(t["X1"], 0, S.NTP), res[:, :, :]).then_inc(stored, 16)
            sp.wait_ge(normed, NT + 1)
            sp.dma_start(tiles_of(t["H1"], 0, NR // P), acc.rearrange("p (n f) -> p n f", f=F)).then_inc(stored, 16)
            sp.wait_ge(stored, 32)
            sp.wait_ge(h_in, 16 * PAIRS + 16)

        @block.tensor
        def _(pe):
            pe.sem_inc(turned, 1)
            pe.sem_inc(gated, 1)

            def ahead(j):
                pe.wait_ge(h_in, j * 16 + 16)
                pe.wait_ge(copied, j * 2 + 2)
                for k in range(2):
                    mm = pe.transpose(ps_h[:, k * P:(k + 1) * P], h_a[:, k, :], t["ident"][:, :])
                mm.then_inc(turned, 1)
                pe.wait_ge(staged, j * 2 + 2)
                pe.matmul(ps_msg[:, 0:2 * P], t["msg_wT"][:, :], aggs[:, :], start=True, stop=False)
                pe.matmul(ps_msg[:, 0:2 * P], t["embed_b"][0:T9, :], kinds[:, :], start=False, stop=True).then_inc(messaged, 1)
                pe.wait_ge(copied, j * 2 + 4)
                pe.wait_ge(gate_free, j * 2 + 2)
                for k in range(2):
                    m, h = msgT[:, k * P:(k + 1) * P], hT[:, k * P:(k + 1) * P]
                    pe.matmul(ps_g[:, k, 0:2 * F], m, t["ih_wT"][:, 0:2 * F], start=True, stop=False)
                    pe.matmul(ps_g[:, k, 0:2 * F], h, t["hh_wT"][:, 0:2 * F], start=False, stop=True)
                    pe.matmul(ps_g[:, k, 2 * F:3 * F], m, t["ih_wT"][:, 2 * F:3 * F], start=True, stop=True)
                    pe.matmul(ps_g[:, k, 3 * F:4 * F], h, t["hh_wT"][:, 2 * F:3 * F], start=True, stop=True)
                    mm = pe.matmul(ps_deg[:, k:k + 1], kinds[:, k * P:(k + 1) * P], t["ones"][0:T9, :], start=True, stop=True)
                mm.then_inc(gated, 1)
            ahead(0)
            with pe.Fori(0, PAIRS) as i:
                ahead(i + 1)

        @block.scalar
        def _(act):
            act.sem_inc(copied, 2)

            def ahead(j):
                act.wait_ge(gated, j + 1)
                act.activation(aggs[:, :], acc[:, ds(j * (2 * P), 2 * P)], ACT.Copy).then_inc(staged, 1)
                act.activation(kinds[:, :], acc9[:, ds(j * (2 * P), 2 * P)], ACT.Copy).then_inc(staged, 1)
                act.wait_ge(turned, j + 2)
                act.activation(hT[:, :], ps_h[:, 0:2 * P], ACT.Copy).then_inc(copied, 1)
                act.wait_ge(messaged, j + 1)
                act.activation(msgT[:, :], ps_msg[:, 0:2 * P], ACT.Copy).then_inc(copied, 1)
            ahead(0)
            with act.Fori(0, PAIRS) as i:
                ahead(i + 1)
                act.wait_ge(dv, i * C + C + 1)
                act.activation(rz[:, :, :], gates[:, :, 0:2 * F], ACT.Sigmoid).then_inc(acted, 1)
                act.wait_ge(dv, i * C + C + 4)
                act.activation(n_out[:, :, :], cand[:, :, :], ACT.Tanh).then_inc(acted, 1)
            act.wait_ge(roots, 1)
            act.activation(var[:, :], var[:, :], ACT.Sqrt).then_inc(roots, 1)
            act.activation(deg[:, :], deg[:, :], ACT.Sqrt).then_inc(roots, 1)
            act.wait_ge(roots, 4)
            with act.Fori(0, NT) as i:
                act.activation(acc[:, ds(i * F, F)], res[:, ds(i, 1), :], ACT.Relu, bias=mean[:, ds(i, 1)],
                               scale=var[:, ds(i, 1)]).then_inc(normed, 1)

        @block.vector
        def _(v):
            v.sem_inc(gate_free, 2)
            v.sem_inc(dv, C)
            with v.Fori(0, PAIRS) as i:
                link = Link(v, dv, i * C + C)
                v.wait_ge(gated, i + 2)
                link(v.tensor_tensor(gates[:, :, :], ps_g[:, :, :], bcast(t["gate_b"][:, :], 1, 2), ALU.add))
                v.sem_inc(gate_free, 1)
                link(v.tensor_copy(deg[:, ds(i * 2, 2)], ps_deg[:, 0:2]))
                v.sem_inc(gate_free, 1)
                v.wait_ge(acted, i * 2 + 1)
                link(v.tensor_tensor(cand[:, :, :], rz[:, :, 0:F], gates[:, :, 3 * F:4 * F], ALU.mult))
                link(v.tensor_tensor(cand[:, :, :], cand[:, :, :], gates[:, :, 2 * F:3 * F], ALU.add))
                v.wait_ge(acted, i * 2 + 2)
                v.wait_ge(b_in, i * 32 + 32)
                link(v.tensor_tensor(h_b[:, :, :], h_b[:, :, :], n_out[:, :, :], ALU.subtract))
                link(v.tensor_tensor(h_b[:, :, :], h_b[:, :, :], rz[:, :, F:2 * F], ALU.mult))
                link(v.tensor_tensor(h_b[:, :, :], h_b[:, :, :], n_out[:, :, :], ALU.add))
                x1 = res[:, ds(i * 2, 2), :]
                link(v.tensor_tensor(x1, h_b[:, :, :], x_b[:, :, :], ALU.add))
                v.bn_stats(stats[:, ds(i * 2, 1), :], res[:, ds(i * 2, 1), :])
                link(v.bn_stats(stats[:, ds(i * 2 + 1, 1), :], res[:, ds(i * 2 + 1, 1), :]), False)
                assert link.n == C
            v.wait_ge(dv, PAIRS * C + C)
            v.wait_ge(gated, PAIRS + 2)
            link = Link(v, fin)
            norm_constants(link, v, stats, mean, var, tmp)
            link(v.tensor_scalar(deg[:, :], deg[:, :], 1.0, None, ALU.add))
            v.sem_inc(roots, 1)
            v.wait_ge(roots, 3)
            link(v.reciprocal(var[:, :], var[:, :]))
            link(v.reciprocal(t["dinv_in"][:, :], deg[:, :]))
            link(v.tensor_tensor(var[:, :], var[:, :], t["dinv_in"][:, :], ALU.mult))
            link(v.scalar_tensor_tensor(mean[:, :], mean[:, :], -1.0, var[:, :], ALU.mult, ALU.mult))
            v.memset(acc[:, NT * F:NR], 0.0).then_inc(normed, 1)
            v.sem_inc(roots, 1)


def normed_sum(v, link, res, i, mean, var, gamma, beta, x_old):
    for k in range(Q):
        at = i * Q + k
        link(v.tensor_scalar(res[:, ds(at, 1), :], res[:, ds(at, 1), :], mean[:, ds(at, 1)], var[:, ds(at, 1)],
                             ALU.subtract, ALU.mult), k == Q - 1)
    four = res[:, ds(i * Q, Q), :]
    link(v.tensor_tensor(four, four, bcast(gamma[:, :], 1, Q), ALU.mult))
    link(v.tensor_tensor(four, four, bcast(beta[:, :], 1, Q), ALU.add))
    link(v.tensor_tensor(four, four, x_old, ALU.add))


def gcn_phase(nc, S, t):
    NT, TURNS = S.NT, S.NTP // Q
    acc, x_all = t["big"][:, 0, :], t["big"][:, 1, :]
    with ExitStack() as c:
        sb = lambda n, s, d=F32: c.enter_context(nc.sbuf_tensor(f"gcn_{n}", s, d))
        sem = lambda n: c.enter_context(nc.semaphore(f"gcn_{n}"))
        ps = lambda n, s: c.enter_context(nc.psum_tensor(f"gcn_{n}", s, F32))
        res = sb("res", [P, S.NTP, F])
        mean, var, tmp = (sb(n, [P, S.NTP]) for n in ("mean", "var", "tmp"))
        blocks = c.enter_context(ExitStack())
        own = lambda n, s: blocks.enter_context(nc.sbuf_tensor(f"gcn_{n}", s, F32))
        h_q, aggs, placed = own("h_q", [P, Q, F]), own("aggs", [P, Q * P]), sem("placed")
        stats = own("stats", [P, S.NTP, 6])
        ps_h, ps_o = ps("ps_h", [P, 512]), ps("ps_o", [P, 512])
        h_in, pe_done, dv = sem("h_in"), sem("pe_done"), sem("dv")
        dv2, fin, roots = sem("dv2"), sem("fin"), sem("roots")
        C, C2 = 9, 11
        block = blocks.enter_context(nc.Block())

        @block.sync
        def _(sp):
            with sp.Fori(0, TURNS) as i:
                sp.dma_start(res[:, ds(i * Q, Q), :], tiles_of(t["H1"], i * Q, Q)).then_inc(h_in, 16)
                sp.wait_ge(h_in, i * 16 + 16)
                sp.nop(nofuse=True)
            with sp.Fori(0, TURNS) as i:
                sp.dma_start(x_all[:, ds(i * (Q * F), Q * F)].rearrange("p (n f) -> p n f", f=F), tiles_of(t["X1"], i * Q, Q)
                             ).then_inc(h_in, 16)
                sp.wait_ge(h_in, i * 16 + 16 * TURNS + 16)
                sp.nop(nofuse=True)
            sp.wait_ge(dv2, TURNS * C2 + C2)
            sp.dma_start(tiles_of(t["X2"], 0, S.NTP), res[:, :, :]).then_inc(h_in, 16)
            sp.wait_ge(h_in, 16 * (2 * TURNS + 1))

        @block.tensor
        def _(pe):
            pe.sem_inc(pe_done, 2)
            with pe.Fori(0, TURNS) as i:
                pe.wait_ge(placed, i + 1)
                pe.wait_ge(dv, i * C + C)
                for k in range(Q):
                    mm = pe.transpose(ps_h[:, k * P:(k + 1) * P], h_q[:, k, :], t["ident"][:, :])
                mm.then_inc(pe_done, 1)
                pe.wait_ge(dv, i * C + C + 1)
                for k in range(Q):
                    mm = pe.matmul(ps_o[:, k * P:(k + 1) * P], aggs[:, k * P:(k + 1) * P], t["gcn_wT"][:, :],
                                   start=True, stop=True)
                mm.then_inc(pe_done, 1)

        @block.vector
        def _(v):
            v.sem_inc(dv, C)
            with v.Fori(0, TURNS) as i:
                link = Link(v, dv, i * C + C)
                v.wait_ge(pe_done, i * 2 + 3)
                link(v.tensor_tensor(aggs[:, :], ps_h[:, :], acc[:, ds(i * (Q * P), Q * P)], ALU.add))
                v.wait_ge(pe_done, i * 2 + 4)
                for k in range(Q):
                    link(v.scalar_tensor_tensor(res[:, ds(i * Q + k, 1), :].rearrange("p a f -> p (a f)"),
                                                ps_o[:, k * P:(k + 1) * P], t["dinv_in"][:, ds(i * Q + k, 1)],
                                                t["gcn_b"][:, :], ALU.mult, ALU.add), k == Q - 1)
                for k in range(Q):
                    link(v.bn_stats(stats[:, ds(i * Q + k, 1), :], res[:, ds(i * Q + k, 1), :]), False)
                assert link.n == C
            v.wait_ge(dv, TURNS * C + C)
            link = Link(v, fin)
            norm_constants(link, v, stats, mean, var, tmp)
            v.sem_inc(roots, 1)
            v.wait_ge(roots, 2)
            link(v.reciprocal(var[:, :], var[:, :]))
            v.sem_inc(dv2, C2)
            with v.Fori(0, TURNS) as i:
                link2 = Link(v, dv2, i * C2 + C2)
                v.wait_ge(h_in, i * 16 + 16 * TURNS + 16)
                normed_sum(v, link2, res, i, mean, var, t["gcn_gamma"], t["gcn_beta"],
                           x_all[:, ds(i * (Q * F), Q * F)].rearrange("p (n f) -> p n f", f=F))
                for k in range(Q):
                    link2(v.bn_stats(stats[:, ds(i * Q + k, 1), :], res[:, ds(i * Q + k, 1), :]), False)
                assert link2.n == C2
            v.wait_ge(dv2, TURNS * C2 + C2)
            norm_constants(link, v, stats, mean, var, tmp)
            link(v.tensor_scalar(tmp[:, 0:NT], t["deg_src"][:, :], 1.0, None, ALU.max))
            v.sem_inc(roots, 1)
            v.wait_ge(roots, 5)
            link(v.reciprocal(var[:, :], var[:, :]))
            link(v.reciprocal(tmp[:, 0:NT], tmp[:, 0:NT]))
            if S.NTP > NT:
                link(v.memset(t["dinv_src"][:, NT:S.NTP], 0.0))
            link(v.scalar_tensor_tensor(t["dinv_src"][:, 0:NT], t["deg_src"][:, :], 0.5, tmp[:, 0:NT], ALU.is_gt, ALU.mult))
            link(v.tensor_tensor(var[:, :], var[:, :], t["dinv_src"][:, :], ALU.mult))
            link(v.scalar_tensor_tensor(mean[:, :], mean[:, :], -1.0, var[:, :], ALU.mult, ALU.mult))

        @block.scalar
        def _(act):
            with act.Fori(0, TURNS) as i:
                act.wait_ge(pe_done, i * 2 + 1)
                act.wait_ge(h_in, i * 16 + 16)
                act.activation(h_q[:, :, :], res[:, ds(i * Q, Q), :], ACT.Copy).then_inc(placed, 1)
            act.wait_ge(roots, 1)
            act.activation(var[:, :], var[:, :], ACT.Sqrt).then_inc(roots, 1)
            act.wait_ge(roots, 3)
            act.activation(var[:, :], var[:, :], ACT.Sqrt).then_inc(roots, 1)
            act.activation(tmp[:, 0:NT], tmp[:, 0:NT], ACT.Sqrt).then_inc(roots, 1)
        blocks.close()
        product_block(nc, S, t, "mixes", res, mean, var, t["bases"], BASES, None, t["HB"], None)


def product_block(nc, S, t, tag, res, mean, var, weight, M, bias, table, h_table):
    TURNS = S.NTP // Q
    with ExitStack() as c:
        sb = lambda n, s, d=F32: c.enter_context(nc.sbuf_tensor(f"{tag}_{n}", s, d))
        sem = lambda n: c.enter_context(nc.semaphore(f"{tag}_{n}"))
        ps = lambda n, s: c.enter_context(nc.psum_tensor(f"{tag}_{n}", s, F32))
        h_q, hT, prod = sb("h_q", [P, Q, F]), sb("hT", [P, Q * P]), sb("prod", [P, Q, M * F])
        ps_h, ps_b = ps("ps_h", [P, 512]), ps("ps_b", [P, Q, 512])
        made, turned, taken, based, out, saved, free = (
            sem(n) for n in ("made", "turned", "taken", "based", "out", "saved", "free"))
        stores = 1 + (h_table is not None)
        extra = S.NR - S.NTP * P
        pads = c.enter_context(nc.sbuf_tensor(f"{tag}_pads", [P, extra // P, M * F], F32))
        block = c.enter_context(nc.Block())

        @block.sync
        def _(sp):
            sp.wait_ge(taken, 1)
            sp.dma_start(tiles_of(table, S.NTP, extra // P), pads[:, :, :]).then_inc(saved, 16)
            sp.sem_inc(free, 1)
            with sp.Fori(0, TURNS) as i:
                sp.wait_ge(out, i * 2 + 4)
                sp.dma_start(tiles_of(table, i * Q, Q), prod[:, :, :]).then_inc(saved, 16)
                if h_table is not None:
                    sp.wait_ge(made, i * Q + Q)
                    sp.dma_start(tiles_of(h_table, i * Q, Q), h_q[:, :, :]).then_inc(saved, 16)
                sp.wait_ge(saved, i * (16 * stores) + 16 * stores + 16)
                sp.sem_inc(free, 1)

        @block.scalar
        def _(act):
            with act.Fori(0, TURNS) as i:
                act.wait_ge(turned, i + 1)
                if h_table is not None:
                    act.wait_ge(free, i + 1)
                for k in range(Q):
                    at = i * Q + k
                    act.activation(h_q[:, k, :], res[:, ds(at, 1), :].rearrange("p a f -> p (a f)"), ACT.Relu,
                                   bias=mean[:, ds(at, 1)], scale=var[:, ds(at, 1)]).then_inc(made, 1)
                if bias is None:
                    act.wait_ge(based, i + 1)
                    act.wait_ge(free, i + 1)
                    for k in range(Q // 2, Q):
                        cp = act.activation(prod[:, k, :], ps_b[:, k, 0:M * F], ACT.Copy)
                    cp.then_inc(out, 1)

        @block.tensor
        def _(pe):
            pe.sem_inc(turned, 1)
            with pe.Fori(0, TURNS) as i:
                pe.wait_ge(made, i * Q + Q)
                pe.wait_ge(taken, i + 1)
                for k in range(Q):
                    mm = pe.transpose(ps_h[:, k * P:(k + 1) * P], h_q[:, k, :], t["ident"][:, :])
                mm.then_inc(turned, 1)
                pe.wait_ge(taken, i + 2)
                pe.wait_ge(out, i * 2 + 2)
                for k in range(Q):
                    mm = pe.matmul(ps_b[:, k, 0:M * F], hT[:, k * P:(k + 1) * P], weight[:, :], start=True, stop=True)
                mm.then_inc(based, 1)

        @block.vector
        def _(v):
            v.memset(pads[:, :, :], 0.0).then_inc(taken, 1)
            v.sem_inc(out, 2)
            with v.Fori(0, TURNS) as i:
                v.wait_ge(turned, i + 2)
                v.tensor_copy(hT[:, :], ps_h[:, :]).then_inc(taken, 1)
                v.wait_ge(based, i + 1)
                v.wait_ge(free, i + 1)
                if bias is None:
                    for k in range(Q // 2):
                        cp = v.tensor_copy(prod[:, k, :], ps_b[:, k, 0:M * F])
                    cp.then_inc(out, 1)
                else:
                    v.tensor_tensor(prod[:, 0:2, :], ps_b[:, 0:2, 0:F], bcast(bias[:, :], 1, 2), ALU.add).then_inc(out, 1)
                    v.tensor_tensor(prod[:, 2:4, :], ps_b[:, 2:4, 0:F], bcast(bias[:, :], 1, 2), ALU.add).then_inc(out, 1)


def relation_norm_phase(nc, S, t):
    TURNS = S.NTP // Q
    with ExitStack() as c:
        sb = lambda n, s, d=F32: c.enter_context(nc.sbuf_tensor(f"rel_{n}", s, d))
        sem = lambda n: c.enter_context(nc.semaphore(f"rel_{n}"))
        res = sb("res", [P, S.NTP, F])
        mean, var, tmp = (sb(n, [P, S.NTP]) for n in ("mean", "var", "tmp"))
        blocks = c.enter_context(ExitStack())
        own = lambda n, s: blocks.enter_context(nc.sbuf_tensor(f"rel_{n}", s, F32))
        parts = own("parts", [P, 2, COPIES, 2 * F])
        x_q = own("x_q", [P, Q, F])
        total = own("total", [P, Q, F])
        stats = own("stats", [P, S.NTP, 6])
        part_in = [sem(f"part_in{k}") for k in range(2)]
        x_in, dv, fin, roots = sem("x_in"), sem("dv"), sem("fin"), sem("roots")
        C = 2 + 2 * Q
        block = blocks.enter_context(nc.Block())

        @block.sync
        def _(sp):
            with sp.Fori(0, TURNS) as i:
                for k in range(2):
                    sp.wait_ge(dv, i * C + 1 + k)
                    for q in range(COPIES):
                        sp.dma_start(parts[:, k, q, :].rearrange("p (n f) -> p n f", n=2),
                                     tiles_of(t["scat"][q], i * Q + 2 * k, 2)).then_inc(part_in[k], 16)
                    if k == 0:
                        sp.wait_ge(dv, i * C + C)
                        sp.dma_start(x_q[:, :, :], tiles_of(t["X2"], i * Q, Q)).then_inc(x_in, 16)
            sp.wait_ge(dv, TURNS * C + C)
            sp.dma_start(tiles_of(t["X3"], 0, S.NTP), res[:, :, :]).then_inc(x_in, 16)
            sp.wait_ge(x_in, 16 * (TURNS + 1))

        @block.vector
        def _(v):
            v.sem_inc(dv, C)
            with v.Fori(0, TURNS) as i:
                link = Link(v, dv, i * C + C)
                for k in range(2):
                    v.wait_ge(part_in[k], i * (16 * COPIES) + 16 * COPIES)
                    link(v.tensor_reduce(total[:, 2 * k:2 * k + 2, :].rearrange("p n f -> p (n f)"),
                                         parts[:, k, :, :].rearrange("p c f -> p f c"), AX_X, ALU.add), k == 1)
                v.wait_ge(x_in, i * 16 + 16)
                for k in range(Q):
                    link(v.scalar_tensor_tensor(res[:, ds(i * Q + k, 1), :].rearrange("p a f -> p (a f)"), total[:, k, :],
                                                t["dinv_src"][:, ds(i * Q + k, 1)], x_q[:, k, :], ALU.mult, ALU.add), k == Q - 1)
                for k in range(Q):
                    link(v.bn_stats(stats[:, ds(i * Q + k, 1), :], res[:, ds(i * Q + k, 1), :]), False)
                assert link.n == C
            v.wait_ge(dv, TURNS * C + C)
            link = Link(v, fin)
            norm_constants(link, v, stats, mean, var, tmp)
            v.sem_inc(roots, 1)
            v.wait_ge(roots, 2)
            link(v.reciprocal(var[:, :], var[:, :]))
            link(v.scalar_tensor_tensor(mean[:, :], mean[:, :], -1.0, var[:, :], ALU.mult, ALU.mult))

        @block.scalar
        def _(act):
            act.wait_ge(roots, 1)
            act.activation(var[:, :], var[:, :], ACT.Sqrt).then_inc(roots, 1)
        blocks.close()
        product_block(nc, S, t, "proj", res, mean, var, t["node_wT"], 1, t["proj_b"], t["proj"], t["H3"])


def relation_phase(nc, S, t):
    NGP, R2, R4 = S.NGP, 2, 4
    ROWS = IDS + 3 * BASES
    with ExitStack() as c:
        sb = lambda n, s, d=F32: c.enter_context(nc.sbuf_tensor(f"msg_{n}", s, d))
        sem = lambda n: c.enter_context(nc.semaphore(f"msg_{n}"))
        ps = lambda n, s: c.enter_context(nc.psum_tensor(f"msg_{n}", s, F32))
        src_f = sb("src_f", [P, NGP * J])
        rows = sb("rows", [ROWS, R4, GE], BF16)
        hb = sb("hb", [P, R4, 2, F])
        node = sb("node", [P, 1])
        node_i = sb("node_i", [P, 1], I32)
        node_w = sb("node_w", [P, S.NWIN])
        dst_sp = sb("dst_sp", [P, R2, GE])
        lhs = sb("lhs", [P, R2, 2, GE])
        same = sb("same", [P, R4, J, P])
        msg = sb("msg", [P, R2, GE])
        out = sb("out", [P, R2, J, F])
        idx, idx_all = sb("idx", [P, R2, J], I32), sb("idx_all", [P, NGP * J], I32)
        ps_dst, ps_src, ps_c = ps("ps_dst", [P, 512]), ps("ps_src", [P, 512]), ps("ps_c", [P, 2, 512])
        ps_msg, ps_sum = [ps(f"ps_msg{k}", [P, 512]) for k in range(R2)], [ps(f"ps_sum{k}", [P, 512]) for k in range(R2)]
        loaded = [sem(f"loaded{k}") for k in range(R4)]
        scattered = [sem(f"scattered{k}") for k in range(R2)]
        src_spread, dst_spread, prep, idx_in = sem("src_spread"), sem("dst_spread"), sem("prep"), sem("idx_in")
        spread, mixed, summed = sem("spread"), sem("mixed"), sem("summed")
        same_made, dst_copied = sem("same_made"), sem("dst_copied")
        lhs_made, msg_copied, out_copied = sem("lhs_made"), sem("msg_copied"), sem("out_copied")
        block = c.enter_context(nc.Block())

        @block.sync
        def _(sp):
            def load(i, r, w, s):
                n, g = r * U + s, i * U + s
                sp.wait_ge(spread, n + 1)
                sp.dma_start(rows[:, s, :], t["rows"][ds(g, 1), :, :].rearrange("a m e -> (a m) e")).then_inc(loaded[s], 16)
                at = window_start(sp, S, t, g, w)
                sp.wait_ge(mixed, n + 1)
                sp.dma_start(hb[:, s, :, :].rearrange("p q f -> p (q f)"),
                             t["HB"][ds(at, W), :].rearrange("n (c f) -> (n c) f", c=2)).then_inc(loaded[s], 16)
            pipelined(sp, S, t, [(0, load)])

        @block.gpsimd
        def _(pool):
            for k in range(R2):
                for j in range(J):
                    pool.dma_start(out[:, k, j, :], t["HB"][0:P, 0:F]).then_inc(scattered[k], 16)

            def scatter(i, r, w, s):
                k = s % R2
                pool.wait_ge(out_copied, r * U + s + 1 + R2)
                pool.nop(nofuse=True)
                for j in range(J):
                    pool.indirect_dma_start(t["scat"][(k * J + j) % COPIES], bass.IndirectOffsetOnAxis(ap=idx[:, k, j:j + 1], axis=0),
                                            out[:, k, j, :], None, compute_op=ALU.add).then_inc(scattered[k], 16)

            def after(turns):
                for k in range(R2):
                    pool.wait_ge(scattered[k], (turns * (U // R2) + 1) * 16 * J)
            pipelined(pool, S, t, [(0, scatter)], after=after)

        @block.scalar
        def _(act):
            act.dma_start(idx_all[:, :], t["IDX"]).then_inc(idx_in, 16)
            act.wait_ge(idx_in, 16)
            act.sem_inc(dst_copied, 1)
            act.sem_inc(msg_copied, R2)
            act.sem_inc(out_copied, R2)

            def copy_dst(i, r, w, s):
                n = r * U + s
                act.wait_ge(dst_spread, n + 1)
                act.wait_ge(lhs_made, n + 1)
                act.activation(dst_sp[:, s % R2, :], ps_dst[:, :], ACT.Copy).then_inc(dst_copied, 1)

            def copy_msg(i, r, w, s):
                n = r * U + s
                act.wait_ge(mixed, n + 1 + R4)
                act.wait_ge(summed, n + 1 + R4 - R2)
                act.activation(msg[:, s % R2, :], ps_msg[s % R2][:, :], ACT.Copy).then_inc(msg_copied, 1)

            def copy_out(i, r, w, s):
                n, k = r * U + s, s % R2
                act.wait_ge(scattered[k], r * (16 * J * (U // R2)) + 16 * J * (s // R2) + 16 * J)
                act.activation(idx[:, k, :], idx_all[:, ds((i * U + s) * J, J)], ACT.Copy)
                act.wait_ge(summed, n + 1 + R4)
                act.activation(out[:, k, :, :].rearrange("p j f -> p (j f)"), ps_sum[k][:, :], ACT.Copy).then_inc(out_copied, 1)
            pipelined(act, S, t, [(2, copy_dst), (1, copy_msg), (0, copy_out)])

        @block.vector
        def _(v):
            link = Link(v, prep)
            link(v.tensor_copy(src_f[:, :], t["src_i"][:, :]), False)
            link(v.tensor_copy(node_i[:, :], t["pcol"][:, :]))
            link(v.tensor_scalar(node_i[:, :], node_i[:, :], 1, None, ALU.arith_shift_right))
            link(v.tensor_copy(node[:, :], node_i[:, :]))
            link(v.tensor_scalar(node_w[:, :], t["win0"][:, :], node[:, 0:1], None, ALU.add))
            v.sem_inc(same_made, 1)
            v.sem_inc(lhs_made, R2)

            def find_same(i, r, w, s):
                n, g = r * U + s, i * U + s
                v.wait_ge(src_spread, n + 1)
                v.wait_ge(summed, n + 1)
                v.tensor_tensor(same[:, s, :, :], ps_src[:, :].rearrange("p (e j) -> p j e", j=J),
                                bcast(src_f[:, ds(g * J, J)], 2, P), ALU.is_equal).then_inc(same_made, 1)

            def make_lhs(i, r, w, s):
                n = r * U + s
                v.wait_ge(dst_copied, n + 2)
                v.wait_ge(spread, n + 1 + R4)
                v.wait_ge(mixed, n + 1 + R4 - R2)
                col = node[:, 0:1] if w is None else node_w[:, ds(w, 1)]
                for q in range(2):
                    make = v.scalar_tensor_tensor(lhs[:, s % R2, q, :], dst_sp[:, s % R2, :], col, ps_c[:, q, :], ALU.is_equal, ALU.mult)
                make.then_inc(lhs_made, 1)
            pipelined(v, S, t, [(0, find_same), (0, make_lhs)])

        @block.tensor
        def _(pe):
            pe.sem_inc(spread, R4)
            pe.sem_inc(mixed, R4)
            pe.sem_inc(summed, R4)

            def spread_rows(i, r, w, s):
                n = r * U + s
                pe.wait_ge(loaded[s], r * 32 + 32)
                pe.wait_ge(same_made, n + 1)
                pe.matmul(ps_src[:, :], t["select"][:, 1, :], rows[:, s, :], start=True, stop=True).then_inc(src_spread, 1)
                pe.wait_ge(dst_copied, n + 1)
                pe.matmul(ps_dst[:, :], t["select"][:, 0, :], rows[:, s, :], start=True, stop=True).then_inc(dst_spread, 1)
                pe.wait_ge(lhs_made, n + 1 + R2 - 1)
                pe.matmul(ps_c[:, 0, :], t["select"][:, 3, :], rows[:, s, :], start=True, stop=True)
                pe.matmul(ps_c[:, 1, :], t["select"][:, 4, :], rows[:, s, :], start=True, stop=True).then_inc(spread, 1)

            def mix(i, r, w, s):
                n = r * U + s
                pe.wait_ge(lhs_made, n + 1 + R2)
                pe.wait_ge(msg_copied, n + 1)
                for j in range(J):
                    for q in range(2):
                        mm = pe.matmul(ps_msg[s % R2][:, j * F:(j + 1) * F], lhs[:, s % R2, q, :].rearrange("p (e j) -> p j e", j=J)[:, j, :],
                                       hb[:, s, q, :], start=(q == 0), stop=(q == 1))
                mm.then_inc(mixed, 1)

            def sum_same(i, r, w, s):
                n = r * U + s
                pe.wait_ge(msg_copied, n + 1 + R2)
                pe.wait_ge(same_made, n + 2)
                pe.wait_ge(out_copied, n + 1)
                for j in range(J):
                    mm = pe.matmul(ps_sum[s % R2][:, j * F:(j + 1) * F], same[:, s, j, :], msg[:, s % R2, j * F:(j + 1) * F],
                                   start=True, stop=True)
                mm.then_inc(summed, 1)
            pipelined(pe, S, t, [(2, spread_rows), (1, mix), (0, sum_same)])


def logit_phase(nc, S, attr, t):
    full, rest = S.E // GE, S.E % GE
    CA = 7
    with ExitStack() as c:
        sb = lambda n, s, d=F32: c.enter_context(nc.sbuf_tensor(f"log_{n}", s, d))
        sem = lambda n: c.enter_context(nc.semaphore(f"log_{n}"))
        ps = lambda n, s: c.enter_context(nc.psum_tensor(f"log_{n}", s, F32))
        most = t["big"][0:2, :, :]
        slot = sb("slot", [P, U, J], I32)
        rows = sb("rows", [P, U, J, F])
        at_in, atT = sb("at_in", [P, 2, J * ED]), sb("atT", [P, J * ED])
        xs = sb("xs", [P, 2, J * F])
        weighed, far = sb("weighed", [P, J * F]), sb("far", [P, J, W])
        val = sb("val", [P, 2, 2, J, 2, W])
        top = sb("top", [P, 2, 2])
        ps_at, ps_top = ps("ps_at", [P, 512]), ps("ps_top", [P, 512])
        ps_x = [ps(f"ps_x{k}", [P, 512]) for k in range(2)]
        ps_v = [ps(f"ps_v{k}", [P, 2, 512]) for k in range(2)]
        gathered = [sem(f"gathered{k}") for k in range(U)]
        attr_in, stored = [sem(f"attr_in{k}") for k in range(2)], [sem(f"stored{k}") for k in range(2)]
        pad_in, idx_ready, at_turned, at_copied, projected, x_copied = (
            sem(n) for n in ("pad_in", "idx_ready", "at_turned", "at_copied", "projected", "x_copied"))
        valued, val_turned, topped, top_turned, merged, saved = (
            sem(n) for n in ("valued", "val_turned", "topped", "top_turned", "merged", "saved"))
        block = c.enter_context(nc.Block())

        @block.sync
        def _(sp):
            whole = attr[0:full * GE, :].rearrange("(g p j) d -> g p (j d)", p=P, j=J)

            def turn(i, r, w):
                for s in range(U):
                    n, k = r * U + s, s % 2
                    sp.wait_ge(at_turned, n + 1)
                    if not isinstance(i, int) or i * U + s < full:
                        sp.dma_start(at_in[:, k, :], whole[ds(i * U + s, 1), :, :].rearrange("a p d -> (a p) d")
                                     ).then_inc(attr_in[k], 16)
                    elif i * U + s == full and rest:
                        m = rest // J
                        tail = attr[full * GE:S.E, :].rearrange("(p j) d -> p (j d)", j=J)
                        other = attr[0:(P - m) * J, :].rearrange("(p j) d -> p (j d)", j=J)
                        sp.dma_start(at_in[m:P, k, :], other).then_inc(pad_in, 16)
                        sp.wait_ge(pad_in, (w * 16 + 16) if w is not None else 16)
                        sp.dma_start(at_in[0:m, k, :], tail).then_inc(attr_in[k], 16)
                    else:
                        sp.dma_start(at_in[:, k, :], whole[0]).then_inc(attr_in[k], 16)

            def after(turns):
                sp.wait_ge(merged, turns * U + 2)
                sp.dma_start(t["MX"].rearrange("(a b) n -> a b n", a=2), most).then_inc(saved, 16)
                sp.wait_ge(saved, 16)
            forms(sp, S, t, turn, after, last_apart=True)

        @block.gpsimd
        def _(pool):
            def gather(i, r, w, s):
                pool.wait_ge(idx_ready, r * U + s + 1)
                pool.nop(nofuse=True)
                for j in range(J):
                    pool.indirect_dma_start(rows[:, s, j, :], None, t["proj"],
                                            bass.IndirectOffsetOnAxis(ap=slot[:, s, j:j + 1], axis=0)
                                            ).then_inc(gathered[s], 16)
            pipelined(pool, S, t, [(0, gather)])

        @block.scalar
        def _(act):
            for k in range(2):
                act.dma_start(xs[:, k, :], t["proj"][0:P * J, :].rearrange("(p j) f -> p (j f)", j=J)).then_inc(stored[k], 16)
            act.sem_inc(at_copied, 1)
            act.sem_inc(x_copied, 2)
            edges = t["edges"].rearrange("(g p j) f -> g p (j f)", p=P, j=J)

            def give_indices(i, r, w, s):
                act.wait_ge(projected, r * U + s + 1)
                act.activation(slot[:, s, :], t["src_i"][:, ds((i * U + s) * J, J)], ACT.Copy).then_inc(idx_ready, 1)

            def copy_attributes(i, r, w, s):
                n = r * U + s
                act.wait_ge(at_turned, n + 3)
                act.wait_ge(projected, n + U)
                act.activation(atT[:, :], ps_at[:, 0:J * ED], ACT.Copy).then_inc(at_copied, 1)

            def store_x(i, r, w, s):
                n, g, k = r * U + s, i * U + s, s % 2
                act.wait_ge(projected, n + U + 1)
                act.wait_ge(stored[k], r * (16 * (U // 2)) + 16 * (s // 2) + 16)
                act.wait_ge(valued, n * CA + 1)
                act.activation(xs[:, k, :], ps_x[k][:, :], ACT.Copy).then_inc(x_copied, 1)
                act.wait_ge(x_copied, n + 3)
                act.dma_start(edges[ds(g, 1), :, :].rearrange("a p d -> (a p) d"), xs[:, k, :]).then_inc(stored[k], 16)

            def after(turns):
                for k in range(2):
                    act.wait_ge(stored[k], turns * (U // 2) * 16 + 16)
            pipelined(act, S, t, [(3, store_x), (4, copy_attributes), (3 + U, give_indices)],
                      (give_indices, copy_attributes, store_x), after)

        @block.tensor
        def _(pe):
            pe.sem_inc(at_turned, 2)
            pe.sem_inc(projected, U)
            pe.sem_inc(val_turned, 2)
            pe.sem_inc(top_turned, 2)

            def turn_attributes(i, r, w, s):
                n, k = r * U + s, s % 2
                pe.wait_ge(attr_in[k], r * (16 * (U // 2)) + 16 * (s // 2) + 16)
                pe.wait_ge(at_copied, n + 1)
                for q in range(2):
                    mm = pe.transpose(ps_at[:, q * P:(q + 1) * P], at_in[:, k, q * P:(q + 1) * P], t["ident"][:, :])
                mm.then_inc(at_turned, 1)

            def project(i, r, w, s):
                n, k = r * U + s, s % 2
                pe.wait_ge(x_copied, n + 1)
                pe.wait_ge(gathered[s], r * (16 * J) + 16 * J)
                pe.matmul(ps_x[k][:, :], t["ident"][:, :], rows[:, s, :, :].rearrange("p j f -> p (j f)"),
                          start=True, stop=False, skip_group_check=True)
                pe.wait_ge(at_copied, n + 2)
                for q in range(2):
                    mm = pe.matmul(ps_x[k][:, q * 2 * F:(q + 1) * 2 * F], atT[:, q * P:(q + 1) * P],
                                   t["edge_wT"][:, :], start=False, stop=(q == 1), skip_group_check=True)
                mm.then_inc(projected, 1)

            def turn_values(i, r, w, s):
                n, k = r * U + s, s % 2
                pe.wait_ge(valued, n * CA + 3 * CA)
                pe.wait_ge(topped, n + 1)
                for hp in range(2):
                    for j in range(J):
                        mm = pe.transpose(ps_v[k][:, hp, j * P:(j + 1) * P],
                                          val[:, k, hp, j, :, :].rearrange("p a n -> p (a n)"), t["ident"][:, :])
                mm.then_inc(val_turned, 1)

            def turn_top(i, r, w, s):
                n, k = r * U + s, s % 2
                pe.wait_ge(topped, n + 3)
                pe.wait_ge(merged, n + 2)
                pe.transpose(ps_top[0:2, k * P:(k + 1) * P], top[:, k, :], t["ident"][:, :]).then_inc(top_turned, 1)
            pipelined(pe, S, t, [(0, turn_top), (1, turn_values), (3, project), (4, turn_attributes)],
                      (turn_attributes, project, turn_values, turn_top))

        @block.vector
        def _(v):
            v.memset(most, -BIG).then_inc(merged, 1)
            v.sem_inc(merged, 1)
            v.sem_inc(valued, 2 * CA)
            v.sem_inc(topped, 2)

            def values(i, r, w, s):
                n, g, k = r * U + s, i * U + s, s % 2
                link = Link(v, valued, n * CA + 2 * CA)
                v.wait_ge(x_copied, n + 3)
                link(v.tensor_tensor(weighed[:, :].rearrange("p (j f) -> p j f", j=J), xs[:, k, :].rearrange("p (j f) -> p j f", j=J),
                                     bcast(t["attn"][:, :], 1, J), ALU.mult), False)
                v.wait_ge(valued, n * CA + 2 * CA)
                link(one_hot(v, t, far[:, :, :], g, w, ALU.not_equal))
                e = t["logits"][:, ds(g * (J * HEADS), J * HEADS)]
                link(v.tensor_reduce(e, weighed[:, :].rearrange("p (a d) -> p a d", d=HD), AX_X, ALU.add))
                v.wait_ge(val_turned, n + 1)
                for h in range(HEADS):
                    link(v.scalar_tensor_tensor(val[:, k, h // 2, :, h % 2, :], far[:, :, :], -BIG,
                                                bcast(e.rearrange("p (j h) -> p j h", j=J)[:, :, h], 2, W),
                                                ALU.mult, ALU.add), False)
                assert link.n == CA

            def tops(i, r, w, s):
                n, k = r * U + s, s % 2
                v.wait_ge(val_turned, n + 3)
                v.wait_ge(top_turned, n + 1)
                v.tensor_reduce(top[:, k, :], ps_v[k][:, :, :], AX_X, ALU.max).then_inc(topped, 1)

            def merge(i, r, w, s):
                n, k = r * U + s, s % 2
                at = window_start(v, S, t, i * U + s, w)
                v.wait_ge(top_turned, n + 3)
                v.wait_ge(merged, n + 2)
                v.tensor_tensor(most[:, :, ds(at, W)], most[:, :, ds(at, W)],
                                ps_top[0:2, k * P:(k + 1) * P].rearrange("p (a n) -> p a n", a=2), ALU.max).then_inc(merged, 1)
            pipelined(v, S, t, [(2, values), (1, tops), (0, merge)])


def attention_phase(nc, S, t):
    H4 = J * HEADS
    with ExitStack() as c:
        sb = lambda n, s, d=F32: c.enter_context(nc.sbuf_tensor(f"att_{n}", s, d))
        sem = lambda n: c.enter_context(nc.semaphore(f"att_{n}"))
        ps = lambda n: [c.enter_context(nc.psum_tensor(f"att_{n}{k}", [P, 512], F32)) for k in range(2)]
        xe, diff = sb("xe", [P, U, J * F]), sb("diff", [P, U, H4])
        xw = sb("xw", [P, U, J, F + HEADS])
        by_node = sb("by_node", [W, 2, F + HEADS])
        onehot, hotT = sb("onehot", [P, U, J, W]), sb("hotT", [W, 2, GE], BF16)
        most, rest, mostT = sb("most", [HEADS, U, W]), sb("rest", [W, 2, HEADS]), sb("mostT", [W, 2, 3, HEADS], BF16)
        dst_row, node_w = sb("dst_row", [2, U, GE], BF16), sb("node_w", [W, S.NWIN])
        acc, den = t["big"][:, 0, :], t["big"][0:HEADS, 1, :]
        ps_dst, ps_max, ps_node = ps("ps_dst"), ps("ps_max"), ps("ps_node")
        ps_most = c.enter_context(nc.psum_tensor("att_ps_most", [P, 512], F32))
        ps_sum = c.enter_context(nc.psum_tensor("att_ps_sum", [P, 512], F32))
        x_in, most_in = [sem(f"x_in{k}") for k in range(U)], [sem(f"most_in{k}") for k in range(U)]
        turned, part = sem("turned"), sem("part")
        exped, weighed, summed, maxed = sem("exped"), sem("weighed"), sem("summed"), sem("maxed")
        sum_copied, turned_back = sem("sum_copied"), sem("turned_back")
        keys_made, added = sem("keys_made"), sem("added")
        differed = sem("differed")
        block = c.enter_context(nc.Block())

        @block.sync
        def _(sp):
            edges = t["edges"].rearrange("(g p j) f -> g p (j f)", p=P, j=J)

            def load_most(i, r, w, s):
                at = window_start(sp, S, t, i * U + s, w)
                sp.wait_ge(turned, r * U + s + 1)
                sp.nop(nofuse=True)
                sp.dma_start(most[:, s, :], t["MX"][:, ds(at, W)]).then_inc(most_in[s], 16)
                sp.dma_start(dst_row[:, s, :], t["rows"][ds(i * U + s, 1), 0:2, :].rearrange("a m e -> (a m) e")).then_inc(most_in[s], 16)

            def load(i, r, w, s):
                sp.wait_ge(weighed, r * U + s + 1)
                sp.nop(nofuse=True)
                sp.dma_start(xe[:, s, :], edges[ds(i * U + s, 1), :, :].rearrange("a p d -> (a p) d")).then_inc(x_in[s], 16)
            pipelined(sp, S, t, [(0, load), (4, load_most)])

        @block.vector
        def _(v):
            v.memset(acc, 0.0).then_inc(added, 1)
            v.memset(den, 0.0).then_inc(added, 1)
            v.sem_inc(added, 2)
            v.sem_inc(weighed, U)
            v.tensor_scalar(node_w[:, :], t["win0"][0:W, :], t["pcol"][0:W, 0:1], None, ALU.add).then_inc(keys_made, 1)
            v.wait_ge(keys_made, 1)
            v.sem_inc(keys_made, 1)
            v.sem_inc(differed, 6)

            def weigh(i, r, w, s):
                n = r * U + s
                v.wait_ge(summed, n + 1)
                one_hot(v, t, onehot[:, s, :, :], i * U + s, w)
                v.wait_ge(x_in[s], r * 16 + 16)
                v.wait_ge(exped, n + 1 + U)
                v.tensor_tensor(xw[:, s, :, 0:F].rearrange("p j (h d) -> p j h d", d=HD),
                                xe[:, s, :].rearrange("p (j h d) -> p j h d", j=J, d=HD),
                                bcast(xw[:, s, :, F:F + HEADS], 3, HD), ALU.mult).then_inc(weighed, 1)

            def differ(i, r, w, s):
                n = r * U + s
                v.wait_ge(maxed, n + 1 + U)
                v.wait_ge(exped, n + 1)
                v.tensor_reduce(diff[:, s, :].rearrange("p (j h) -> p j h", h=HEADS),
                                ps_max[s % 2][:, 0:3 * H4].rearrange("p (j q h) -> p j h q", q=3, h=HEADS), AX_X, ALU.add
                                ).then_inc(differed, 1)
                v.wait_ge(differed, n * 3 + 7)
                v.tensor_tensor(diff[:, s, :], t["logits"][:, ds((i * U + s) * H4, H4)], diff[:, s, :],
                                ALU.subtract).then_inc(differed, 1)
                v.wait_ge(differed, n * 3 + 8)
                v.tensor_scalar(diff[:, s, :], diff[:, s, :], 0.0, None, ALU.min).then_inc(differed, 1)

            def make_keys(i, r, w, s):
                n, k = r * U + s, s % 2
                v.wait_ge(turned, n + 1 + U)
                v.wait_ge(maxed, n + 1 + U - 2)
                top = ps_most[0:W, 0:HEADS]
                v.tensor_copy(mostT[:, k, 0, :], top).then_inc(part, 1)
                v.tensor_scalar(hotT[:, k, :], ps_dst[k][0:W, :], t["pcol"][0:W, 0:1] if w is None else node_w[:, ds(w, 1)],
                                None, ALU.is_equal)
                v.wait_ge(part, n * 3 + 1)
                v.tensor_tensor(rest[:, k, :], top, mostT[:, k, 0, :], ALU.subtract).then_inc(part, 1)
                v.wait_ge(part, n * 3 + 2)
                v.tensor_copy(mostT[:, k, 1, :], rest[:, k, :]).then_inc(part, 1)
                v.wait_ge(part, n * 3 + 3)
                v.tensor_tensor(mostT[:, k, 2, :], rest[:, k, :], mostT[:, k, 1, :], ALU.subtract).then_inc(keys_made, 1)

            def add(i, r, w, s):
                n = r * U + s
                at = window_start(v, S, t, i * U + s, w)
                v.wait_ge(turned_back, n + 3)
                v.wait_ge(added, n * 2 + 4)
                v.tensor_tensor(acc[:, ds(at, W)], acc[:, ds(at, W)], ps_sum[:, 0:W], ALU.add).then_inc(added, 1)
                v.tensor_tensor(den[:, ds(at, W)], den[:, ds(at, W)], ps_sum[0:HEADS, W:2 * W], ALU.add).then_inc(added, 1)

            pipelined(v, S, t, [(2, weigh), (0, add), (3, differ), (4, make_keys)], (make_keys, differ, weigh, add))

        @block.scalar
        def _(act):
            act.sem_inc(exped, U)
            act.sem_inc(sum_copied, 2)

            def exps(i, r, w, s):
                n = r * U + s
                act.wait_ge(differed, n * 3 + 9)
                act.wait_ge(summed, n + 1)
                act.activation(xw[:, s, :, F:F + HEADS], diff[:, s, :].rearrange("p (j h) -> p j h", h=HEADS), ACT.Exp).then_inc(exped, 1)

            def copy_sum(i, r, w, s):
                n = r * U + s
                act.wait_ge(summed, n + 1 + U)
                act.wait_ge(turned_back, n + 1)
                act.activation(by_node[:, s % 2, :], ps_node[s % 2][0:W, 0:F + HEADS], ACT.Copy).then_inc(sum_copied, 1)
            pipelined(act, S, t, [(1, copy_sum), (3, exps)], (exps, copy_sum))

        @block.tensor
        def _(pe):
            pe.sem_inc(summed, U)
            pe.sem_inc(maxed, U)
            pe.sem_inc(turned, U)
            pe.sem_inc(turned_back, 2)

            def sums(i, r, w, s):
                n = r * U + s
                pe.wait_ge(weighed, n + 1 + U)
                pe.wait_ge(sum_copied, n + 1)
                for j in range(J):
                    mm = pe.matmul(ps_node[s % 2][0:W, 0:F + HEADS], onehot[:, s, j, :], xw[:, s, j, :],
                                   start=(j == 0), stop=(j == J - 1))
                mm.then_inc(summed, 1)

            def turn_back(i, r, w, s):
                n = r * U + s
                pe.wait_ge(sum_copied, n + 3)
                pe.wait_ge(added, n * 2 + 4)
                pe.nop(nofuse=True)
                pe.transpose(ps_sum[:, 0:W], by_node[:, s % 2, 0:F], t["ident"][0:W, 0:W])
                pe.transpose(ps_sum[0:HEADS, W:2 * W], by_node[:, s % 2, F:F + HEADS], t["ident"][0:W, 0:W]).then_inc(turned_back, 1)

            def find_max(i, r, w, s):
                n = r * U + s
                pe.wait_ge(keys_made, n + 3)
                pe.wait_ge(differed, n * 3 + 1)
                for j in range(J):
                    mm = pe.matmul(ps_max[s % 2][:, j * 3 * HEADS:(j + 1) * 3 * HEADS],
                                   hotT[:, s % 2, :].rearrange("n (p j) -> n j p", j=J)[:, j, :],
                                   mostT[:, s % 2, :, :].rearrange("n q h -> n (q h)"), start=True, stop=True)
                mm.then_inc(maxed, 1)

            def turn_keys(i, r, w, s):
                n = r * U + s
                pe.wait_ge(most_in[s], r * 32 + 32)
                pe.wait_ge(keys_made, n + 2)
                pe.nop(nofuse=True)
                pe.transpose(ps_most[0:W, 0:HEADS], most[:, s, :], t["ident"][0:HEADS, 0:HEADS])
                pe.matmul(ps_dst[s % 2][0:W, :], t["select"][0:2, 0, 0:W], dst_row[:, s, :], start=True, stop=True).then_inc(turned, 1)
            pipelined(pe, S, t, [(0, turn_back), (1, sums), (3, find_max), (4, turn_keys)], (turn_keys, find_max, sums, turn_back))


def output_phase(nc, S, t, y):
    TURNS = S.NTP // Q
    full, rest = S.N // P, S.N % P
    acc, den = t["big"][:, 0, :], t["big"][0:HEADS, 1, :]
    with ExitStack() as c:
        sb = lambda n, s, d=F32: c.enter_context(nc.sbuf_tensor(f"out_{n}", s, d))
        sem = lambda n: c.enter_context(nc.semaphore(f"out_{n}"))
        ps = lambda n, s: c.enter_context(nc.psum_tensor(f"out_{n}", s, F32))
        res = sb("res", [P, S.NTP, F])
        h_q, aggs, placed = sb("h_q", [P, Q, F]), sb("aggs", [P, Q * P]), sem("placed")
        stats = sb("stats", [P, S.NTP, 6])
        mean, var, tmp = (sb(n, [P, S.NTP]) for n in ("mean", "var", "tmp"))
        head = sb("head", [HEADS, F])
        ps_h, ps_o, ps_den = ps("ps_h", [P, 512]), ps("ps_o", [P, 512]), ps("ps_den", [P, 512])
        h_in, pe_done, dv = sem("h_in"), sem("pe_done"), sem("dv")
        dv2, fin, roots, stored = sem("dv2"), sem("fin"), sem("roots"), sem("stored")
        C, C2 = 6 + Q, 7
        block = c.enter_context(nc.Block())

        @block.sync
        def _(sp):
            with sp.Fori(0, TURNS) as i:
                sp.dma_start(res[:, ds(i * Q, Q), :], tiles_of(t["H3"], i * Q, Q)).then_inc(h_in, 16)
                sp.wait_ge(h_in, i * 16 + 16)
                sp.nop(nofuse=True)
            with sp.Fori(0, TURNS) as i:
                sp.wait_ge(dv, i * C + 2 * C)
                sp.nop(nofuse=True)
                sp.dma_start(acc[:, ds(i * (Q * F), Q * F)].rearrange("p (n f) -> p n f", f=F), tiles_of(t["X3"], i * Q, Q)
                             ).then_inc(h_in, 16)
                sp.wait_ge(h_in, i * 16 + 16 * TURNS + 16)
                sp.nop(nofuse=True)
            sp.wait_ge(dv2, TURNS * C2 + C2)
            sp.dma_start(y[0:full * P, :].rearrange("(n p) f -> p n f", p=P), res[:, 0:full, :]).then_inc(stored, 16)
            if rest:
                sp.dma_start(y[full * P:S.N, :], res[0:rest, full, :]).then_inc(stored, 16)
            sp.wait_ge(stored, 16 * (1 + bool(rest)))

        @block.tensor
        def _(pe):
            pe.sem_inc(pe_done, 2)
            with pe.Fori(0, TURNS) as i:
                pe.wait_ge(placed, i + 1)
                pe.wait_ge(dv, i * C + C)
                pe.matmul(ps_den[:, :], head[:, :], den[:, ds(i * (Q * P), Q * P)], start=True, stop=True)
                for k in range(Q):
                    mm = pe.transpose(ps_h[:, k * P:(k + 1) * P], h_q[:, k, :], t["ident"][:, :])
                mm.then_inc(pe_done, 1)
                pe.wait_ge(dv, i * C + C + 4)
                for k in range(Q):
                    mm = pe.matmul(ps_o[:, k * P:(k + 1) * P], aggs[:, k * P:(k + 1) * P], t["out_wT"][:, :], start=True, stop=True)
                mm.then_inc(pe_done, 1)

        @block.vector
        def _(v):
            v.tensor_copy(head[:, :].rearrange("h (a d) -> h a d", d=HD), bcast(t["ident"][0:HEADS, 0:HEADS], 2, HD)).then_inc(dv, 1)
            v.sem_inc(dv, C - 1)
            with v.Fori(0, TURNS) as i:
                link = Link(v, dv, i * C + C)
                cols = ds(i * (Q * P), Q * P)
                v.wait_ge(pe_done, i * 2 + 3)
                link(v.tensor_scalar(aggs[:, :], ps_den[:, :], 1.0e-30, None, ALU.max))
                link(v.reciprocal(aggs[:, :], aggs[:, :]))
                link(v.tensor_tensor(aggs[:, :], aggs[:, :], acc[:, cols], ALU.mult))
                link(v.tensor_tensor(aggs[:, :], aggs[:, :], ps_h[:, :], ALU.add))
                v.wait_ge(pe_done, i * 2 + 4)
                four = res[:, ds(i * Q, Q), :]
                link(v.tensor_tensor(four, ps_o[:, :].rearrange("p (n f) -> p n f", n=Q), bcast(t["out_b"][:, :], 1, Q), ALU.add))
                link(v.tensor_scalar(four, four, 0.0, None, ALU.max))
                for k in range(Q):
                    link(v.bn_stats(stats[:, ds(i * Q + k, 1), :], res[:, ds(i * Q + k, 1), :]), False)
                assert link.n == C
            v.wait_ge(dv, TURNS * C + C)
            link = Link(v, fin)
            norm_constants(link, v, stats, mean, var, tmp)
            v.sem_inc(roots, 1)
            v.wait_ge(roots, 2)
            link(v.reciprocal(var[:, :], var[:, :]))
            v.sem_inc(dv2, C2)
            with v.Fori(0, TURNS) as i:
                link2 = Link(v, dv2, i * C2 + C2)
                v.wait_ge(h_in, i * 16 + 16 * TURNS + 16)
                normed_sum(v, link2, res, i, mean, var, t["out_gamma"], t["out_beta"],
                           acc[:, ds(i * (Q * F), Q * F)].rearrange("p (n f) -> p n f", f=F))
                assert link2.n == C2
            v.wait_ge(dv2, TURNS * C2 + C2)

        @block.scalar
        def _(act):
            with act.Fori(0, TURNS) as i:
                act.wait_ge(pe_done, i * 2 + 1)
                act.wait_ge(h_in, i * 16 + 16)
                act.activation(h_q[:, :, :], res[:, ds(i * Q, Q), :], ACT.Copy).then_inc(placed, 1)
            act.wait_ge(roots, 1)
            act.activation(var[:, :], var[:, :], ACT.Sqrt).then_inc(roots, 1)


NAMES = ["x", "src", "dst", "edge_attr_64", "edge_type_50", "edge_type_9", "L0_gnn_W_msg", "L0_gnn_b_msg",
         "L0_gnn_edge_embed", "L0_gnn_W_ih", "L0_gnn_W_hh", "L0_gnn_b_ih", "L0_gnn_b_hh", "L1_gnn_W", "L1_gnn_b",
         "L1_gnn_gamma", "L1_gnn_beta", "L2_gnn_bases", "L2_gnn_comps", "L2_gnn_alpha", "L3_gnn_W_proj_w",
         "L3_gnn_W_proj_b", "L3_gnn_attn_vec", "L3_gnn_W_out_w", "L3_gnn_W_out_b", "L3_gnn_ln_gamma",
         "L3_gnn_ln_beta"]


def build_program(nc, a, out, kind="Internal"):
    S = Shapes(a["x"].shape[0], a["src"].shape[0])
    dram = lambda n, s, d=F32: nc.dram_tensor(n, s, d, kind=kind).ap()
    t = {
        "T9": dram("T9", (P, S.NGP * J)),
        "IDX": dram("IDX", (P, S.NGP * J), I32),
        "rows": dram("rows", (S.NGP, IDS + 3 * BASES, GE), BF16),
        "scat": [dram(f"scat{k}", (S.NR, F)) for k in range(COPIES)],
        "HB": dram("HB", (S.NR, BASES * F)),
        "MX": dram("MX", (HEADS, S.NR)),
        "proj": dram("proj", (S.NR, F)),
        "edges": dram("edges", (S.NGP * GE, F)),
    }
    for k in range(4):
        t[f"H{k}"] = dram(f"H{k}", (S.NR, F))
        t[f"X{k}"] = dram(f"X{k}", (S.NR, F))
    with ExitStack() as c:
        sb = lambda n, s, d=F32: c.enter_context(nc.sbuf_tensor(n, s, d))
        t["ident"] = sb("ident", [P, P])
        t["iota"] = sb("iota", [P, P])
        t["pcol"] = sb("pcol", [P, 1])
        t["win0"] = sb("win0", [P, S.NWIN])
        t["win_far"] = sb("win_far", [P, S.NWIN])
        t["src_i"] = sb("src_i", [P, S.NGP * J], I32)
        t["dst_rel"] = sb("dst_rel", [P, S.NGP * J])
        t["base"] = sb("base_row", [1, S.NB * P], I32)
        t["wide"] = sb("wide", [1, 1], I32)
        t["deg_src"] = sb("deg_src", [P, S.NT])
        t["dinv_in"] = sb("dinv_in", [P, S.NTP])
        t["dinv_src"] = sb("dinv_src", [P, S.NTP])
        t["relation"] = sb("relation", [P, 3 * BASES], BF16)
        t["select"] = sb("select", [IDS + 3 * BASES, 5, P], BF16)
        for n, w in WEIGHTS.items():
            t[n] = sb(n, [P, w])
        setup_phase(nc, S, a["src"], a["dst"], a["edge_type_9"], a["edge_type_50"], t)
        first_norm_phase(nc, S, a["x"], t)
        with nc.sbuf_tensor("sums_a", [P, 2, S.NR], F32) as t["big"]:
            sum_phase(nc, S, t, "L0", t["H0"], True)
            weights_phase(nc, S, a, t)
            gru_phase(nc, S, t)
            sum_phase(nc, S, t, "L1", t["H1"], False)
            gcn_phase(nc, S, t)
        relation_phase(nc, S, t)
        relation_norm_phase(nc, S, t)
        with nc.sbuf_tensor("sums_b", [P, 2, S.NR], F32) as t["big"]:
            with nc.sbuf_tensor("logits", [P, S.NGP * J * HEADS], F32) as t["logits"]:
                logit_phase(nc, S, a["edge_attr_64"], t)
                attention_phase(nc, S, t)
            output_phase(nc, S, t, out)
    return S, t


def kernel(**inputs):
    import numpy as _np
    import concourse.bacc as _bacc
    from concourse import mybir as _mybir
    from concourse.bass_utils import run_bass_kernel_spmd as _run

    nc = _bacc.Bacc("TRN2", target_bir_lowering=False, num_devices=1)
    arrays, args = {}, {}
    for name in NAMES:
        a = _np.ascontiguousarray(inputs[name])
        arrays[f"in_{name}_dram"] = a
        args[name] = nc.dram_tensor(f"in_{name}_dram", a.shape, _mybir.dt.from_np(a.dtype), kind="ExternalInput").ap()
    out = nc.dram_tensor("out_0_dram", args["x"].shape, F32, kind="ExternalOutput").ap()
    build_program(nc, args, out)
    r = _run(nc, [arrays], core_ids=[0])
    return r.results[0]["out_0_dram"]
```
